# Optimizing a Trainium2 kernel written in Bass

```python
import numpy as np
import jax
import jax.numpy as jnp

def _softmax(x, axis=-1):
    return jax.nn.softmax(x, axis=axis)

def _gelu(x):
    return jax.nn.gelu(x, approximate=True)

def _silu(x):
    return jax.nn.silu(x)

def _sigmoid(x):
    return jax.nn.sigmoid(x)

def _layernorm(x, axis=-1, eps=1e-05):
    m = jnp.mean(x, axis=axis, keepdims=True)
    v = jnp.var(x, axis=axis, keepdims=True)
    return (x - m) / jnp.sqrt(v + eps)

def _scatter_add(tgt, idx, src, axis=0):
    return tgt.at[idx].add(src)

def _segment_sum(src, seg, n):
    return jax.ops.segment_sum(src, seg, n)
kernel_name = 'mk_decoder_preln_d2_seqx_r8_54b733'

def setup_inputs(seed: int=0):
    np.random.seed(seed)
    _w = jnp.asarray

    def _rec_inputs():
        import jax
        import jax.numpy as jnp
        _rk = jax.random.key(seed)
        x = -0.0005146 + 1 * jax.random.normal(jax.random.fold_in(_rk, 1), (64, 64, 128), jnp.float32)
        _lenS = 64 - jax.random.randint(jax.random.fold_in(_rk, 7), (64,), 0, max(1, 64 // 4) + 1, jnp.int32)
        _lenS2 = 64 - jax.random.randint(jax.random.fold_in(_rk, 8), (64,), 0, max(1, 64 // 4) + 1, jnp.int32)
        _ctx_1024P = jax.random.normal(jax.random.fold_in(_rk, 11), (64, 16, 128), jnp.float32)
        _ctx_1024c = jax.random.dirichlet(jax.random.fold_in(_rk, 511), 0.3 * jnp.ones((16,), jnp.float32), (64, 64))
        _ctx_1024t = jnp.einsum('bsk,bkd->bsd', _ctx_1024c, _ctx_1024P)
        _ctx_1024t = _ctx_1024t * jax.lax.rsqrt(jnp.mean(jnp.square(_ctx_1024t)) + 1e-12) * 0.953939
        ctx_1024 = -0.000125008 + 0.999885 * (_ctx_1024t + 0.3 * jax.random.normal(jax.random.fold_in(_rk, 611), (64, 64, 128), jnp.float32))
        _validS = jnp.arange(64)[None, :] < _lenS[:, None]
        _validS2 = jnp.arange(64)[None, :] < _lenS2[:, None]
        _causal = jnp.tril(jnp.ones((64, 64), dtype=bool))
        mask_1x1xSxS2_bk0 = jnp.logical_not(jnp.broadcast_to(_validS2[0:1, None, None, :], (1, 1, 64, 64)))
        return (x, ctx_1024, mask_1x1xSxS2_bk0)
    x, ctx_1024, mask_1x1xSxS2_bk0 = _rec_inputs()

    def _L0_attn_setup():
        import jax, jax.numpy as jnp
        import numpy as np
        D_MODEL = 128
        N_HEADS = 16
        HEAD_DIM = D_MODEL // N_HEADS
        N_EXPERTS = 4
        HIDDEN = 4 * D_MODEL
        B, T = (1, 256)

        def _apply_rope(x, sin, cos):
            x1, x2 = (x[..., ::2], x[..., 1::2])
            r1 = x1 * cos - x2 * sin
            r2 = x1 * sin + x2 * cos
            return jnp.stack((r1, r2), axis=-1).reshape(x.shape)
        key = jax.random.key(seed)
        ks = jax.random.split(key, 16)
        s = 0.02
        d, E, Hd = (D_MODEL, N_EXPERTS, HIDDEN)
        return {'x': jax.random.normal(ks[0], (B, T, d), dtype=jnp.float32), 'w_dw': jax.random.normal(ks[1], (d, 3), dtype=jnp.float32) * s, 'w_pw': jax.random.normal(ks[2], (d, d), dtype=jnp.float32) * s, 'w_qkv': jax.random.normal(ks[3], (3 * d, d), dtype=jnp.float32) * s, 'w_o': jax.random.normal(ks[4], (d, d), dtype=jnp.float32) * s, 'w_gate': jax.random.normal(ks[5], (d, d), dtype=jnp.float32) * s, 'b_gate': jnp.zeros((d,), dtype=jnp.float32), 'ln_g': jnp.ones((d,), dtype=jnp.float32), 'ln_b': jnp.zeros((d,), dtype=jnp.float32), 'w_moe_gate': jax.random.normal(ks[6], (E, d), dtype=jnp.float32) * s, 'w1': jax.random.normal(ks[7], (E, Hd, d), dtype=jnp.float32) * s, 'b1': jnp.zeros((E, Hd), dtype=jnp.float32), 'w2': jax.random.normal(ks[8], (E, d, Hd), dtype=jnp.float32) * s, 'b2': jnp.zeros((E, d), dtype=jnp.float32)}
    _L0_attn_all = _L0_attn_setup()
    _L0_attn_in = {k: v for k, v in _L0_attn_all.items() if k in ('w_dw', 'w_pw', 'w_qkv', 'w_o', 'w_gate', 'b_gate', 'ln_g', 'ln_b', 'w_moe_gate', 'w1', 'b1', 'w2', 'b2')}
    del _L0_attn_all

    def _L0_xattn_setup():
        import jax, jax.numpy as jnp
        import numpy as np
        DIM = 128
        HEADS = 16
        DIM_HEAD = 64
        INNER = HEADS * DIM_HEAD
        EPS = 1e-05

        def layer_norm(x, gamma, beta):
            mu = jnp.mean(x, axis=-1, keepdims=True)
            var = jnp.mean(jnp.square(x - mu), axis=-1, keepdims=True)
            return (x - mu) * jax.lax.rsqrt(var + EPS) * gamma + beta
        key = jax.random.key(seed)
        ks = jax.random.split(key, 6)
        b, n1, n2 = (8, 512, 32)
        x = jax.random.normal(ks[0], (b, n1, DIM), dtype=jnp.float32)
        latents = jax.random.normal(ks[1], (b, n2, DIM), dtype=jnp.float32)
        s = 1.0 / np.sqrt(DIM)
        Wq = jax.random.normal(ks[2], (DIM, INNER), dtype=jnp.float32) * s
        Wkv = jax.random.normal(ks[3], (DIM, 2 * INNER), dtype=jnp.float32) * s
        Wout = jax.random.normal(ks[4], (INNER, DIM), dtype=jnp.float32) * (1.0 / np.sqrt(INNER))
        g1 = jnp.ones((DIM,), jnp.float32)
        b1 = jnp.zeros((DIM,), jnp.float32)
        g2 = jnp.ones((DIM,), jnp.float32)
        b2 = jnp.zeros((DIM,), jnp.float32)
        return {'x': x, 'latents': latents, 'g1': g1, 'b1': b1, 'g2': g2, 'b2': b2, 'Wq': Wq, 'Wkv': Wkv, 'Wout': Wout}
    _L0_xattn_all = _L0_xattn_setup()
    _L0_xattn_in = {k: v for k, v in _L0_xattn_all.items() if k in ('g1', 'b1', 'g2', 'b2', 'Wq', 'Wkv', 'Wout')}
    del _L0_xattn_all

    def _L0_ffn_setup():
        import jax, jax.numpy as jnp
        import numpy as np
        B, S, H = (4, 256, 128)
        E, K = (8, 2)
        I_R, I_S = (4 * H, 8 * H)
        CAP_FACTOR = 1.25
        SCALE = 1.0
        key = jax.random.key(seed)
        ks = jax.random.split(key, 9)
        std = 0.02
        return {'x': jax.random.normal(ks[0], (B, S, H), jnp.float32), 'router_w': std * jax.random.normal(ks[1], (E, H), jnp.float32), 'rg': std * jax.random.normal(ks[2], (E, H, I_R), jnp.float32), 'ru': std * jax.random.normal(ks[3], (E, H, I_R), jnp.float32), 'rd': std * jax.random.normal(ks[4], (E, I_R, H), jnp.float32), 'sg': std * jax.random.normal(ks[5], (H, I_S), jnp.float32), 'su': std * jax.random.normal(ks[6], (H, I_S), jnp.float32), 'sd': std * jax.random.normal(ks[7], (I_S, H), jnp.float32)}
    _L0_ffn_all = _L0_ffn_setup()
    _L0_ffn_in = {k: v for k, v in _L0_ffn_all.items() if k in ('router_w', 'rg', 'ru', 'rd', 'sg', 'su', 'sd')}
    del _L0_ffn_all

    def _L1_attn_setup():
        import jax, jax.numpy as jnp
        import numpy as np
        B, T, C, H = (4, 256, 128, 16)
        INIT_STD = 0.02
        key = jax.random.key(seed)
        ks = jax.random.split(key, 9)
        x = jax.random.normal(ks[0], (B, T, C), dtype=jnp.float32)

        def dense(kw):
            return jax.random.normal(kw, (C, C), dtype=jnp.float32) * INIT_STD
        return {'x': x, 'Wq': dense(ks[1]), 'bq': jnp.zeros((C,), jnp.float32), 'Wk': dense(ks[2]), 'bk': jnp.zeros((C,), jnp.float32), 'Wv': dense(ks[3]), 'bv': jnp.zeros((C,), jnp.float32), 'Wo': dense(ks[4]), 'bo': jnp.zeros((C,), jnp.float32)}
    _L1_attn_all = _L1_attn_setup()
    _L1_attn_in = {k: v for k, v in _L1_attn_all.items() if k in ('Wq', 'bq', 'Wk', 'bk', 'Wv', 'bv', 'Wo', 'bo')}
    del _L1_attn_all

    def _L1_xattn_setup():
        import jax, jax.numpy as jnp
        import numpy as np
        B, S, E, H, D = (4, 256, 128, 16, 64)
        NUM_BUCKETS, MAX_DISTANCE = (32, 128)

        def _relative_position_bucket(relative_position, num_buckets, max_distance):
            max_exact = num_buckets // 2
            max_distance = max(max_distance, max_exact + 1)
            distance = jnp.maximum(-relative_position, 0)
            is_small = distance < max_exact
            safe_distance = jnp.maximum(distance, 1)
            log_scale = jnp.log(safe_distance / max_exact) / jnp.log(max_distance / max_exact)
            large_bucket = max_exact + (log_scale * (num_buckets - max_exact)).astype(jnp.int32)
            large_bucket = jnp.minimum(large_bucket, num_buckets - 1)
            return jnp.where(is_small, distance, large_bucket)
        key = jax.random.key(seed)
        ks = jax.random.split(key, 7)
        w_scale = 1.0 / np.sqrt(E)
        inputs_q = jax.random.normal(ks[0], (B, S, E), jnp.float32)
        inputs_kv = jax.random.normal(ks[1], (B, S, E), jnp.float32)
        Wq = jax.random.normal(ks[2], (E, H * D), jnp.float32) * w_scale
        Wk = jax.random.normal(ks[3], (E, H * D), jnp.float32) * w_scale
        Wv = jax.random.normal(ks[4], (E, H * D), jnp.float32) * w_scale
        Wo = jax.random.normal(ks[5], (H * D, E), jnp.float32) * (1.0 / np.sqrt(H * D))
        rel_bias = jax.random.normal(ks[6], (H, NUM_BUCKETS), jnp.float32) * 0.02
        mask = jnp.tril(jnp.ones((S, S), dtype=bool))[None, None]
        return {'inputs_q': inputs_q, 'inputs_kv': inputs_kv, 'mask': mask, 'Wq': Wq, 'Wk': Wk, 'Wv': Wv, 'Wo': Wo, 'rel_bias': rel_bias}
    _L1_xattn_all = _L1_xattn_setup()
    _L1_xattn_in = {k: v for k, v in _L1_xattn_all.items() if k in ('Wq', 'Wk', 'Wv', 'Wo', 'rel_bias')}
    del _L1_xattn_all

    def _L1_ffn_setup():
        import jax, jax.numpy as jnp
        import numpy as np
        B, S, D, E = (2, 256, 128, 8)
        key = jax.random.key(seed)
        ks = jax.random.split(key, 5)
        x = jax.random.normal(ks[0], (B, S, D), dtype=jnp.float32)
        router_w = jax.random.normal(ks[1], (E, D), dtype=jnp.float32) * 0.02
        router_b = jnp.zeros((E,), dtype=jnp.float32)
        expert_w = jax.random.normal(ks[2], (E, D, D), dtype=jnp.float32) * 0.02
        expert_b = jnp.zeros((E, D), dtype=jnp.float32)
        return {'x': x, 'router_w': router_w, 'router_b': router_b, 'expert_w': expert_w, 'expert_b': expert_b}
    _L1_ffn_all = _L1_ffn_setup()
    _L1_ffn_in = {k: v for k, v in _L1_ffn_all.items() if k in ('router_w', 'router_b', 'expert_w', 'expert_b')}
    del _L1_ffn_all
    return {'x': x, 'ctx_1024': ctx_1024, 'mask_1x1xSxS2_bk0': mask_1x1xSxS2_bk0, 'L0_attn_w_dw': _L0_attn_in['w_dw'], 'L0_attn_w_pw': _L0_attn_in['w_pw'], 'L0_attn_w_qkv': _L0_attn_in['w_qkv'], 'L0_attn_w_o': _L0_attn_in['w_o'], 'L0_attn_w_gate': _L0_attn_in['w_gate'], 'L0_attn_b_gate': _L0_attn_in['b_gate'], 'L0_attn_ln_g': _L0_attn_in['ln_g'], 'L0_attn_ln_b': _L0_attn_in['ln_b'], 'L0_attn_w_moe_gate': _L0_attn_in['w_moe_gate'], 'L0_attn_w1': _L0_attn_in['w1'], 'L0_attn_b1': _L0_attn_in['b1'], 'L0_attn_w2': _L0_attn_in['w2'], 'L0_attn_b2': _L0_attn_in['b2'], 'L0_xattn_g1': _L0_xattn_in['g1'], 'L0_xattn_b1': _L0_xattn_in['b1'], 'L0_xattn_g2': _L0_xattn_in['g2'], 'L0_xattn_b2': _L0_xattn_in['b2'], 'L0_xattn_Wq': _L0_xattn_in['Wq'], 'L0_xattn_Wkv': _L0_xattn_in['Wkv'], 'L0_xattn_Wout': _L0_xattn_in['Wout'], 'L0_ffn_router_w': _L0_ffn_in['router_w'], 'L0_ffn_rg': _L0_ffn_in['rg'], 'L0_ffn_ru': _L0_ffn_in['ru'], 'L0_ffn_rd': _L0_ffn_in['rd'], 'L0_ffn_sg': _L0_ffn_in['sg'], 'L0_ffn_su': _L0_ffn_in['su'], 'L0_ffn_sd': _L0_ffn_in['sd'], 'L1_attn_Wq': _L1_attn_in['Wq'], 'L1_attn_bq': _L1_attn_in['bq'], 'L1_attn_Wk': _L1_attn_in['Wk'], 'L1_attn_bk': _L1_attn_in['bk'], 'L1_attn_Wv': _L1_attn_in['Wv'], 'L1_attn_bv': _L1_attn_in['bv'], 'L1_attn_Wo': _L1_attn_in['Wo'], 'L1_attn_bo': _L1_attn_in['bo'], 'L1_xattn_Wq': _L1_xattn_in['Wq'], 'L1_xattn_Wk': _L1_xattn_in['Wk'], 'L1_xattn_Wv': _L1_xattn_in['Wv'], 'L1_xattn_Wo': _L1_xattn_in['Wo'], 'L1_xattn_rel_bias': _L1_xattn_in['rel_bias'], 'L1_ffn_router_w': _L1_ffn_in['router_w'], 'L1_ffn_router_b': _L1_ffn_in['router_b'], 'L1_ffn_expert_w': _L1_ffn_in['expert_w'], 'L1_ffn_expert_b': _L1_ffn_in['expert_b']}

def reference(x, ctx_1024, mask_1x1xSxS2_bk0, L0_attn_w_dw, L0_attn_w_pw, L0_attn_w_qkv, L0_attn_w_o, L0_attn_w_gate, L0_attn_b_gate, L0_attn_ln_g, L0_attn_ln_b, L0_attn_w_moe_gate, L0_attn_w1, L0_attn_b1, L0_attn_w2, L0_attn_b2, L0_xattn_g1, L0_xattn_b1, L0_xattn_g2, L0_xattn_b2, L0_xattn_Wq, L0_xattn_Wkv, L0_xattn_Wout, L0_ffn_router_w, L0_ffn_rg, L0_ffn_ru, L0_ffn_rd, L0_ffn_sg, L0_ffn_su, L0_ffn_sd, L1_attn_Wq, L1_attn_bq, L1_attn_Wk, L1_attn_bk, L1_attn_Wv, L1_attn_bv, L1_attn_Wo, L1_attn_bo, L1_xattn_Wq, L1_xattn_Wk, L1_xattn_Wv, L1_xattn_Wo, L1_xattn_rel_bias, L1_ffn_router_w, L1_ffn_router_b, L1_ffn_expert_w, L1_ffn_expert_b):
    import jax
    import jax.numpy as jnp

    def _L0_attn_ref(x, w_dw, w_pw, w_qkv, w_o, w_gate, b_gate, ln_g, ln_b, w_moe_gate, w1, b1, w2, b2):
        import jax, jax.numpy as jnp
        import numpy as np
        D_MODEL = 128
        N_HEADS = 16
        HEAD_DIM = D_MODEL // N_HEADS
        N_EXPERTS = 4
        HIDDEN = 4 * D_MODEL
        B, T = (1, 256)

        def _apply_rope(x, sin, cos):
            x1, x2 = (x[..., ::2], x[..., 1::2])
            r1 = x1 * cos - x2 * sin
            r2 = x1 * sin + x2 * cos
            return jnp.stack((r1, r2), axis=-1).reshape(x.shape)
        Bv, Tv, d = x.shape
        H, Dh = (N_HEADS, HEAD_DIM)
        dt = x.dtype
        xp = jnp.pad(x, ((0, 0), (2, 0), (0, 0)))
        y = xp[:, 0:Tv] * w_dw[:, 0] + xp[:, 1:Tv + 1] * w_dw[:, 1] + xp[:, 2:Tv + 2] * w_dw[:, 2]
        y = jnp.einsum('btd,ed->bte', y, w_pw)
        x = x + y
        qkv = jnp.einsum('btd,ed->bte', x, w_qkv).reshape(Bv, Tv, 3, H, Dh)
        q, k, v = (qkv[:, :, 0], qkv[:, :, 1], qkv[:, :, 2])
        inv_freq = 1.0 / 10000.0 ** (jnp.arange(0, Dh, 2, dtype=dt) / Dh)
        pos = jnp.arange(Tv, dtype=dt)
        theta = pos[:, None] * inv_freq[None, :]
        sin = jnp.sin(theta)[None, :, None, :]
        cos = jnp.cos(theta)[None, :, None, :]
        q = _apply_rope(q, sin, cos)
        k = _apply_rope(k, sin, cos)
        q_phi = jax.nn.elu(q) + 1.0
        k_phi = jax.nn.elu(k) + 1.0
        kv = k_phi[..., :, None] * v[..., None, :]
        kv_prefix = jnp.cumsum(kv, axis=1)
        k_prefix = jnp.cumsum(k_phi, axis=1)
        num = jnp.einsum('bthd,bthdm->bthm', q_phi, kv_prefix)
        denom = jnp.sum(q_phi * k_prefix, axis=-1, keepdims=True)
        attn = num / (denom + 1e-06)
        attn = attn.reshape(Bv, Tv, d)
        attn = jnp.einsum('btd,ed->bte', attn, w_o)
        delta = x - jnp.concatenate([x[:, :1], x[:, :-1]], axis=1)
        gate = jax.nn.sigmoid(jnp.einsum('btd,ed->bte', delta, w_gate) + b_gate)
        x = x + gate * attn
        mu = jnp.mean(x, axis=-1, keepdims=True)
        var = jnp.mean((x - mu) ** 2, axis=-1, keepdims=True)
        h = (x - mu) / jnp.sqrt(var + 1e-05) * ln_g + ln_b
        gw = jax.nn.softmax(jnp.einsum('btd,ed->bte', h, w_moe_gate), axis=-1)
        hid = jax.nn.silu(jnp.einsum('btd,efd->btef', h, w1) + b1)
        eo = jnp.einsum('btef,edf->bted', hid, w2) + b2
        ffn = jnp.einsum('bte,bted->btd', gw, eo)
        return x + ffn

    def _L0_xattn_ref(x, latents, g1, b1, g2, b2, Wq, Wkv, Wout):
        import jax, jax.numpy as jnp
        import numpy as np
        DIM = 128
        HEADS = 16
        DIM_HEAD = 64
        INNER = HEADS * DIM_HEAD
        EPS = 1e-05

        def layer_norm(x, gamma, beta):
            mu = jnp.mean(x, axis=-1, keepdims=True)
            var = jnp.mean(jnp.square(x - mu), axis=-1, keepdims=True)
            return (x - mu) * jax.lax.rsqrt(var + EPS) * gamma + beta
        b, l, _ = latents.shape
        xn = layer_norm(x, g1, b1)
        ln = layer_norm(latents, g2, b2)
        q = ln @ Wq
        kv_input = jnp.concatenate([xn, ln], axis=1)
        kv = kv_input @ Wkv
        k, v = jnp.split(kv, 2, axis=-1)

        def heads(t):
            return t.reshape(t.shape[0], t.shape[1], HEADS, DIM_HEAD).transpose(0, 2, 1, 3)
        q, k, v = (heads(q), heads(k), heads(v))
        scale = 1.0 / np.sqrt(np.sqrt(DIM_HEAD))
        logits = jnp.einsum('bhqd,bhkd->bhqk', q * scale, k * scale)
        w = jax.nn.softmax(logits.astype(jnp.float32), axis=-1).astype(logits.dtype)
        out = jnp.einsum('bhqk,bhkd->bhqd', w, v)
        out = out.transpose(0, 2, 1, 3).reshape(b, l, INNER)
        return out @ Wout

    def _L0_ffn_ref(x, router_w, rg, ru, rd, sg, su, sd):
        import jax, jax.numpy as jnp
        import numpy as np
        B, S, H = (4, 256, 128)
        E, K = (8, 2)
        I_R, I_S = (4 * H, 8 * H)
        CAP_FACTOR = 1.25
        SCALE = 1.0
        b, s, h = x.shape
        T = b * s
        capacity = max(int(CAP_FACTOR * T / E), 1)
        xf = x.reshape(T, h)
        eps = jnp.finfo(x.dtype).eps
        xn = xf * jax.lax.rsqrt(jnp.mean(xf * xf, axis=-1, keepdims=True) + eps)
        logits = xn @ router_w.T
        probs = jax.nn.softmax(logits, axis=-1)
        topk_p, topk_i = jax.lax.top_k(probs, K)
        rw = topk_p / jnp.sum(topk_p, axis=-1, keepdims=True)
        one_hot = jax.nn.one_hot(topk_i, E, dtype=x.dtype)
        mask = one_hot.sum(1)
        wdense = (one_hot * rw[..., None]).sum(1)
        sel = mask.T.astype(bool)
        order = jnp.argsort(~sel, axis=1, stable=True)
        dispatch = order[:, :capacity]
        count = sel.sum(axis=1)
        valid = (jnp.arange(capacity)[None, :] < count[:, None]).astype(x.dtype)
        xg = xf[dispatch]
        gate = jax.nn.silu(jnp.einsum('ech,ehi->eci', xg, rg))
        up = jnp.einsum('ech,ehi->eci', xg, ru)
        eout = jnp.einsum('eci,eih->ech', gate * up, rd)
        w = jnp.take_along_axis(wdense.T, dispatch, axis=1)
        contrib = eout * (w * valid)[..., None]
        routed = jnp.zeros_like(xf).at[dispatch.reshape(-1)].add(contrib.reshape(-1, h))
        shared = jax.nn.silu(x @ sg) * (x @ su) @ sd
        return shared + SCALE * routed.reshape(b, s, h)

    def _L1_attn_ref(x, Wq, bq, Wk, bk, Wv, bv, Wo, bo):
        import jax, jax.numpy as jnp
        import numpy as np
        B, T, C, H = (4, 256, 128, 16)
        INIT_STD = 0.02
        b, t, c = x.shape
        hd = c // H

        def split_heads(y):
            return jnp.transpose(y.reshape(b, t, H, hd), (0, 2, 1, 3))
        q = split_heads(x @ Wq + bq)
        k = split_heads(x @ Wk + bk)
        v = split_heads(x @ Wv + bv)
        scale = 1.0 / jnp.sqrt(jnp.float32(hd))
        att = jnp.einsum('bhqd,bhkd->bhqk', q, k) * scale
        mask = jnp.tril(jnp.ones((t, t), dtype=bool))[None, None]
        att = jnp.where(mask, att, jnp.float32(-jnp.inf))
        att = jax.nn.softmax(att, axis=-1)
        y = jnp.einsum('bhqk,bhkd->bhqd', att, v)
        y = jnp.transpose(y, (0, 2, 1, 3)).reshape(b, t, c)
        return y @ Wo + bo

    def _L1_xattn_ref(inputs_q, inputs_kv, mask, Wq, Wk, Wv, Wo, rel_bias):
        import jax, jax.numpy as jnp
        import numpy as np
        B, S, E, H, D = (4, 256, 128, 16, 64)
        NUM_BUCKETS, MAX_DISTANCE = (32, 128)

        def _relative_position_bucket(relative_position, num_buckets, max_distance):
            max_exact = num_buckets // 2
            max_distance = max(max_distance, max_exact + 1)
            distance = jnp.maximum(-relative_position, 0)
            is_small = distance < max_exact
            safe_distance = jnp.maximum(distance, 1)
            log_scale = jnp.log(safe_distance / max_exact) / jnp.log(max_distance / max_exact)
            large_bucket = max_exact + (log_scale * (num_buckets - max_exact)).astype(jnp.int32)
            large_bucket = jnp.minimum(large_bucket, num_buckets - 1)
            return jnp.where(is_small, distance, large_bucket)
        batch, q_len, embed = inputs_q.shape
        k_len = inputs_kv.shape[1]
        q = (inputs_q @ Wq).reshape(batch, q_len, H, D)
        k = (inputs_kv @ Wk).reshape(batch, k_len, H, D)
        v = (inputs_kv @ Wv).reshape(batch, k_len, H, D)
        attention = jnp.einsum('bqhd,bkhd->bhqk', q, k) * (1.0 / jnp.sqrt(D))
        rel_pos = jnp.arange(k_len, dtype=jnp.int32)[None, :] - jnp.arange(q_len, dtype=jnp.int32)[:, None]
        bucket = _relative_position_bucket(rel_pos, NUM_BUCKETS, MAX_DISTANCE)
        attention = attention + jnp.take(rel_bias, bucket, axis=1)[None]
        attention = jnp.where(mask, attention, jnp.finfo(jnp.float32).min)
        normalized = jax.nn.softmax(attention, axis=-1)
        output = jnp.einsum('bhqk,bkhd->bqhd', normalized, v).reshape(batch, q_len, H * D)
        return output @ Wo

    def _L1_ffn_ref(x, router_w, router_b, expert_w, expert_b):
        import jax, jax.numpy as jnp
        import numpy as np
        B, S, D, E = (2, 256, 128, 8)
        logits = jnp.einsum('bsd,ed->bse', x, router_w) + router_b
        probs = jax.nn.softmax(logits, axis=-1)
        weights = jnp.max(probs, axis=-1)
        top1 = jnp.argmax(probs, axis=-1)
        y_all = jnp.einsum('bsd,eod->bseo', x, expert_w) + expert_b
        y = jnp.take_along_axis(y_all, top1[:, :, None, None], axis=2)[:, :, 0, :]
        out = y * weights[:, :, None]
        return out
    x = x + _L0_attn_ref(_layernorm(x, axis=-1), L0_attn_w_dw, L0_attn_w_pw, L0_attn_w_qkv, L0_attn_w_o, L0_attn_w_gate, L0_attn_b_gate, L0_attn_ln_g, L0_attn_ln_b, L0_attn_w_moe_gate, L0_attn_w1, L0_attn_b1, L0_attn_w2, L0_attn_b2)
    x = x + _L0_xattn_ref(ctx_1024, _layernorm(x, axis=-1), L0_xattn_g1, L0_xattn_b1, L0_xattn_g2, L0_xattn_b2, L0_xattn_Wq, L0_xattn_Wkv, L0_xattn_Wout)
    x = x + _L0_ffn_ref(_layernorm(x, axis=-1), L0_ffn_router_w, L0_ffn_rg, L0_ffn_ru, L0_ffn_rd, L0_ffn_sg, L0_ffn_su, L0_ffn_sd)
    x = x + _L1_attn_ref(_layernorm(x, axis=-1), L1_attn_Wq, L1_attn_bq, L1_attn_Wk, L1_attn_bk, L1_attn_Wv, L1_attn_bv, L1_attn_Wo, L1_attn_bo)
    x = x + _L1_xattn_ref(_layernorm(x, axis=-1), ctx_1024, mask_1x1xSxS2_bk0, L1_xattn_Wq, L1_xattn_Wk, L1_xattn_Wv, L1_xattn_Wo, L1_xattn_rel_bias)
    x = x + _L1_ffn_ref(_layernorm(x, axis=-1), L1_ffn_router_w, L1_ffn_router_b, L1_ffn_expert_w, L1_ffn_expert_b)
    return x

_drawn_inputs = setup_inputs


def setup_inputs(seed=0):
    import zlib

    import numpy as np

    out = dict(_drawn_inputs(seed))
    spreads = {'L0_attn_b_gate': (0.0, 0.8),
     'L0_attn_ln_g': (1.0, 0.6),
     'L0_attn_ln_b': (0.0, 0.8),
     'L0_attn_b1': (0.0, 0.8),
     'L0_attn_b2': (0.0, 0.268),
     'L0_xattn_g1': (1.0, 0.2),
     'L0_xattn_b1': (0.0, 0.394),
     'L0_xattn_g2': (1.0, 0.2),
     'L0_xattn_b2': (0.0, 0.307),
     'L1_attn_bq': (0.0, 0.8),
     'L1_attn_bk': (0.0, 2.0),
     'L1_attn_bv': (0.0, 0.675),
     'L1_attn_bo': (0.0, 0.722),
     'L1_ffn_router_b': (0.0, 0.494),
     'L1_ffn_expert_b': (0.0, 0.8)}
    factors = {'L0_attn_w_dw': 8.0,
     'L0_attn_w_pw': 8.0,
     'L0_attn_w_qkv': 8.0,
     'L0_attn_w_o': 8.0,
     'L0_attn_w_gate': 8.0,
     'L0_attn_w_moe_gate': 8.0,
     'L0_attn_w1': 4.181,
     'L0_attn_w2': 3.799,
     'L0_ffn_router_w': 8.0,
     'L0_ffn_rg': 8.0,
     'L0_ffn_ru': 8.0,
     'L0_ffn_rd': 8.0,
     'L0_ffn_sg': 7.009,
     'L0_ffn_su': 6.993,
     'L0_ffn_sd': 6.967,
     'L1_attn_Wq': 8.0,
     'L1_attn_Wk': 8.0,
     'L1_attn_Wv': 7.579,
     'L1_attn_Wo': 3.979,
     'L1_xattn_rel_bias': 200.0,
     'L1_ffn_router_w': 3.013,
     'L1_ffn_expert_w': 2.956}
    for name, (base, spread) in spreads.items():
        noise = np.random.default_rng([zlib.crc32(name.encode()), seed]).standard_normal(out[name].shape)
        drawn = base * np.exp(spread * noise) if base else spread * noise
        out[name] = jnp.asarray(drawn.astype(out[name].dtype))
    for name, factor in factors.items():
        out[name] = (out[name] * factor).astype(out[name].dtype)
    return out
```

```python
from contextlib import ExitStack

import concourse.bass as bass
from concourse import mybir
import numpy as np

F32 = mybir.dt.float32
U32 = mybir.dt.uint32
U8 = mybir.dt.uint8
ALU = mybir.AluOpType
ACT = mybir.ActivationFunctionType
AX = mybir.AxisListType

P = 128
D = 128
SEQ = 64
NSEQ = 64
TOKENS = NSEQ * SEQ
TILES = TOKENS // P
GT = 4
GROUPS = TILES // GT
GB = GT * P // SEQ
N = GT * P
H = 16
HP = H // 2
DH0 = D // H
DHX = 64
INNER = H * DHX
E0 = 4
F0 = 4
E1 = 8
FR = 4
FS = 8
CAP = max(int(1.25 * TOKENS / E1), 1)
SLOTS = E1 * CAP
CT = CAP // P
LOWEST = float(np.finfo(np.float32).min)
RMS_EPS = float(np.finfo(np.float32).eps)
LN_EPS = 1e-5


def stage_semaphore(nc, m, name):
    m.stage_semaphores.append(nc.alloc_semaphore(name=name))
    return m.stage_semaphores[-1]


def reuse_semaphores(nc, m):
    nc.clear_and_free_semaphores(m.stage_semaphores)
    m.stage_semaphores = []
    nc.all_engine_barrier()


def over(ap, axis, count):
    shape = list(ap.shape)
    return ap.unsqueeze(axis).broadcast_to(shape[:axis] + [count] + shape[axis:])


def tiles_of(ap):
    return ap.rearrange("p (t n) -> p t n", n=P)


def seqs_of(ap):
    return ap.rearrange("p (b t) -> p b t", t=SEQ)


class Shared:
    pass


class NormSemaphores:

    def __init__(self, sem, name):
        self.sums = sem(name + "_sums")
        self.stats = sem(name + "_stats")
        self.var = sem(name + "_var")
        self.rstd = sem(name + "_rstd")
        self.normed = sem(name + "_normed")


def normalize(dve, m, g, src, dst, sem, count, before, start=None):
    base = GT * (count * g + before)
    for t in range(GT):
        dve.bn_stats(m.bn[:, t, :], src(t)).then_inc(sem.sums, 1)
    dve.wait_ge(sem.sums, base + GT)
    dve.memset(m.spare[:], 0.0)
    for t in range(GT):
        dve.bn_aggr(m.mean_var[:, t, :], m.bn[:, t, :]).then_inc(sem.stats, 1)
    dve.wait_ge(sem.stats, base + GT)
    dve.tensor_scalar(m.var_eps[:], m.mean_var[:, :, 1], LN_EPS, None, ALU.add).then_inc(sem.var, 1)
    dve.wait_ge(sem.rstd, count * g + before + 1)
    for t in range(GT):
        dve.tensor_scalar(dst(t), src(t), m.mean_var[:, t, 0:1], m.rstd[:, t:t + 1],
                          ALU.subtract, ALU.mult).then_inc(sem.normed, 1)


def inverse_root(pool, m, g, sem, count, before):
    pool.wait_ge(sem.var, count * g + before + 1)
    pool.tensor_tensor(m.rstd[:], m.var_eps[:], m.minus_half[:], ALU.pow).then_inc(sem.rstd, 1)



def linear_attention(nc, m):
    w = m.w
    with ExitStack() as ctx:
        def sb(name, shape):
            return ctx.enter_context(nc.sbuf_tensor("la_" + name, shape, F32))

        def sem(name):
            return stage_semaphore(nc, m, "la_" + name)

        xn = sb("xn", [P, GT, D])
        hT = sb("hT", [P, N])
        conv = sb("conv", [P, N])
        x1T = sb("x1T", [P, N])
        delta = sb("delta", [P, N])
        by_cos = sb("by_cos", [P, 2, N])
        by_sin = sb("by_sin", [P, 2, N])
        rot = sb("rot", [P, 2, N])
        low = sb("low", [P, 2, N])
        phi = sb("phi", [P, 2, N])
        k_prefix = sb("k_prefix", [P, N])
        qk = sb("qk", [P, N])
        rden = sb("rden", [P, N])
        qheads = sb("qheads", [P, 2, H * SEQ])
        scores = sb("scores", [P, 2, HP * SEQ])
        vheads = sb("vheads", [P, GB, HP * (P + 2 * DH0)])
        attnT = sb("attnT", [P, N])
        gate = sb("gate", [P, N])
        x2T = sb("x2T", [P, N])
        x2 = sb("x2", [P, GT, D])
        h2T = sb("h2T", [P, N])
        top = sb("top", [P, GT])
        gw = sb("gw", [P, GT, E0])
        gsum = sb("gsum", [P, GT])
        hid = sb("hid", [P, 2, F0, N])
        bank = m.bank

        ln = NormSemaphores(sem, "ln")
        zeroed = sem("zeroed")
        hT_turned = sem("hT_turned")
        hT_ready = sem("hT_ready")
        conv_part = sem("conv_part")
        pw_done = sem("pw_done")
        x1_ready = sem("x1_ready")
        delta_ready = sem("delta_ready")
        qk_done = sem("qk_done")
        v_done = sem("v_done")
        v_ready = sem("v_ready")
        rope_part = sem("rope_part")
        rot_ready = sem("rot_ready")
        low_ready = sem("low_ready")
        exp_ready = sem("exp_ready")
        phi_ready = sem("phi_ready")
        prefix_ready = sem("prefix_ready")
        qk_ready = sem("qk_ready")
        den_done = sem("den_done")
        den_ready = sem("den_ready")
        qheads_ready = sem("qheads_ready")
        scores_done = sem("scores_done")
        scores_ready = sem("scores_ready")
        num_done = sem("num_done")
        attn_ready = sem("attn_ready")
        out_done = sem("out_done")
        gate_ready = sem("gate_ready")
        gated = sem("gated")
        x2T_ready = sem("x2T_ready")
        x2_turned = sem("x2_turned")
        x2_ready = sem("x2_ready")
        x2_added = sem("x2_added")
        h2_turned = sem("h2_turned")
        h2_ready = sem("h2_ready")
        logits_done = sem("logits_done")
        gw_step = sem("gw_step")
        gw_exp = sem("gw_exp")
        hid_done = sem("hid_done")
        hid_ready = sem("hid_ready")
        expert_done = sem("expert_done")
        expert_used = sem("expert_used")

        def vdiag(par):
            v = vheads[SEQ * par:SEQ * par + SEQ].rearrange("p b (h c) -> p b h c", c=P + 2 * DH0)
            return v[:, :, :, DH0 * par:DH0 * par + DH0]

        with nc.Block() as block:

            @block.tensor
            def _(pe):
                pe.wait_ge(m.loaded_linear, m.loaded_linear_all)
                pe.wait_ge(m.ready_constants, m.ready_constants_all)
                with pe.Fori(0, GROUPS) as g:
                    for t in range(GT):
                        pe.wait_ge(ln.normed, GT * 2 * g + t + 1)
                        mm = pe.transpose(bank(0)[:, P * t:P * t + P], xn[:, t, :], w["ident"][:])
                    mm.then_inc(hT_turned, 1)
                    pe.wait_ge(conv_part, 3 * g + 3)
                    pe.matmul(bank(1), w["pw"][:], conv[:], start=True, stop=True).then_inc(pw_done, 1)
                    pe.wait_ge(x1_ready, g + 1)
                    for n in range(4):
                        mm = pe.matmul(bank(2 + n), w["qk"][:, n, :], x1T[:], start=True, stop=True)
                    mm.then_inc(qk_done, 1)
                    for b in range(GB):
                        for par in range(2):
                            mm = pe.matmul(bank(6)[SEQ * par:SEQ * par + SEQ, HP * DH0 * b:HP * DH0 * (b + 1)],
                                           x1T[:, SEQ * b:SEQ * b + SEQ], w["v0"][:, par, :], start=True, stop=True)
                    mm.then_inc(v_done, 1)
                    pe.wait_ge(qk_ready, g + 1)
                    pe.matmul(bank(7), w["same_head"][:], qk[:], start=True, stop=True).then_inc(den_done, 1)

                    def numerator(b):
                        pe.wait_ge(scores_ready, GB * g + b + 1)
                        for hp in range(HP):
                            mm = pe.matmul(bank(2)[:, SEQ * b:SEQ * b + SEQ], vheads[:, b, P * hp:P * hp + P],
                                           scores[:, b % 2, SEQ * hp:SEQ * hp + SEQ],
                                           start=(hp == 0), stop=(hp == HP - 1))
                        mm.then_inc(num_done, 1)

                    for b in range(GB):
                        pe.wait_ge(qheads_ready, GB * g + b + 1)
                        if b >= 2:
                            pe.wait_ge(scores_ready, GB * g + b - 1)
                        for par in range(2):
                            mm = pe.matmul(bank(4 + b % 2)[SEQ * par:SEQ * par + SEQ, :],
                                           phi[:, 1, SEQ * b:SEQ * b + SEQ],
                                           qheads[:, b % 2, HP * SEQ * par:HP * SEQ * (par + 1)],
                                           start=True, stop=True)
                        mm.then_inc(scores_done, 1)
                        if b == 0:
                            pe.wait_ge(v_ready, 2 * g + 2)
                        else:
                            numerator(b - 1)
                    numerator(GB - 1)
                    pe.wait_ge(delta_ready, g + 1)
                    pe.matmul(bank(1), w["gate"][:], delta[:], start=True, stop=True)
                    pe.wait_ge(attn_ready, g + 1)
                    pe.matmul(bank(3), w["o0"][:], attnT[:], start=True, stop=True).then_inc(out_done, 1)
                    pe.wait_ge(x2T_ready, g + 1)
                    for t in range(GT):
                        mm = pe.transpose(bank(0)[:, P * t:P * t + P], x2T[:, P * t:P * t + P], w["ident"][:])
                    mm.then_inc(x2_turned, 1)
                    for t in range(GT):
                        pe.wait_ge(ln.normed, GT * (2 * g + 1) + t + 1)
                        mm = pe.transpose(bank(6)[:, P * t:P * t + P], xn[:, t, :], w["ident"][:])
                    mm.then_inc(h2_turned, 1)
                    pe.wait_ge(h2_ready, g + 1)
                    for t in range(GT):
                        mm = pe.matmul(bank(7)[:, E0 * t:E0 * t + E0], h2T[:, P * t:P * t + P], w["moe_gate"][:],
                                       start=True, stop=True)
                    mm.then_inc(logits_done, 1)

                    def expert_out(e):
                        pe.wait_ge(hid_ready, F0 * (E0 * g + e) + F0)
                        if e >= 2:
                            pe.wait_ge(expert_used, GT * (E0 * g + e - 1))
                        for t in range(GT):
                            out = bank(e % 2)[:, P * t:P * t + P]
                            pe.matmul(out, w["ones"][0:1, :], w["b2"][0:1, e, :], start=True, stop=False)
                            for f in range(F0):
                                mm = pe.matmul(out, hid[:, e % 2, f, P * t:P * t + P], w["w2"][:, e, f, :],
                                               start=False, stop=(f == F0 - 1))
                        mm.then_inc(expert_done, 1)

                    for e in range(E0):
                        for f in range(F0):
                            if e >= 1:
                                pe.wait_ge(hid_ready, F0 * (E0 * g + e - 1) + f + 1)
                            pe.matmul(bank(2 + f), w["w1"][:, e, f, :], h2T[:], start=True, stop=True)\
                                .then_inc(hid_done, 1)
                        if e >= 1:
                            expert_out(e - 1)
                    expert_out(E0 - 1)

            @block.scalar
            def _(act):
                act.wait_ge(m.loaded_linear, m.loaded_linear_all)
                act.wait_ge(zeroed, 2)
                with act.Fori(0, GROUPS) as g:
                    act.wait_ge(hT_turned, g + 1)
                    act.activation(hT[:], bank(0), ACT.Copy).then_inc(hT_ready, 1)
                    act.wait_ge(v_done, g + 1)
                    for par in range(2):
                        src = bank(6)[SEQ * par:SEQ * par + SEQ, :].rearrange("p (b h c) -> p b h c", h=HP, c=DH0)
                        act.activation(vdiag(par), src, ACT.Copy).then_inc(v_ready, 1)
                    act.wait_ge(low_ready, g + 1)
                    act.activation(low[:], low[:], ACT.Exp).then_inc(exp_ready, 1)
                    act.wait_ge(out_done, g + 1)
                    act.activation(gate[:], bank(1), ACT.Sigmoid, bias=w["b_gate"][:, 0:1]).then_inc(gate_ready, 1)
                    act.wait_ge(x2_turned, g + 1)
                    act.activation(x2[:], tiles_of(bank(0)), ACT.Copy).then_inc(x2_ready, 1)
                    act.wait_ge(h2_turned, g + 1)
                    act.activation(h2T[:], bank(6), ACT.Identity, bias=w["ln_b"][:, 0:1], scale=w["ln_g"][:, 0:1])\
                        .then_inc(h2_ready, 1)
                    act.wait_ge(gw_step, 5 * g + 2)
                    act.activation(gw[:], gw[:], ACT.Exp).then_inc(gw_exp, 1)
                    for e in range(E0):
                        for f in range(F0):
                            act.wait_ge(hid_done, F0 * (E0 * g + e) + f + 1)
                            if f == 0 and e >= 2:
                                act.wait_ge(expert_done, E0 * g + e - 1)
                            act.activation(hid[:, e % 2, f, :], bank(2 + f), ACT.Silu,
                                           bias=w["b1"][:, F0 * e + f:F0 * e + f + 1]).then_inc(hid_ready, 1)

            @block.gpsimd
            def _(pool):
                pool.memset(vheads[:], 0.0).then_inc(zeroed, 1)
                pool.memset(delta[:], 0.0).then_inc(zeroed, 1)
                pool.wait_ge(m.loaded_linear, m.loaded_linear_all)
                with pool.Fori(0, GROUPS) as g:
                    inverse_root(pool, m, g, ln, 2, 0)
                    pool.wait_ge(zeroed, 2)
                    pool.wait_ge(x1_ready, g + 1)
                    x1 = seqs_of(x1T[:])
                    pool.tensor_tensor(seqs_of(delta[:])[:, :, 1:], x1[:, :, 1:], x1[:, :, :SEQ - 1],
                                       ALU.subtract).then_inc(delta_ready, 1)
                    pool.wait_ge(rope_part, 2 * g + 2)
                    pool.tensor_tensor(rot[:], by_cos[:], by_sin[:], ALU.add).then_inc(rot_ready, 1)
                    pool.wait_ge(phi_ready, g + 1)
                    for b in range(GB):
                        if b >= 2:
                            pool.wait_ge(scores_done, GB * g + b - 1)
                        q = over(phi[:, 0, SEQ * b:SEQ * b + SEQ], 1, H)
                        pool.tensor_tensor(seqs_of(qheads[:, b % 2, :]), q, over(w["head_rows"][:], 2, SEQ),
                                           ALU.mult).then_inc(qheads_ready, 1)
                    inverse_root(pool, m, g, ln, 2, 1)
                    pool.wait_ge(x2_ready, g + 1)
                    rows = m.X[:, bass.ds(GT * g, GT), :]
                    pool.tensor_tensor(rows, rows, x2[:], ALU.add).then_inc(x2_added, 1)

            @block.vector
            def _(dve):
                dve.wait_ge(m.loaded_x, m.loaded_x_all)
                dve.wait_ge(m.loaded_linear, m.loaded_linear_all)
                with dve.Fori(0, GROUPS) as g:
                    normalize(dve, m, g, lambda t: m.X[:, bass.ds(GT * g + t, 1), :], lambda t: xn[:, t, :],
                              ln, 2, 0)
                    dve.wait_ge(hT_ready, g + 1)
                    h, y = seqs_of(hT[:]), seqs_of(conv[:])
                    dve.tensor_scalar(conv[:], hT[:], w["dw"][:, 2:3], None, ALU.mult).then_inc(conv_part, 1)
                    for n, back in enumerate((1, 2)):
                        dve.wait_ge(conv_part, 3 * g + n + 1)
                        dve.scalar_tensor_tensor(out=y[:, :, back:], in0=h[:, :, :SEQ - back],
                                                 scalar=w["dw"][:, 2 - back:3 - back], in1=y[:, :, back:],
                                                 op0=ALU.mult, op1=ALU.add).then_inc(conv_part, 1)
                    dve.wait_ge(pw_done, g + 1)
                    dve.tensor_tensor(x1T[:], hT[:], bank(1), ALU.add).then_inc(x1_ready, 1)
                    dve.wait_ge(qk_done, g + 1)
                    for out, first, table in ((by_cos, 2, w["cos"]), (by_sin, 4, w["sin"])):
                        dve.tensor_tensor(seqs_of(out[:].rearrange("p a n -> p (a n)")),
                                          seqs_of(m.ps[:, first:first + 2, :].rearrange("p a n -> p (a n)")),
                                          over(table[:], 1, 2 * GB), ALU.mult).then_inc(rope_part, 1)
                    dve.wait_ge(rot_ready, g + 1)
                    dve.tensor_scalar(low[:], rot[:], 0.0, None, ALU.min).then_inc(low_ready, 1)
                    dve.wait_ge(exp_ready, g + 1)
                    dve.scalar_tensor_tensor(out=phi[:], in0=rot[:], scalar=0.0, in1=low[:],
                                             op0=ALU.max, op1=ALU.add).then_inc(phi_ready, 1)
                    dve.wait_ge(phi_ready, g + 1)
                    dve.tensor_tensor_scan(k_prefix[:], w["not_first"][:], phi[:, 1, :], 0.0,
                                           ALU.mult, ALU.add).then_inc(prefix_ready, 1)
                    dve.wait_ge(prefix_ready, g + 1)
                    dve.tensor_tensor(qk[:], phi[:, 0, :], k_prefix[:], ALU.mult).then_inc(qk_ready, 1)
                    dve.wait_ge(den_done, g + 1)
                    dve.tensor_scalar(rden[:], bank(7), 1e-6, None, ALU.add).then_inc(den_ready, 1)
                    for b in range(GB):
                        if b == 2:
                            dve.wait_ge(den_ready, 2 * g + 1)
                            dve.reciprocal(rden[:], rden[:]).then_inc(den_ready, 1)
                        dve.wait_ge(scores_done, GB * g + b + 1)
                        if b >= 2:
                            dve.wait_ge(num_done, GB * g + b - 1)
                        dve.tensor_tensor(seqs_of(scores[:, b % 2, :]), seqs_of(bank(4 + b % 2)),
                                          over(w["causal_kq"][:], 1, HP), ALU.mult).then_inc(scores_ready, 1)
                    dve.wait_ge(den_ready, 2 * g + 2)
                    dve.wait_ge(num_done, GB * g + GB)
                    dve.tensor_tensor(attnT[:], bank(2), rden[:], ALU.mult).then_inc(attn_ready, 1)
                    dve.wait_ge(gate_ready, g + 1)
                    dve.tensor_tensor(gate[:], bank(3), gate[:], ALU.mult).then_inc(gated, 1)
                    dve.wait_ge(gated, g + 1)
                    dve.tensor_tensor(x2T[:], x1T[:], gate[:], ALU.add).then_inc(x2T_ready, 1)
                    dve.wait_ge(x2_ready, g + 1)
                    normalize(dve, m, g, lambda t: x2[:, t, :], lambda t: xn[:, t, :], ln, 2, 1)
                    dve.wait_ge(logits_done, g + 1)
                    lg = bank(7)[:, 0:GT * E0].rearrange("p (t e) -> p t e", e=E0)
                    dve.tensor_reduce(top[:], lg, AX.X, ALU.max).then_inc(gw_step, 1)
                    dve.wait_ge(gw_step, 5 * g + 1)
                    dve.tensor_tensor(gw[:], lg, over(top[:], 2, E0), ALU.subtract).then_inc(gw_step, 1)
                    dve.wait_ge(gw_exp, g + 1)
                    dve.tensor_reduce(gsum[:], gw[:], AX.X, ALU.add).then_inc(gw_step, 1)
                    dve.wait_ge(gw_step, 5 * g + 3)
                    dve.reciprocal(gsum[:], gsum[:]).then_inc(gw_step, 1)
                    dve.wait_ge(gw_step, 5 * g + 4)
                    dve.tensor_tensor(gw[:], gw[:], over(gsum[:], 2, E0), ALU.mult).then_inc(gw_step, 1)
                    dve.wait_ge(gw_step, 5 * g + 5)
                    dve.wait_ge(x2_added, g + 1)
                    for e in range(E0):
                        dve.wait_ge(expert_done, E0 * g + e + 1)
                        for t in range(GT):
                            if e >= 1:
                                dve.wait_ge(expert_used, GT * (E0 * g + e - 1) + t + 1)
                            row = m.X[:, bass.ds(GT * g + t, 1), :]
                            dve.scalar_tensor_tensor(out=row, in0=bank(e % 2)[:, P * t:P * t + P].unsqueeze(1),
                                                     scalar=gw[:, t, e:e + 1], in1=row,
                                                     op0=ALU.mult, op1=ALU.add).then_inc(expert_used, 1)


def latent_attention(nc, m):
    w = m.w
    KEYS = 2 * SEQ
    UNITS = 2 * GT
    UH = HP // 2
    PROJ = 40
    with ExitStack() as ctx:
        def sb(name, shape):
            return ctx.enter_context(nc.sbuf_tensor("xa_" + name, shape, F32))

        def sem(name):
            return stage_semaphore(nc, m, "xa_" + name)

        cn = sb("cn", [P, GT, D])
        xn = sb("xn", [P, GT, D])
        lat = sb("lat", [P, GT, D])
        kvT = sb("kvT", [P, GB, KEYS])
        qT = sb("qT", [P, HP, N])
        kT = sb("kT", [P, HP, GB * KEYS])
        v = sb("v", [P, GB, INNER])
        probs = sb("probs", [P, 2, 2 * UH, KEYS])
        probsT = sb("probsT", [P, 2, 2 * UH, P])
        top = sb("top", [P, 2, 2 * UH])
        total = sb("total", [P, 2, 2 * UH])
        attnT = sb("attnT", [P, 2, HP, P])
        bank = m.bank

        ln = NormSemaphores(sem, "ln")
        kv_turned = sem("kv_turned")
        kv_ready = sem("kv_ready")
        proj_done = sem("proj_done")
        proj_even = sem("proj_even")
        proj_odd = sem("proj_odd")
        scores_done = sem("scores_done")
        top_ready = sem("top_ready")
        less_top = sem("less_top")
        exp_ready = sem("exp_ready")
        sum_ready = sem("sum_ready")
        inverse_ready = sem("inverse_ready")
        probs_ready = sem("probs_ready")
        probs_turned = sem("probs_turned")
        probsT_ready = sem("probsT_ready")
        attn_done = sem("attn_done")
        attn_ready = sem("attn_ready")
        out_done = sem("out_done")
        x_added = sem("x_added")

        def heads(u):
            for par in range(2):
                for n in range(UH):
                    yield UH * par + n, par, n, UH * (u % 2) + n

        def projected(n):
            if n < 8:
                return qT[:, n, :]
            if n < 24:
                return kT[:, (n - 8) // 2, N * (n % 2):N * (n % 2 + 1)]
            return v[:, (n - 24) // 2, N * (n % 2):N * (n % 2 + 1)]

        def proj_bank(n):
            return bank(n % 4 + (4 if n >= 24 else 0))

        with nc.Block() as block:

            @block.tensor
            def _(pe):
                pe.wait_ge(m.loaded_latent, m.loaded_latent_all)
                with pe.Fori(0, GROUPS) as g:
                    for n, src in ((0, cn), (2, lat)):
                        for t in range(GT):
                            pe.wait_ge(ln.normed, GT * (3 * g + n) + t + 1)
                            mm = pe.transpose(bank(4 + n // 2)[:, P * t:P * t + P], src[:, t, :], w["ident"][:])
                        mm.then_inc(kv_turned, 1)
                    pe.wait_ge(kv_ready, 2 * g + 2)
                    for n in range(PROJ):
                        if n >= 4:
                            pe.wait_ge((proj_even, proj_odd)[n % 2], PROJ // 2 * g + (n - 4) // 2 + 1)
                        if n < 8:
                            lhsT, rhs = w["xq"][:, P * n:P * n + P], kvT[:, :, SEQ:]
                        elif n < 24:
                            lhsT = w["xk"][:, P * ((n - 8) // 2):P * ((n - 8) // 2 + 1)]
                            rhs = kvT[:, GB // 2 * (n % 2):GB // 2 * (n % 2 + 1), :]
                        else:
                            lhsT, rhs = kvT[:, (n - 24) // 2, :], w["xv"][:, N * (n % 2):N * (n % 2 + 1)]
                        pe.matmul(proj_bank(n), lhsT, rhs, start=True, stop=True).then_inc(proj_done, 1)

                    def score(u):
                        for _, par, n, hp in heads(u):
                            rows = slice(DHX * par, DHX * par + DHX)
                            for b in range(2):
                                seq = 2 * (u // 2) + b
                                mm = pe.matmul(bank(2 * (u % 2) + par)[SEQ * b:SEQ * b + SEQ, KEYS * n:KEYS * (n + 1)],
                                               qT[rows, hp, SEQ * seq:SEQ * seq + SEQ],
                                               kT[rows, hp, KEYS * seq:KEYS * (seq + 1)], start=True, stop=True)
                        mm.then_inc(scores_done, 1)

                    def turn(u):
                        if u == 0:
                            pe.wait_ge(proj_even, PROJ // 2 * g + PROJ // 2)
                            pe.wait_ge(proj_odd, PROJ // 2 * g + PROJ // 2)
                        pe.wait_ge(probs_ready, UNITS * g + u + 1)
                        if u >= 1:
                            pe.wait_ge(probsT_ready, UNITS * g + u)
                        for a in range(2 * UH):
                            mm = pe.transpose(bank(4 + a // UH)[:, P * (a % UH):P * (a % UH + 1)],
                                              probs[:, u % 2, a, :], w["ident"][:])
                        mm.then_inc(probs_turned, 1)

                    def attend(u):
                        pe.wait_ge(probsT_ready, UNITS * g + u + 1)
                        if u >= 1:
                            pe.wait_ge(attn_ready, UNITS * g + u)
                        for a, par, n, hp in heads(u):
                            head = 2 * hp + par
                            for b in range(2):
                                mm = pe.matmul(bank(6)[DHX * par:DHX * par + DHX, P * n + SEQ * b:P * n + SEQ * (b + 1)],
                                               v[:, 2 * (u // 2) + b, DHX * head:DHX * (head + 1)],
                                               probsT[:, u % 2, a, SEQ * b:SEQ * b + SEQ], start=True, stop=True)
                        mm.then_inc(attn_done, 1)

                    def project(t):
                        pe.wait_ge(attn_ready, UNITS * g + 2 * t + 2)
                        for hp in range(HP):
                            mm = pe.matmul(bank(7)[:, P * t:P * t + P], attnT[:, t % 2, hp, :], w["xo"][:, hp, :],
                                           start=(hp == 0), stop=(hp == HP - 1))
                        mm.then_inc(out_done, 1)

                    for u in range(UNITS + 3):
                        if u < UNITS:
                            score(u)
                        if 1 <= u <= UNITS:
                            turn(u - 1)
                        if 2 <= u < UNITS + 2:
                            attend(u - 2)
                        if u >= 4 and u % 2 == 0:
                            project(u // 2 - 2)

            @block.scalar
            def _(act):
                act.wait_ge(m.loaded_latent, m.loaded_latent_all)
                with act.Fori(0, GROUPS) as g:
                    for n in range(2):
                        act.wait_ge(kv_turned, 2 * g + n + 1)
                        act.activation(kvT[:, :, SEQ * n:SEQ * n + SEQ], seqs_of(bank(4 + n)), ACT.Identity,
                                       bias=w["x_affine"][:, 2 * n + 1:2 * n + 2], scale=w["x_affine"][:, 2 * n:2 * n + 1])\
                            .then_inc(kv_ready, 1)
                    for n in range(0, PROJ, 2):
                        act.wait_ge(proj_done, PROJ * g + n + 1)
                        act.activation(projected(n), proj_bank(n), ACT.Copy).then_inc(proj_even, 1)
                    for u in range(UNITS + 2):
                        if u < UNITS:
                            act.wait_ge(less_top, UNITS * g + u + 1)
                            act.activation(probs[:, u % 2], probs[:, u % 2], ACT.Exp, scale=DHX ** -0.5)\
                                .then_inc(exp_ready, 1)
                        if 1 <= u <= UNITS:
                            act.wait_ge(probs_turned, UNITS * g + u)
                            if u >= 3:
                                act.wait_ge(attn_done, UNITS * g + u - 2)
                            act.activation(probsT[:, (u - 1) % 2].rearrange("p a n -> p (a n)"),
                                           m.ps[:, 4:6, :].rearrange("p a n -> p (a n)"), ACT.Copy)\
                                .then_inc(probsT_ready, 1)
                        if u >= 2:
                            n = u - 2
                            act.wait_ge(attn_done, UNITS * g + n + 1)
                            if n >= 4 and n % 2 == 0:
                                act.wait_ge(out_done, GT * g + n // 2 - 1)
                            act.activation(attnT[:, n // 2 % 2, UH * (n % 2):UH * (n % 2 + 1), :], tiles_of(bank(6)),
                                           ACT.Copy).then_inc(attn_ready, 1)

            @block.gpsimd
            def _(pool):
                with pool.Fori(0, GROUPS) as g:
                    for n in range(3):
                        inverse_root(pool, m, g, ln, 3, n)
                    for u in range(UNITS):
                        pool.wait_ge(inverse_ready, UNITS * g + u + 1)
                        pool.tensor_tensor(probs[:, u % 2], probs[:, u % 2], over(total[:, u % 2], 2, KEYS),
                                           ALU.mult).then_inc(probs_ready, 1)

            @block.vector
            def _(dve):
                dve.wait_ge(m.loaded_ctx, 16)
                with dve.Fori(0, GROUPS) as g:
                    normalize(dve, m, g, lambda t: m.C[:, bass.ds(GT * g + t, 1), :], lambda t: cn[:, t, :], ln, 3, 0)
                    normalize(dve, m, g, lambda t: m.X[:, bass.ds(GT * g + t, 1), :], lambda t: xn[:, t, :], ln, 3, 1)
                    dve.wait_ge(ln.normed, GT * (3 * g + 2))
                    normalize(dve, m, g, lambda t: xn[:, t, :], lambda t: lat[:, t, :], ln, 3, 2)
                    for n in range(1, PROJ, 2):
                        dve.wait_ge(proj_done, PROJ * g + n + 1)
                        dve.tensor_copy(projected(n), proj_bank(n)).then_inc(proj_odd, 1)
                    for u in range(UNITS + 1):
                        if u < UNITS:
                            s = m.ps[:, 2 * (u % 2):2 * (u % 2) + 2, :].rearrange("p a (h k) -> p (a h) k", k=KEYS)
                            dve.wait_ge(scores_done, UNITS * g + u + 1)
                            dve.tensor_reduce(top[:, u % 2], s, AX.X, ALU.max).then_inc(top_ready, 1)
                            if u >= 2:
                                dve.wait_ge(probs_turned, UNITS * g + u - 1)
                            dve.wait_ge(top_ready, UNITS * g + u + 1)
                            dve.tensor_tensor(probs[:, u % 2], s, over(top[:, u % 2], 2, KEYS), ALU.subtract)\
                                .then_inc(less_top, 1)
                        if u >= 1:
                            n = u - 1
                            dve.wait_ge(exp_ready, UNITS * g + n + 1)
                            dve.tensor_reduce(total[:, n % 2], probs[:, n % 2], AX.X, ALU.add).then_inc(sum_ready, 1)
                            dve.wait_ge(sum_ready, UNITS * g + n + 1)
                            dve.reciprocal(total[:, n % 2], total[:, n % 2]).then_inc(inverse_ready, 1)
                    dve.wait_ge(out_done, GT * g + GT)
                    rows = m.X[:, bass.ds(GT * g, GT), :]
                    dve.tensor_tensor(rows, tiles_of(bank(7)), rows, ALU.add).then_inc(x_added, 1)
                    dve.wait_ge(x_added, g + 1)


def routed_experts(nc, m):
    with ExitStack() as ctx:
        m.pair_weights = ctx.enter_context(nc.sbuf_tensor("pair_weights", [P, 2, TILES + GT], F32))
        m.pair_slots = ctx.enter_context(nc.sbuf_tensor("pair_slots", [P, 2, TILES + GT], U32))
        route_and_share(nc, m)
        run_experts(nc, m)
        combine_experts(nc, m)


def route_and_share(nc, m):
    w = m.w
    PAIRS = 2 * GT
    ROUTE = 31
    with ExitStack() as ctx:
        def sb(name, shape, dtype=F32):
            return ctx.enter_context(nc.sbuf_tensor("rt_" + name, shape, dtype))

        def sem(name):
            return stage_semaphore(nc, m, "rt_" + name)

        xn = sb("xn", [P, GT, D])
        square = sb("square", [P, GT, D])
        square_sum = sb("square_sum", [P, GT])
        mean_square = sb("mean_square", [P, GT])
        inverse_rms = sb("inverse_rms", [P, GT])
        xT = sb("xT", [P, N])
        prob = sb("prob", [P, GT, E1])
        top = sb("top", [P, GT])
        ranked = sb("ranked", [P, GT, E1])
        index = sb("index", [P, GT, E1], U32)
        pick = sb("pick", [P, 2, GT])
        chosen = sb("chosen", [P, PAIRS, E1])
        mask = sb("mask", [P, GT, E1])
        before = sb("before", [P, E1])
        rank = sb("rank", [P, GT, E1])
        slot_of = sb("slot_of", [P, GT, E1])
        pair_rank = sb("pair_rank", [P, PAIRS, E1])
        pair_slot = sb("pair_slot", [P, PAIRS, E1])
        rank8 = sb("rank8", [P, PAIRS])
        slot8 = sb("slot8", [P, PAIRS])
        slot_index = sb("slot_index", [P, PAIRS], U32)
        silu = sb("silu", [P, 2, N])
        mid = sb("mid", [P, FS, N])
        bank = m.bank

        ln = NormSemaphores(sem, "ln")
        cleared = sem("cleared")
        xT_turned = sem("xT_turned")
        xT_ready = sem("xT_ready")
        squared = sem("squared")
        mean_ready = sem("mean_ready")
        rms_ready = sem("rms_ready")
        logits_done = sem("logits_done")
        routed = sem("routed")
        exp_ready = sem("exp_ready")
        rank_done = sem("rank_done")
        scattered = sem("scattered")
        gate_up_done = sem("gate_up_done")
        silu_ready = sem("silu_ready")
        mid_ready = sem("mid_ready")
        shared_done = sem("shared_done")
        shared_added = sem("shared_added")

        with nc.Block() as block:

            @block.sync
            def _(sp):
                sp.dma_start(m.biased_weights[:], m.dram["biased"]).then_inc(m.loaded_biased, 16)
                sp.dma_start(m.top_weights[:], m.dram["top"]).then_inc(m.loaded_top, 16)

            @block.tensor
            def _(pe):
                pe.wait_ge(m.loaded_shared, 16)
                with pe.Fori(0, GROUPS) as g:
                    for t in range(GT):
                        pe.wait_ge(ln.normed, GT * g + t + 1)
                        mm = pe.transpose(bank(0)[:, P * t:P * t + P], xn[:, t, :], w["ident"][:])
                    mm.then_inc(xT_turned, 1)
                    pe.wait_ge(xT_ready, g + 1)
                    for t in range(GT):
                        mm = pe.matmul(bank(1)[:, E1 * t:E1 * t + E1], xT[:, P * t:P * t + P], w["router"][:],
                                       start=True, stop=True)
                    mm.then_inc(logits_done, 1)

                    def ranks():
                        pe.wait_ge(routed, ROUTE * g + 20)
                        for t in range(GT + 1):
                            out = bank(2)[:, E1 * t:E1 * t + E1]
                            for s in range(min(t + 1, GT)):
                                mm = pe.matmul(out, (w["earlier"] if s == t else w["ones"])[:], mask[:, s, :],
                                               start=(s == 0), stop=(s == min(t, GT - 1)))
                        mm.then_inc(rank_done, 1)

                    for f in range(FS):
                        if f >= 2:
                            pe.wait_ge(mid_ready, FS * g + f - 1)
                        pe.matmul(bank(4 + 2 * (f % 2)), w["sg"][:, f, :], xT[:], start=True, stop=True)
                        pe.matmul(bank(5 + 2 * (f % 2)), w["su"][:, f, :], xT[:], start=True, stop=True)\
                            .then_inc(gate_up_done, 1)
                        if f == 2:
                            ranks()
                    for t in range(GT):
                        for f in range(FS):
                            if t == 0:
                                pe.wait_ge(mid_ready, FS * g + f + 1)
                            mm = pe.matmul(bank(3)[:, P * t:P * t + P], mid[:, f, P * t:P * t + P], w["sd"][:, f, :],
                                           start=(f == 0), stop=(f == FS - 1))
                    mm.then_inc(shared_done, 1)

            @block.scalar
            def _(act):
                with act.Fori(0, GROUPS) as g:
                    for t in range(GT):
                        act.wait_ge(ln.normed, GT * g + t + 1)
                        act.activation(square[:, t, :], xn[:, t, :], ACT.Square, accum_out=square_sum[:, t:t + 1])\
                            .then_inc(squared, 1)
                    act.wait_ge(xT_turned, g + 1)
                    act.activation(xT[:], bank(0), ACT.Copy).then_inc(xT_ready, 1)
                    act.wait_ge(routed, ROUTE * g + 3)
                    act.activation(prob[:], prob[:], ACT.Exp).then_inc(exp_ready, 1)
                    for f in range(FS):
                        act.wait_ge(gate_up_done, FS * g + f + 1)
                        act.activation(silu[:, f % 2, :], bank(4 + 2 * (f % 2)), ACT.Silu).then_inc(silu_ready, 1)

            @block.gpsimd
            def _(pool):
                pool.memset(before[:], 0.0).then_inc(cleared, 1)
                pool.memset(m.pair_weights[:, :, TILES:], 0.0).then_inc(cleared, 1)
                pool.memset(m.pair_slots[:, :, TILES:], 0).then_inc(cleared, 1)
                pool.wait_ge(m.slots_cleared, 32)
                with pool.Fori(0, GROUPS) as g:
                    inverse_root(pool, m, g, ln, 1, 0)
                    pool.wait_ge(mean_ready, g + 1)
                    pool.tensor_tensor(inverse_rms[:], mean_square[:], m.minus_half[:], ALU.pow).then_inc(rms_ready, 1)
                    pool.wait_ge(routed, ROUTE * g + 30)
                    pool.tensor_tensor(m.pool_spare[:, 0, :], m.minus_half[:], m.minus_half[:], ALU.add)
                    for n in range(PAIRS):
                        pool.indirect_dma_start(
                            out=m.slot_rows, out_offset=bass.IndirectOffsetOnAxis(ap=slot_index[:, n:n + 1], axis=0),
                            in_=xn[:, n % GT, :], in_offset=None, bounds_check=SLOTS - 1, oob_is_err=False)\
                            .then_inc(scattered, 16)

            @block.vector
            def _(dve):
                dve.wait_ge(cleared, 3)
                with dve.Fori(0, GROUPS) as g:
                    def step(n):
                        dve.wait_ge(routed, ROUTE * g + n)

                    normalize(dve, m, g, lambda t: m.X[:, bass.ds(GT * g + t, 1), :], lambda t: xn[:, t, :], ln, 1, 0)
                    dve.wait_ge(squared, GT * g + GT)
                    dve.tensor_scalar(mean_square[:], square_sum[:], 1.0 / D, RMS_EPS, ALU.mult, ALU.add)\
                        .then_inc(mean_ready, 1)
                    dve.wait_ge(logits_done, g + 1)
                    dve.wait_ge(rms_ready, g + 1)
                    lg = bank(1)[:, 0:GT * E1].rearrange("p (t e) -> p t e", e=E1)
                    dve.tensor_tensor(prob[:], lg, over(inverse_rms[:], 2, E1), ALU.mult).then_inc(routed, 1)
                    step(1)
                    dve.tensor_reduce(top[:], prob[:], AX.X, ALU.max).then_inc(routed, 1)
                    step(2)
                    dve.tensor_tensor(prob[:], prob[:], over(top[:], 2, E1), ALU.subtract).then_inc(routed, 1)
                    dve.wait_ge(exp_ready, g + 1)
                    dve.tensor_reduce(top[:], prob[:], AX.X, ALU.add).then_inc(routed, 1)
                    step(4)
                    dve.reciprocal(top[:], top[:]).then_inc(routed, 1)
                    step(5)
                    dve.tensor_tensor(prob[:], prob[:], over(top[:], 2, E1), ALU.mult).then_inc(routed, 1)
                    step(6)
                    dve.memset(m.spare[:], 0.0)
                    for t in range(GT):
                        dve.max(ranked[:, t, :], prob[:, t, :]).then_inc(routed, 1)
                    step(10)
                    dve.memset(m.spare[:], 0.0)
                    for t in range(GT):
                        dve.max_index(index[:, t, :], ranked[:, t, :], prob[:, t, :]).then_inc(routed, 1)
                    dve.tensor_tensor(top[:], ranked[:, :, 0], ranked[:, :, 1], ALU.add).then_inc(routed, 1)
                    step(15)
                    dve.reciprocal(top[:], top[:]).then_inc(routed, 1)
                    step(16)
                    dve.tensor_tensor(m.pair_weights[:, :, bass.ds(GT * g, GT)],
                                      ranked[:, :, 0:2].rearrange("p t j -> p j t"), over(top[:], 1, 2), ALU.mult)\
                        .then_inc(routed, 1)
                    dve.tensor_copy(pick[:], index[:, :, 0:2].rearrange("p t j -> p j t")).then_inc(routed, 1)
                    step(18)
                    dve.tensor_tensor(chosen[:], over(w["expert_ids"][:], 1, PAIRS),
                                      over(pick[:].rearrange("p j t -> p (j t)"), 2, E1), ALU.is_equal).then_inc(routed, 1)
                    step(19)
                    dve.tensor_tensor(mask[:], chosen[:, 0:GT, :], chosen[:, GT:PAIRS, :], ALU.add).then_inc(routed, 1)

                    def shared(f):
                        dve.wait_ge(silu_ready, FS * g + f + 1)
                        dve.tensor_tensor(mid[:, f, :], bank(5 + 2 * (f % 2)), silu[:, f % 2, :], ALU.mult)\
                            .then_inc(mid_ready, 1)

                    for f in range(3):
                        shared(f)
                    dve.wait_ge(rank_done, g + 1)
                    counted = bank(2)[:, 0:(GT + 1) * E1].rearrange("p (t e) -> p t e", e=E1)
                    dve.tensor_tensor(rank[:], counted[:, 0:GT, :], over(before[:], 1, GT), ALU.add).then_inc(routed, 1)
                    step(21)
                    dve.tensor_tensor(slot_of[:], rank[:], over(w["expert_base"][:], 1, GT), ALU.add).then_inc(routed, 1)
                    dve.tensor_tensor(before[:], counted[:, GT, :], before[:], ALU.add).then_inc(routed, 1)
                    step(22)
                    for values, out in ((slot_of, pair_slot), (rank, pair_rank)):
                        for j in range(2):
                            ins = dve.tensor_tensor(out[:, GT * j:GT * j + GT, :], chosen[:, GT * j:GT * j + GT, :],
                                                    values[:], ALU.mult)
                        ins.then_inc(routed, 1)
                    step(25)
                    dve.tensor_reduce(slot8[:], pair_slot[:], AX.X, ALU.add).then_inc(routed, 1)
                    dve.tensor_reduce(rank8[:], pair_rank[:], AX.X, ALU.add).then_inc(routed, 1)
                    step(27)
                    dve.tensor_scalar(rank8[:], rank8[:], float(CAP), float(4 * SLOTS), ALU.is_ge, ALU.mult)\
                        .then_inc(routed, 1)
                    step(28)
                    dve.tensor_tensor(slot8[:], slot8[:], rank8[:], ALU.add).then_inc(routed, 1)
                    step(29)
                    dve.tensor_copy(slot_index[:], slot8[:]).then_inc(routed, 1)
                    dve.tensor_scalar(m.pair_slots[:, :, bass.ds(GT * g, GT)],
                                      slot8[:].rearrange("p (j t) -> p j t", j=2), float(SLOTS), None, ALU.min)\
                        .then_inc(routed, 1)
                    for f in range(3, FS):
                        shared(f)
                    dve.wait_ge(shared_done, g + 1)
                    rows = m.X[:, bass.ds(GT * g, GT), :]
                    dve.tensor_tensor(rows, tiles_of(bank(3)), rows, ALU.add).then_inc(shared_added, 1)
                    dve.wait_ge(scattered, 16 * PAIRS * (g + 1))
                    dve.memset(m.spare[:], 0.0)
                dve.wait_ge(shared_added, GROUPS)
                dve.wait_ge(routed, ROUTE * GROUPS)


def run_experts(nc, m):
    HALF = CAP // 2
    UNITS = 2 * FR
    w = m.w
    with ExitStack() as ctx:
        def sb(name, shape):
            return ctx.enter_context(nc.sbuf_tensor("ex_" + name, shape, F32))

        def sem(name):
            return stage_semaphore(nc, m, "ex_" + name)

        weights = sb("weights", [P, 2, 3 * FR * P])
        gate_w, up_w, down_w = (weights[:, :, FR * P * n:FR * P * (n + 1)].rearrange("p k (f c) -> p k f c", c=P)
                                for n in range(3))
        rows = sb("rows", [P, 2, CT, D])
        xT = sb("xT", [P, CAP])
        silu = sb("silu", [P, 2, HALF])
        mid = sb("mid", [P, FR, CAP])
        result = sb("result", [P, 2, CT, D])
        bank = m.bank

        loaded = [sem("loaded_even"), sem("loaded_odd")]
        turned = sem("turned")
        xT_ready = sem("xT_ready")
        gate_up_done = sem("gate_up_done")
        silu_ready = sem("silu_ready")
        mid_ready = sem("mid_ready")
        down_done = sem("down_done")
        result_ready = sem("result_ready")
        stored = [sem("stored_even"), sem("stored_odd")]

        with nc.Block() as block:

            @block.sync
            def _(sp):
                def load(e, k):
                    sp.dma_start(rows[:, k], slot_tiles(m.slot_rows, e)).then_inc(loaded[k], 16)
                    sp.dma_start(weights[:, k, :], m.dram["experts"][bass.ds(e, 1)].rearrange("e p n -> p (e n)"))\
                        .then_inc(loaded[k], 16)

                def store(e, k, count):
                    sp.wait_ge(result_ready, count)
                    sp.dma_start(slot_tiles(m.result_rows[0:SLOTS], e), result[:, k]).then_inc(stored[k], 16)

                load(0, 0)
                load(1, 1)
                with sp.Fori(0, E1 // 2 - 1) as i:
                    for k in range(2):
                        store(2 * i + k, k, 2 * i + k + 1)
                        sp.wait_ge(stored[k], 16 * (i + 1))
                        load(2 * i + k + 2, k)
                for k in range(2):
                    store(E1 - 2 + k, k, E1 - 1 + k)
                for k in range(2):
                    sp.wait_ge(stored[k], 16 * (E1 // 2))

            @block.tensor
            def _(pe):
                with pe.Fori(0, E1 // 2) as i:
                    for k in range(2):
                        def e(count, n):
                            return count * (2 * i + k) + n

                        pe.wait_ge(loaded[k], 32 * (i + 1))
                        for c in range(CT):
                            mm = pe.transpose(bank(c // GT)[:, P * (c % GT):P * (c % GT) + P], rows[:, k, c, :], w["ident"][:])
                        mm.then_inc(turned, 1)
                        pe.wait_ge(xT_ready, e(1, 1))
                        for n in range(UNITS):
                            f, half = n // 2, n % 2
                            if n >= 2:
                                pe.wait_ge(mid_ready, e(UNITS, n - 1))
                            for buf, b in ((gate_w, 4), (up_w, 5)):
                                mm = pe.matmul(bank(b + 2 * half)[:, 0:HALF], buf[:, k, f, :],
                                               xT[:, HALF * half:HALF * half + HALF], start=True, stop=True)
                            mm.then_inc(gate_up_done, 1)
                        pe.wait_ge(mid_ready, e(UNITS, UNITS))
                        for c in range(CT):
                            for f in range(FR):
                                mm = pe.matmul(bank(2 + c // GT)[:, P * (c % GT):P * (c % GT) + P],
                                               mid[:, f, P * c:P * c + P], down_w[:, k, f, :],
                                               start=(f == 0), stop=(f == FR - 1))
                        mm.then_inc(down_done, 1)

            @block.scalar
            def _(act):
                with act.Fori(0, E1 // 2) as i:
                    for k in range(2):
                        def e(count, n):
                            return count * (2 * i + k) + n

                        act.wait_ge(turned, e(1, 1))
                        act.activation(xT[:], m.ps[:, 0:2, :].rearrange("p a n -> p (a n)")[:, 0:CAP], ACT.Copy)\
                            .then_inc(xT_ready, 1)
                        for n in range(UNITS):
                            act.wait_ge(gate_up_done, e(UNITS, n + 1))
                            act.activation(silu[:, n % 2, :], bank(4 + 2 * (n % 2))[:, 0:HALF], ACT.Silu)\
                                .then_inc(silu_ready, 1)
                        act.wait_ge(down_done, e(1, 1))
                        act.activation(result[:, k].rearrange("p c d -> p (c d)"),
                                       m.ps[:, 2:4, :].rearrange("p a n -> p (a n)")[:, 0:CAP], ACT.Copy)\
                            .then_inc(result_ready, 1)

            @block.vector
            def _(dve):
                with dve.Fori(0, E1 // 2) as i:
                    for k in range(2):
                        def e(count, n):
                            return count * (2 * i + k) + n

                        for n in range(UNITS):
                            f, half = n // 2, n % 2
                            dve.wait_ge(silu_ready, e(UNITS, n + 1))
                            dve.tensor_tensor(mid[:, f, HALF * half:HALF * half + HALF], bank(5 + 2 * half)[:, 0:HALF],
                                              silu[:, half, :], ALU.mult).then_inc(mid_ready, 1)


def slot_tiles(rows, e):
    return rows.rearrange("(e c p) d -> e p c d", c=CT, p=P)[bass.ds(e, 1)].rearrange("e p c d -> p (e c) d")


def combine_experts(nc, m):
    PAIRS = 2 * GT
    with ExitStack() as ctx:
        def sem(name):
            return stage_semaphore(nc, m, "cb_" + name)

        got = ctx.enter_context(nc.sbuf_tensor("cb_got", [P, 2, PAIRS, D], F32))
        slot = ctx.enter_context(nc.sbuf_tensor("cb_slot", [P, 2, PAIRS], U32))
        weight = ctx.enter_context(nc.sbuf_tensor("cb_weight", [P, 2, PAIRS], F32))
        slot_ready = sem("slot_ready")
        gathered = [sem("gathered_even"), sem("gathered_odd")]
        added = sem("added")
        picked = sem("picked")
        carried = sem("carried")

        with nc.Block() as block:

            @block.gpsimd
            def _(pool):
                pool.memset(m.pool_spare[:], 0.0).then_inc(carried, 1)
                with pool.Fori(0, GROUPS // 2) as i:
                    for k in range(2):
                        pool.wait_ge(slot_ready, 2 * i + k + 1)
                        pool.wait_ge(carried, 2 * i + k + 1)
                        pool.tensor_tensor(m.pool_spare[:, 0, :], m.minus_half[:], m.minus_half[:], ALU.add)\
                            .then_inc(carried, 1)
                        for n in range(PAIRS):
                            pool.indirect_dma_start(
                                out=got[:, k, n, :], out_offset=None, in_=m.result_rows,
                                in_offset=bass.IndirectOffsetOnAxis(ap=slot[:, k, n:n + 1], axis=0))\
                                .then_inc(gathered[k], 16)

            @block.vector
            def _(dve):
                def picks(g, k):
                    where = bass.ds(GT * g, GT)
                    dve.tensor_copy(weight[:, k].rearrange("p (j t) -> p j t", j=2), m.pair_weights[:, :, where])\
                        .then_inc(picked, 1)
                    dve.tensor_copy(slot[:, k].rearrange("p (j t) -> p j t", j=2), m.pair_slots[:, :, where])\
                        .then_inc(slot_ready, 1)

                dve.memset(m.spare[:], 0.0).then_inc(added, 1)
                picks(0, 0)
                with dve.Fori(0, GROUPS // 2) as i:
                    for k in range(2):
                        g = 2 * i + k
                        dve.wait_ge(added, PAIRS * g + 1)
                        picks(g + 1, 1 - k)
                        dve.wait_ge(picked, g + 1)
                        dve.wait_ge(gathered[k], 16 * PAIRS * (i + 1))
                        for n in range(PAIRS):
                            if n >= GT:
                                dve.wait_ge(added, PAIRS * g + n - GT + 2)
                            row = m.X[:, bass.ds(GT * g + n % GT, 1), :]
                            dve.scalar_tensor_tensor(out=row, in0=got[:, k, n:n + 1, :], scalar=weight[:, k, n:n + 1],
                                                     in1=row, op0=ALU.mult, op1=ALU.add).then_inc(added, 1)
                dve.wait_ge(added, GROUPS * PAIRS + 1)
                dve.wait_ge(picked, GROUPS + 1)


def causal_attention(nc, m):
    w = m.w
    with ExitStack() as ctx:
        def sb(name, shape):
            return ctx.enter_context(nc.sbuf_tensor("ca_" + name, shape, F32))

        def sem(name):
            return stage_semaphore(nc, m, "ca_" + name)

        xn = sb("xn", [P, GT, D])
        hT = sb("hT", [P, N])
        qkT = sb("qkT", [P, 2, N])
        vheads = sb("vheads", [P, GB, HP * (P + 2 * DH0)])
        kheads = sb("kheads", [P, 2, 2, H * SEQ])
        probs = sb("probs", [P, 2, H, SEQ])
        probsT = sb("probsT", [P, 2, HP, P])
        top = sb("top", [P, 2, H])
        total = sb("total", [P, 2, H])
        attnT = sb("attnT", [P, N])
        bank = m.bank

        ln = NormSemaphores(sem, "ln")
        zeroed = sem("zeroed")
        hT_turned = sem("hT_turned")
        hT_ready = sem("hT_ready")
        qk_done = sem("qk_done")
        qk_ready = sem("qk_ready")
        v_done = sem("v_done")
        v_ready = sem("v_ready")
        kheads_ready = sem("kheads_ready")
        scores_done = sem("scores_done")
        masked = sem("masked")
        top_ready = sem("top_ready")
        less_top = sem("less_top")
        exp_ready = sem("exp_ready")
        sum_ready = sem("sum_ready")
        inverse_ready = sem("inverse_ready")
        probs_ready = sem("probs_ready")
        probs_turned = sem("probs_turned")
        probsT_ready = sem("probsT_ready")
        attn_done = sem("attn_done")
        attn_ready = sem("attn_ready")
        out_done = sem("out_done")
        x_added = sem("x_added")

        def vdiag(par):
            v = vheads[SEQ * par:SEQ * par + SEQ].rearrange("p b (h c) -> p b h c", c=P + 2 * DH0)
            return v[:, :, :, DH0 * par:DH0 * par + DH0]

        with nc.Block() as block:

            @block.tensor
            def _(pe):
                pe.wait_ge(m.loaded_causal, 16)
                with pe.Fori(0, GROUPS) as g:
                    for t in range(GT):
                        pe.wait_ge(ln.normed, GT * g + t + 1)
                        mm = pe.transpose(bank(4)[:, P * t:P * t + P], xn[:, t, :], w["ident"][:])
                    mm.then_inc(hT_turned, 1)
                    pe.wait_ge(hT_ready, g + 1)
                    for n in range(2):
                        mm = pe.matmul(bank(n), w["cqk"][:, n, :], hT[:], start=True, stop=True)
                    mm.then_inc(qk_done, 1)
                    for b in range(GB):
                        for par in range(2):
                            out = bank(7)[SEQ * par:SEQ * par + SEQ, HP * DH0 * b:HP * DH0 * (b + 1)]
                            pe.matmul(out, w["ones"][0:1, 0:SEQ], w["bv"][0:1, par, :], start=True, stop=False)
                            mm = pe.matmul(out, hT[:, SEQ * b:SEQ * b + SEQ], w["cv"][:, par, :], start=False, stop=True)
                    mm.then_inc(v_done, 1)

                    def score(t):
                        pe.wait_ge(kheads_ready, GB * g + 2 * t + 2)
                        if t == 0:
                            pe.wait_ge(qk_ready, 2 * g + 2)
                        if t >= 2:
                            pe.wait_ge(masked, GT * g + t - 1)
                        for b in range(2):
                            seq = 2 * t + b
                            for half in range(2):
                                mm = pe.matmul(bank(2 * (t % 2) + half)[SEQ * b:SEQ * b + SEQ, :],
                                               qkT[:, 0, SEQ * seq:SEQ * seq + SEQ],
                                               kheads[:, t % 2, b, N * half:N * half + N], start=True, stop=True)
                        mm.then_inc(scores_done, 1)

                    def turn(t):
                        pe.wait_ge(probs_ready, GT * g + t + 1)
                        if t >= 1:
                            pe.wait_ge(probsT_ready, GT * g + t)
                        for hp in range(HP):
                            mm = pe.transpose(bank(4 + hp // 4)[:, P * (hp % 4):P * (hp % 4 + 1)],
                                              probs[:, t % 2, 2 * hp:2 * hp + 2, :].rearrange("p a k -> p (a k)"),
                                              w["ident"][:])
                        mm.then_inc(probs_turned, 1)

                    def attend(t):
                        pe.wait_ge(probsT_ready, GT * g + t + 1)
                        if t == 0:
                            pe.wait_ge(v_ready, 2 * g + 2)
                        for b in range(2):
                            for hp in range(HP):
                                mm = pe.matmul(bank(6)[:, P * t + SEQ * b:P * t + SEQ * (b + 1)],
                                               vheads[:, 2 * t + b, P * hp:P * hp + P],
                                               probsT[:, t % 2, hp, SEQ * b:SEQ * b + SEQ],
                                               start=(hp == 0), stop=(hp == HP - 1))
                        mm.then_inc(attn_done, 1)

                    for s in range(GT + 2):
                        if s < GT:
                            score(s)
                        if 1 <= s <= GT:
                            turn(s - 1)
                        if s >= 2:
                            attend(s - 2)
                    pe.wait_ge(attn_ready, g + 1)
                    for t in range(GT):
                        out = bank(7)[:, P * t:P * t + P]
                        pe.matmul(out, w["ones"][0:1, :], w["bo"][0:1, :], start=True, stop=False)
                        mm = pe.matmul(out, attnT[:, P * t:P * t + P], w["co"][:], start=False, stop=True)
                    mm.then_inc(out_done, 1)

            @block.scalar
            def _(act):
                act.wait_ge(m.loaded_causal, 16)
                act.wait_ge(zeroed, 1)
                with act.Fori(0, GROUPS) as g:
                    act.wait_ge(hT_turned, g + 1)
                    act.activation(hT[:], bank(4), ACT.Copy).then_inc(hT_ready, 1)
                    act.wait_ge(qk_done, g + 1)
                    for n in range(2):
                        act.activation(qkT[:, n, :], bank(n), ACT.Identity, bias=w["c_bias"][:, n:n + 1]).then_inc(qk_ready, 1)
                    act.wait_ge(v_done, g + 1)
                    for par in range(2):
                        src = bank(7)[SEQ * par:SEQ * par + SEQ, :].rearrange("p (b h c) -> p b h c", h=HP, c=DH0)
                        act.activation(vdiag(par), src, ACT.Copy).then_inc(v_ready, 1)
                    for s in range(GT + 1):
                        if s < GT:
                            act.wait_ge(less_top, GT * g + s + 1)
                            act.activation(probs[:, s % 2], probs[:, s % 2], ACT.Exp).then_inc(exp_ready, 1)
                        if s >= 1:
                            act.wait_ge(probs_turned, GT * g + s)
                            if s >= 3:
                                act.wait_ge(attn_done, GT * g + s - 2)
                            act.activation(probsT[:, (s - 1) % 2].rearrange("p a n -> p (a n)"),
                                           m.ps[:, 4:6, :].rearrange("p a n -> p (a n)"), ACT.Copy)\
                                .then_inc(probsT_ready, 1)
                    act.wait_ge(attn_done, GT * g + GT)
                    act.activation(attnT[:], bank(6), ACT.Copy).then_inc(attn_ready, 1)

            @block.gpsimd
            def _(pool):
                pool.memset(vheads[:], 0.0).then_inc(zeroed, 1)
                with pool.Fori(0, GROUPS) as g:
                    inverse_root(pool, m, g, ln, 1, 0)
                    for s in range(GT + 1):
                        if s < GT:
                            pool.wait_ge(qk_ready, 2 * g + 2)
                            if s >= 2:
                                pool.wait_ge(scores_done, GT * g + s - 1)
                            for b in range(2):
                                k = qkT[:, 1, SEQ * (2 * s + b):SEQ * (2 * s + b + 1)]
                                pool.tensor_tensor(seqs_of(kheads[:, s % 2, b, :]), over(k, 1, H),
                                                   over(w["head_rows_flat"][:], 2, SEQ), ALU.mult).then_inc(kheads_ready, 1)
                        if s >= 1:
                            n = s - 1
                            pool.wait_ge(inverse_ready, GT * g + n + 1)
                            pool.tensor_tensor(probs[:, n % 2], probs[:, n % 2], over(total[:, n % 2], 2, SEQ),
                                               ALU.mult).then_inc(probs_ready, 1)

            @block.vector
            def _(dve):
                with dve.Fori(0, GROUPS) as g:
                    normalize(dve, m, g, lambda t: m.X[:, bass.ds(GT * g + t, 1), :], lambda t: xn[:, t, :], ln, 1, 0)
                    for s in range(GT + 1):
                        if s < GT:
                            scores = m.ps[:, 2 * (s % 2):2 * (s % 2) + 2, :].rearrange("p a (h k) -> p (a h) k", k=SEQ)
                            dve.wait_ge(scores_done, GT * g + s + 1)
                            if s >= 2:
                                dve.wait_ge(probs_turned, GT * g + s - 1)
                            dve.scalar_tensor_tensor(out=probs[:, s % 2], in0=scores, scalar=float(DH0) ** -0.5,
                                                     in1=over(w["causal_bias"][:], 1, H), op0=ALU.mult, op1=ALU.add)\
                                .then_inc(masked, 1)
                            dve.wait_ge(masked, GT * g + s + 1)
                            dve.tensor_reduce(top[:, s % 2], probs[:, s % 2], AX.X, ALU.max).then_inc(top_ready, 1)
                            dve.wait_ge(top_ready, GT * g + s + 1)
                            dve.tensor_tensor(probs[:, s % 2], probs[:, s % 2], over(top[:, s % 2], 2, SEQ),
                                              ALU.subtract).then_inc(less_top, 1)
                        if s >= 1:
                            n = s - 1
                            dve.wait_ge(exp_ready, GT * g + n + 1)
                            dve.tensor_reduce(total[:, n % 2], probs[:, n % 2], AX.X, ALU.add).then_inc(sum_ready, 1)
                            dve.wait_ge(sum_ready, GT * g + n + 1)
                            dve.reciprocal(total[:, n % 2], total[:, n % 2]).then_inc(inverse_ready, 1)
                    dve.wait_ge(out_done, g + 1)
                    rows = m.X[:, bass.ds(GT * g, GT), :]
                    dve.tensor_tensor(rows, tiles_of(bank(7)), rows, ALU.add).then_inc(x_added, 1)
                    dve.wait_ge(x_added, g + 1)


def biased_attention(nc, m):
    w = m.w
    PROJ = 24
    BUCKETS = 32
    with ExitStack() as ctx:
        def sb(name, shape, dtype=F32):
            return ctx.enter_context(nc.sbuf_tensor("ba_" + name, shape, dtype))

        def sem(name):
            return stage_semaphore(nc, m, "ba_" + name)

        mask_bits = sb("mask_bits", [P, SEQ], U8)
        mask = sb("mask", [P, SEQ])
        hidden = sb("hidden", [P, SEQ])
        scaled_mask = sb("scaled_mask", [P, SEQ])
        bias = sb("bias", [P, H, SEQ])
        xn = sb("xn", [P, GT, D])
        rows = sb("rows", [P, GT, D])
        hT = sb("hT", [P, N])
        cT = sb("cT", [P, N])
        qT = sb("qT", [P, HP, N])
        kT = sb("kT", [P, HP, N])
        v = sb("v", [P, GB, N])
        probs = sb("probs", [P, 2, HP, 2, SEQ])
        probsT = sb("probsT", [P, 2, HP, P])
        top = sb("top", [P, 2, H])
        total = sb("total", [P, 2, H])
        attnT = sb("attnT", [P, GT, HP, P])
        bank = m.bank

        ln = NormSemaphores(sem, "ln")
        loaded_mask = sem("loaded_mask")
        bias_done = sem("bias_done")
        bias_step = sem("bias_step")
        bias_ready = sem("bias_ready")
        rows_ready = sem("rows_ready")
        turned = sem("turned")
        turned_ready = sem("turned_ready")
        proj_done = sem("proj_done")
        proj_even = sem("proj_even")
        proj_odd = sem("proj_odd")
        scores_done = sem("scores_done")
        masked = sem("masked")
        biased = sem("biased")
        top_ready = sem("top_ready")
        less_top = sem("less_top")
        exp_ready = sem("exp_ready")
        sum_ready = sem("sum_ready")
        inverse_ready = sem("inverse_ready")
        probs_ready = sem("probs_ready")
        probs_turned = sem("probs_turned")
        probsT_ready = sem("probsT_ready")
        attn_done = sem("attn_done")
        attn_ready = sem("attn_ready")
        out_done = sem("out_done")
        x_added = sem("x_added")

        def proj_bank(n):
            return bank(n % 4 + (4 if n >= 16 else 0))

        def projected(n):
            return (qT, kT, v)[n // 8][:, n % 8, :]

        def heads_flat(t):
            return probs[:, t % 2].rearrange("p h a k -> p (h a) k")

        with nc.Block() as block:

            @block.sync
            def _(sp):
                for b in range(2):
                    sp.dma_start(mask_bits[SEQ * b:SEQ * b + SEQ, :], m.dram["mask"]).then_inc(loaded_mask, 16)

            @block.tensor
            def _(pe):
                pe.wait_ge(m.loaded_biased, 32)
                for b in range(2):
                    for k in range(SEQ):
                        mm = pe.matmul(bank(k // 32)[SEQ * b:SEQ * b + SEQ, H * (k % 32):H * (k % 32 + 1)],
                                       w["distance"][0:BUCKETS, SEQ - 1 - k:2 * SEQ - 1 - k], w["rel_bias"][:],
                                       start=True, stop=True)
                mm.then_inc(bias_done, 1)
                pe.wait_ge(bias_ready, 1)
                with pe.Fori(0, GROUPS) as g:
                    for t in range(GT):
                        pe.wait_ge(ln.normed, GT * g + t + 1)
                        mm = pe.transpose(bank(6)[:, P * t:P * t + P], xn[:, t, :], w["ident"][:])
                    mm.then_inc(turned, 1)
                    pe.wait_ge(rows_ready, g + 1)
                    for t in range(GT):
                        mm = pe.transpose(bank(7)[:, P * t:P * t + P], rows[:, t, :], w["ident"][:])
                    mm.then_inc(turned, 1)
                    pe.wait_ge(turned_ready, 2 * g + 2)
                    for n in range(PROJ):
                        if n >= 4:
                            pe.wait_ge((proj_even, proj_odd)[n % 2], PROJ // 2 * g + (n - 4) // 2 + 1)
                        if n < 16:
                            mm = pe.matmul(proj_bank(n), (w["bq"], w["bk"])[n // 8][:, P * (n % 8):P * (n % 8 + 1)],
                                           (hT, cT)[n // 8][:], start=True, stop=True)
                        else:
                            for par in range(2):
                                mm = pe.matmul(proj_bank(n)[SEQ * par:SEQ * par + SEQ, :],
                                               cT[:, SEQ * (n - 16):SEQ * (n - 15)], w["bvp"][:, par, :], start=True, stop=True)
                        mm.then_inc(proj_done, 1)

                    def score(t):
                        for par in range(2):
                            part = slice(DHX * par, DHX * par + DHX)
                            for hp in range(HP):
                                for b in range(2):
                                    at = slice(SEQ * (2 * t + b), SEQ * (2 * t + b + 1))
                                    mm = pe.matmul(bank(2 * (t % 2) + par)[SEQ * b:SEQ * b + SEQ, SEQ * hp:SEQ * hp + SEQ],
                                                   qT[part, hp, at], kT[part, hp, at], start=True, stop=True)
                        mm.then_inc(scores_done, 1)

                    def turn(t):
                        if t == 0:
                            pe.wait_ge(proj_even, PROJ // 2 * g + PROJ // 2)
                            pe.wait_ge(proj_odd, PROJ // 2 * g + PROJ // 2)
                        pe.wait_ge(probs_ready, GT * g + t + 1)
                        if t >= 1:
                            pe.wait_ge(probsT_ready, GT * g + t)
                        if t >= 2:
                            pe.wait_ge(attn_ready, GT * g + t - 1)
                        for hp in range(HP):
                            mm = pe.transpose(bank(4 + hp // 4)[:, P * (hp % 4):P * (hp % 4 + 1)],
                                              probs[:, t % 2, hp].rearrange("p a k -> p (a k)"), w["ident"][:])
                        mm.then_inc(probs_turned, 1)

                    def attend(t):
                        for hp in range(HP):
                            for par in range(2):
                                part = slice(DHX * par, DHX * par + DHX)
                                for b in range(2):
                                    at = P * (hp % 4) + SEQ * b
                                    mm = pe.matmul(bank(6 + hp // 4)[part, at:at + SEQ],
                                                   v[part, 2 * t + b, DHX * hp:DHX * (hp + 1)],
                                                   probsT[part, t % 2, hp, SEQ * b:SEQ * b + SEQ], start=True, stop=True)
                        mm.then_inc(attn_done, 1)

                    def project(t):
                        if t >= GT - 1:
                            pe.wait_ge(attn_ready, GT * g + t + 1)
                        for hp in range(HP):
                            mm = pe.matmul(bank(0)[:, P * t:P * t + P], attnT[:, t, hp, :], w["bo1"][:, hp, :],
                                           start=(hp == 0), stop=(hp == HP - 1))
                        mm.then_inc(out_done, 1)

                    for s in range(GT + 1):
                        if s < GT:
                            score(s)
                        if 1 <= s:
                            turn(s - 1)
                        if s >= 2:
                            attend(s - 2)
                    pe.wait_ge(attn_ready, GT * g + GT - 2)
                    project(0)
                    pe.wait_ge(probsT_ready, GT * g + GT)
                    pe.wait_ge(attn_ready, GT * g + GT - 1)
                    project(1)
                    attend(GT - 1)
                    project(2)
                    project(3)

            @block.scalar
            def _(act):
                with act.Fori(0, GROUPS) as g:
                    for n, (out, b) in enumerate(((hT, 6), (cT, 7))):
                        act.wait_ge(turned, 2 * g + n + 1)
                        act.activation(out[:], bank(b), ACT.Copy).then_inc(turned_ready, 1)
                    for n in range(0, PROJ, 2):
                        act.wait_ge(proj_done, PROJ * g + n + 1)
                        act.activation(projected(n), proj_bank(n), ACT.Copy).then_inc(proj_even, 1)
                    for s in range(GT + 2):
                        if s < GT:
                            act.wait_ge(less_top, GT * g + s + 1)
                            act.activation(probs[:, s % 2], probs[:, s % 2], ACT.Exp).then_inc(exp_ready, 1)
                        if 1 <= s <= GT:
                            act.wait_ge(probs_turned, GT * g + s)
                            if s >= 3:
                                act.wait_ge(attn_done, GT * g + s - 2)
                            act.activation(probsT[:, (s - 1) % 2].rearrange("p a n -> p (a n)"),
                                           m.ps[:, 4:6, :].rearrange("p a n -> p (a n)"), ACT.Copy)\
                                .then_inc(probsT_ready, 1)
                        if s >= 2:
                            act.wait_ge(attn_done, GT * g + s - 1)
                            act.activation(attnT[:, s - 2].rearrange("p a n -> p (a n)"),
                                           m.ps[:, 6:8, :].rearrange("p a n -> p (a n)"), ACT.Copy)\
                                .then_inc(attn_ready, 1)

            @block.gpsimd
            def _(pool):
                pool.wait_ge(m.loaded_ctx, 16)
                with pool.Fori(0, GROUPS) as g:
                    inverse_root(pool, m, g, ln, 1, 0)
                    pool.tensor_copy(rows[:], m.C[:, bass.ds(GT * g, GT), :]).then_inc(rows_ready, 1)
                    for s in range(GT + 1):
                        if s < GT:
                            pool.wait_ge(masked, GT * g + s + 1)
                            pool.tensor_tensor(heads_flat(s), heads_flat(s), bias[:], ALU.add).then_inc(biased, 1)
                        if s >= 1:
                            n = s - 1
                            pool.wait_ge(inverse_ready, GT * g + n + 1)
                            pool.tensor_tensor(heads_flat(n), heads_flat(n), over(total[:, n % 2], 2, SEQ),
                                               ALU.mult).then_inc(probs_ready, 1)

            @block.vector
            def _(dve):
                dve.wait_ge(loaded_mask, 32)
                dve.tensor_copy(mask[:], mask_bits[:]).then_inc(bias_step, 1)
                dve.wait_ge(bias_step, 1)
                dve.tensor_scalar(hidden[:], mask[:], 1.0, -LOWEST, ALU.subtract, ALU.mult).then_inc(bias_step, 1)
                dve.tensor_scalar(scaled_mask[:], mask[:], DHX ** -0.5, None, ALU.mult).then_inc(bias_step, 1)
                dve.wait_ge(bias_done, 1)
                by_head = m.ps[:, 0:2, :].rearrange("p a (k h) -> p h (a k)", h=H)
                dve.tensor_tensor(bias[:], by_head, over(mask[:], 1, H), ALU.mult).then_inc(bias_step, 1)
                dve.wait_ge(bias_step, 4)
                dve.tensor_tensor(bias[:], bias[:], over(hidden[:], 1, H), ALU.add).then_inc(bias_ready, 1)
                with dve.Fori(0, GROUPS) as g:
                    normalize(dve, m, g, lambda t: m.X[:, bass.ds(GT * g + t, 1), :], lambda t: xn[:, t, :], ln, 1, 0)
                    for n in range(1, PROJ, 2):
                        dve.wait_ge(proj_done, PROJ * g + n + 1)
                        dve.tensor_copy(projected(n), proj_bank(n)).then_inc(proj_odd, 1)
                    for s in range(GT + 1):
                        if s < GT:
                            scores = m.ps[:, 2 * (s % 2):2 * (s % 2) + 2, :].rearrange("p a (h k) -> p a h k", k=SEQ)
                            dve.wait_ge(scores_done, GT * g + s + 1)
                            if s >= 2:
                                dve.wait_ge(probs_turned, GT * g + s - 1)
                            dve.tensor_tensor(probs[:, s % 2].rearrange("p h a k -> p a h k"), scores,
                                              over(over(scaled_mask[:], 1, HP), 1, 2), ALU.mult).then_inc(masked, 1)
                            dve.wait_ge(biased, GT * g + s + 1)
                            dve.tensor_reduce(top[:, s % 2], heads_flat(s), AX.X, ALU.max).then_inc(top_ready, 1)
                            dve.wait_ge(top_ready, GT * g + s + 1)
                            dve.tensor_tensor(heads_flat(s), heads_flat(s), over(top[:, s % 2], 2, SEQ),
                                              ALU.subtract).then_inc(less_top, 1)
                        if s >= 1:
                            n = s - 1
                            dve.wait_ge(exp_ready, GT * g + n + 1)
                            dve.tensor_reduce(total[:, n % 2], heads_flat(n), AX.X, ALU.add).then_inc(sum_ready, 1)
                            dve.wait_ge(sum_ready, GT * g + n + 1)
                            dve.reciprocal(total[:, n % 2], total[:, n % 2]).then_inc(inverse_ready, 1)
                    dve.wait_ge(out_done, GT * g + GT)
                    out = m.X[:, bass.ds(GT * g, GT), :]
                    dve.tensor_tensor(out, tiles_of(bank(0)), out, ALU.add).then_inc(x_added, 1)
                    dve.wait_ge(x_added, g + 1)


def top_expert(nc, m):
    w = m.w
    ROUTE = 17
    with ExitStack() as ctx:
        def sb(name, shape, dtype=F32):
            return ctx.enter_context(nc.sbuf_tensor("te_" + name, shape, dtype))

        def sem(name):
            return stage_semaphore(nc, m, "te_" + name)

        xn = sb("xn", [P, GT, D])
        xT = sb("xT", [P, N])
        prob = sb("prob", [P, GT, E1])
        top = sb("top", [P, GT])
        ranked = sb("ranked", [P, GT, E1])
        index = sb("index", [P, GT, E1], U32)
        pick = sb("pick", [P, GT])
        chosen = sb("chosen", [P, GT, E1])
        chosenT = sb("chosenT", [E1, N])
        bank = m.bank

        ln = NormSemaphores(sem, "ln")
        xT_turned = sem("xT_turned")
        xT_ready = sem("xT_ready")
        logits_done = sem("logits_done")
        exp_ready = sem("exp_ready")
        routed = sem("routed")
        chosen_turned = sem("chosen_turned")
        chosenT_ready = sem("chosenT_ready")
        bias_done = sem("bias_done")
        experts_done = sem("experts_done")
        added = sem("added")

        PER = E1 * GT + 1

        with nc.Block() as block:

            @block.tensor
            def _(pe):
                pe.wait_ge(m.loaded_top, 32)
                with pe.Fori(0, GROUPS) as g:
                    for t in range(GT):
                        pe.wait_ge(ln.normed, GT * g + t + 1)
                        mm = pe.transpose(bank(0)[:, P * t:P * t + P], xn[:, t, :], w["ident"][:])
                    mm.then_inc(xT_turned, 1)
                    pe.wait_ge(xT_ready, g + 1)
                    for t in range(GT):
                        out = bank(1)[:, E1 * t:E1 * t + E1]
                        pe.matmul(out, w["ones"][0:1, :], w["router_b"][0:1, :], start=True, stop=False)
                        mm = pe.matmul(out, xT[:, P * t:P * t + P], w["router1"][:], start=False, stop=True)
                    mm.then_inc(logits_done, 1)
                    for t in range(GT):
                        if t >= 2:
                            pe.wait_ge(added, PER * g + E1 * (t - 1))
                        for half in range(2):
                            mm = pe.matmul(bank(2 + 2 * (t % 2) + half), xT[:, P * t:P * t + P],
                                           w["expert"][:, N * half:N * half + N], start=True, stop=True)
                        mm.then_inc(experts_done, 1)
                        if t == 1:
                            pe.wait_ge(routed, ROUTE * g + ROUTE)
                            for s in range(GT):
                                mm = pe.transpose(bank(6)[0:E1, P * s:P * s + P], chosen[:, s, :], w["ident"][:])
                            mm.then_inc(chosen_turned, 1)
                            pe.wait_ge(chosenT_ready, g + 1)
                            for s in range(GT):
                                mm = pe.matmul(bank(7)[:, P * s:P * s + P], chosenT[:, P * s:P * s + P], w["expert_b"][:],
                                               start=True, stop=True)
                            mm.then_inc(bias_done, 1)

            @block.scalar
            def _(act):
                with act.Fori(0, GROUPS) as g:
                    act.wait_ge(xT_turned, g + 1)
                    act.activation(xT[:], bank(0), ACT.Copy).then_inc(xT_ready, 1)
                    act.wait_ge(routed, ROUTE * g + 2)
                    act.activation(prob[:], prob[:], ACT.Exp).then_inc(exp_ready, 1)
                    act.wait_ge(chosen_turned, g + 1)
                    act.activation(chosenT[:], bank(6)[0:E1, :], ACT.Copy).then_inc(chosenT_ready, 1)

            @block.gpsimd
            def _(pool):
                with pool.Fori(0, GROUPS) as g:
                    inverse_root(pool, m, g, ln, 1, 0)

            @block.vector
            def _(dve):
                with dve.Fori(0, GROUPS) as g:
                    def step(n):
                        dve.wait_ge(routed, ROUTE * g + n)

                    normalize(dve, m, g, lambda t: m.X[:, bass.ds(GT * g + t, 1), :], lambda t: xn[:, t, :], ln, 1, 0)
                    dve.wait_ge(logits_done, g + 1)
                    lg = bank(1)[:, 0:GT * E1].rearrange("p (t e) -> p t e", e=E1)
                    dve.tensor_reduce(top[:], lg, AX.X, ALU.max).then_inc(routed, 1)
                    step(1)
                    dve.tensor_tensor(prob[:], lg, over(top[:], 2, E1), ALU.subtract).then_inc(routed, 1)
                    dve.wait_ge(exp_ready, g + 1)
                    dve.tensor_reduce(top[:], prob[:], AX.X, ALU.add).then_inc(routed, 1)
                    step(3)
                    dve.reciprocal(top[:], top[:]).then_inc(routed, 1)
                    step(4)
                    dve.tensor_tensor(prob[:], prob[:], over(top[:], 2, E1), ALU.mult).then_inc(routed, 1)
                    step(5)
                    dve.memset(m.spare[:], 0.0)
                    for t in range(GT):
                        dve.max(ranked[:, t, :], prob[:, t, :]).then_inc(routed, 1)
                    step(9)
                    dve.memset(m.spare[:], 0.0)
                    for t in range(GT):
                        dve.max_index(index[:, t, :], ranked[:, t, :], prob[:, t, :]).then_inc(routed, 1)
                    dve.tensor_copy(top[:], ranked[:, :, 0]).then_inc(routed, 1)
                    step(13)
                    dve.tensor_copy(pick[:], index[:, :, 0]).then_inc(routed, 1)
                    step(15)
                    dve.tensor_tensor(chosen[:], over(w["expert_ids"][:], 1, GT), over(pick[:], 2, E1), ALU.is_equal)\
                        .then_inc(routed, 1)
                    step(16)
                    dve.tensor_tensor(chosen[:], chosen[:], over(top[:], 2, E1), ALU.mult).then_inc(routed, 1)
                    step(17)
                    for t in range(GT):
                        dve.wait_ge(experts_done, GT * g + t + 1)
                        row = m.X[:, bass.ds(GT * g + t, 1), :]
                        for e in range(E1):
                            if e >= 1:
                                dve.wait_ge(added, PER * g + E1 * t + e)
                            out = bank(2 + 2 * (t % 2) + e // GT)[:, P * (e % GT):P * (e % GT + 1)]
                            dve.scalar_tensor_tensor(out=row, in0=out.unsqueeze(1), scalar=chosen[:, t, e:e + 1], in1=row,
                                                     op0=ALU.mult, op1=ALU.add).then_inc(added, 1)
                    dve.wait_ge(bias_done, g + 1)
                    dve.wait_ge(added, PER * g + PER - 1)
                    rows = m.X[:, bass.ds(GT * g, GT), :]
                    dve.tensor_tensor(rows, tiles_of(bank(7)), rows, ALU.add).then_inc(added, 1)
                    dve.wait_ge(added, PER * g + PER)


PACKS = {
    "constants": [("ident", (P,)), ("ones", (P,)), ("same_head", (P,)), ("head_rows", (H,)), ("head_rows_flat", (H,)), ("causal_kq", (SEQ,)),
                  ("causal_bias", (SEQ,)), ("cos", (SEQ,)), ("sin", (SEQ,)), ("not_first", (N,)),
                  ("earlier", (P,)), ("expert_ids", (E1,)), ("expert_base", (E1,)), ("distance", (P,))],
    "linear": [("dw", (3,)), ("b_gate", (1,)), ("ln_g", (1,)), ("ln_b", (1,)), ("pw", (D,)), ("qk", (4, D)),
               ("v0", (2, HP * DH0)), ("gate", (D,)), ("o0", (D,)), ("moe_gate", (E0,)), ("b1", (E0 * F0,)),
               ("w1", (E0, F0, P)), ("w2", (E0, F0, D))],
    "latent": [("x_affine", (4,)), ("xq", (INNER,)), ("xk", (INNER,)), ("xv", (INNER,)), ("xo", (HP, D))],
    "shared": [("router", (E1,)), ("sg", (FS, P)), ("su", (FS, P)), ("sd", (FS, D))],
    "causal": [("c_bias", (2,)), ("cqk", (2, D)), ("cv", (2, HP * DH0)), ("co", (D,))],
    "biased": [("bq", (INNER,)), ("bk", (INNER,)), ("bvp", (2, HP * DHX)), ("bo1", (HP, D))],
    "top": [("router1", (E1,)), ("expert", (E1 * D,))],
    "rows": [("b2", (E0, D)), ("bv", (2, HP * DH0)), ("bo", (D,)), ("router_b", (E1,))],
}


def decoder(nc, dram, out):
    with ExitStack() as ctx:
        m, w = Shared(), {}
        m.w = w
        m.stage_semaphores = []

        def sb(name, shape, dtype=F32):
            return ctx.enter_context(nc.sbuf_tensor(name, shape, dtype))

        def sem(name):
            return ctx.enter_context(nc.semaphore(name))

        m.X = sb("X", [P, TILES, D])
        m.C = sb("C", [P, TILES, D])
        m.ps = ctx.enter_context(nc.psum_tensor("ps", [P, 8, 512], F32))
        m.bank = lambda n: m.ps[:, n, :]
        m.bn = sb("bn", [P, GT, 6])
        m.mean_var = sb("mean_var", [P, GT, 2])
        m.var_eps = sb("var_eps", [P, GT])
        m.rstd = sb("rstd", [P, GT])
        m.minus_half = sb("minus_half", [P, GT])
        w["rel_bias"] = sb("rel_bias", [32, H])
        w["expert_b"] = sb("expert_b", [E1, D])
        m.spare = sb("spare", [P, 1])
        m.pool_spare = sb("pool_spare", [P, 2, GT])
        m.dram = dram
        m.slot_rows = nc.dram_tensor("slot_rows", (SLOTS, D), F32, kind="Internal").ap()
        m.result_rows = nc.dram_tensor("result_rows", (SLOTS + 1, D), F32, kind="Internal").ap()
        zeros = sb("zeros", [P, D])
        packed = {}
        for pack, parts in PACKS.items():
            rows = 1 if pack == "rows" else P
            width = sum(int(np.prod(shape)) for _, shape in parts)
            if pack in ("biased", "top"):
                packed[pack] = packed[{"biased": "latent", "top": "linear"}[pack]][:, 0:width]
            else:
                packed[pack] = sb("pack_" + pack, [rows, width])
            at = 0
            for name, shape in parts:
                size = int(np.prod(shape))
                view = packed[pack][:, at:at + size]
                if len(shape) == 2:
                    view = view.rearrange("p (a b) -> p a b", a=shape[0])
                elif len(shape) == 3:
                    view = view.rearrange("p (a b c) -> p a b c", a=shape[0], b=shape[1])
                w[name] = view
                at += size

        m.biased_weights, m.top_weights = packed["biased"], packed["top"]
        m.loaded_x = sem("loaded_x")
        m.loaded_constants = sem("loaded_constants")
        m.loaded_linear = sem("loaded_linear")
        m.loaded_latent = sem("loaded_latent")
        m.loaded_ctx = sem("loaded_ctx")
        m.loaded_latent_all = 16
        m.loaded_shared = sem("loaded_shared")
        m.slots_cleared = sem("slots_cleared")
        zeros_ready = sem("zeros_ready")
        m.loaded_causal = sem("loaded_causal")
        m.loaded_biased = sem("loaded_biased")
        m.loaded_top = sem("loaded_top")
        stored = sem("stored")
        power_ready = sem("power_ready")
        m.loaded_x_all, m.ready_constants_all, m.loaded_linear_all = 16, 16, 32
        m.ready_constants = m.loaded_constants

        with nc.Block() as block:
            @block.sync
            def _(sp):
                sp.dma_start(packed["constants"][:], dram["constants"]).then_inc(m.loaded_constants, 16)
                sp.dma_start(m.X[:], dram["x"].rearrange("(t p) d -> p t d", p=P)).then_inc(m.loaded_x, 16)
                sp.dma_start(packed["rows"][:], dram["rows"]).then_inc(m.loaded_linear, 16)
                sp.dma_start(packed["linear"][:], dram["linear"]).then_inc(m.loaded_linear, 16)
                sp.dma_start(m.C[:], dram["ctx"].rearrange("(t p) d -> p t d", p=P)).then_inc(m.loaded_ctx, 16)
                sp.dma_start(packed["latent"][:], dram["latent"]).then_inc(m.loaded_latent, 16)
                sp.dma_start(packed["shared"][:], dram["shared"]).then_inc(m.loaded_shared, 16)
                sp.dma_start(packed["causal"][:], dram["causal"]).then_inc(m.loaded_causal, 16)
                sp.dma_start(w["rel_bias"][:], dram["rel_bias"]).then_inc(m.loaded_biased, 16)
                sp.dma_start(w["expert_b"][:], dram["expert_b"]).then_inc(m.loaded_top, 16)
                sp.wait_ge(zeros_ready, 1)
                sp.dma_start(m.slot_rows.rearrange("(c p) d -> p c d", p=P), over(zeros[:], 1, SLOTS // P))\
                    .then_inc(m.slots_cleared, 16)
                sp.dma_start(m.result_rows[SLOTS:], zeros[0:1, :]).then_inc(m.slots_cleared, 16)

            @block.gpsimd
            def _(pool):
                pool.memset(zeros[:], 0.0).then_inc(zeros_ready, 1)
                pool.memset(m.minus_half[:], -0.5).then_inc(power_ready, 1)

        linear_attention(nc, m)
        latent_attention(nc, m)
        routed_experts(nc, m)
        reuse_semaphores(nc, m)
        causal_attention(nc, m)
        biased_attention(nc, m)
        top_expert(nc, m)
        with nc.Block() as block:
            @block.sync
            def _(sp):
                sp.dma_start(out.rearrange("(t p) d -> p t d", p=P), m.X[:]).then_inc(stored, 16)
                sp.wait_ge(stored, 16)


def constants():
    p = np.arange(P)
    c = {}
    c["ident"] = np.eye(P)
    c["ones"] = np.ones((P, P))
    c["same_head"] = p[:, None] // DH0 == p[None] // DH0
    heads = np.arange(H).reshape(HP, 2).T.reshape(-1)
    c["head_rows"] = p[:, None] // DH0 == heads[None]
    c["head_rows_flat"] = p[:, None] // DH0 == np.arange(H)[None]
    c["causal_kq"] = np.arange(SEQ)[None] >= p[:, None] % SEQ
    c["causal_bias"] = np.where(np.arange(SEQ)[None] <= p[:, None] % SEQ, 0.0, LOWEST)
    inv_freq = np.float32(1.0) / np.float32(10000.0) ** (np.arange(0, DH0, 2, dtype=np.float32) / np.float32(DH0))
    theta = np.arange(SEQ, dtype=np.float32)[:, None] * inv_freq[None]
    pair = p % DH0 // 2
    c["cos"] = np.cos(theta).T[pair]
    c["sin"] = np.sin(theta).T[pair] * np.where(p % 2, 1.0, -1.0)[:, None]
    c["not_first"] = np.broadcast_to(np.arange(N) % SEQ != 0, (P, N))
    c["earlier"] = p[:, None] < p[None]
    c["expert_ids"] = np.broadcast_to(np.arange(E1), (P, E1))
    c["expert_base"] = np.broadcast_to(np.arange(E1) * CAP, (P, E1))
    c["distance"] = bucket_rows()
    return {name: np.asarray(a, np.float32) for name, a in c.items()}


def bucket_rows():
    buckets, furthest = 32, 128
    exact = buckets // 2
    distance = np.maximum(np.arange(P) - (SEQ - 1), 0)
    safe = np.maximum(distance, 1).astype(np.float32)
    log = np.log(safe / np.float32(exact)) / np.log(np.float32(furthest / exact))
    large = np.minimum(exact + (log * np.float32(buckets - exact)).astype(np.int32), buckets - 1)
    bucket = np.where(distance < exact, distance, large)
    return np.arange(P)[:, None] == bucket[None]


def layouts(a):
    per = {}
    swap = np.arange(D) ^ 1
    qkv = a["L0_attn_w_qkv"]
    wq, wk, wv = qkv[:D], qkv[D:2 * D], qkv[2 * D:]
    per["linear"] = {
        "dw": a["L0_attn_w_dw"], "b_gate": a["L0_attn_b_gate"][:, None], "ln_g": a["L0_attn_ln_g"][:, None],
        "ln_b": a["L0_attn_ln_b"][:, None], "pw": a["L0_attn_w_pw"].T,
        "qk": np.stack([wq.T, wk.T, wq[swap].T, wk[swap].T], 1),
        "v0": wv.reshape(HP, 2, DH0, D).transpose(3, 1, 0, 2),
        "gate": a["L0_attn_w_gate"].T, "o0": a["L0_attn_w_o"].T, "moe_gate": a["L0_attn_w_moe_gate"].T,
        "b1": a["L0_attn_b1"].reshape(E0 * F0, P).T,
        "w1": a["L0_attn_w1"].reshape(E0, F0, P, D).transpose(3, 0, 1, 2),
        "w2": a["L0_attn_w2"].reshape(E0, D, F0, P).transpose(3, 0, 2, 1),
    }
    wkv = a["L0_xattn_Wkv"]
    per["latent"] = {
        "x_affine": np.stack([a["L0_xattn_" + n] for n in ("g1", "b1", "g2", "b2")], 1),
        "xq": a["L0_xattn_Wq"], "xk": wkv[:, :INNER], "xv": wkv[:, INNER:],
        "xo": a["L0_xattn_Wout"].reshape(HP, P, D).transpose(1, 0, 2),
    }
    per["shared"] = {
        "router": a["L0_ffn_router_w"].T, "sg": a["L0_ffn_sg"], "su": a["L0_ffn_su"],
        "sd": a["L0_ffn_sd"].reshape(FS, P, D).transpose(1, 0, 2),
    }
    per["causal"] = {
        "c_bias": np.stack([a["L1_attn_bq"], a["L1_attn_bk"]], 1),
        "cqk": np.stack([a["L1_attn_Wq"], a["L1_attn_Wk"]], 1),
        "cv": a["L1_attn_Wv"].reshape(D, HP, 2, DH0).transpose(0, 2, 1, 3),
        "co": a["L1_attn_Wo"],
    }
    per["biased"] = {
        "bq": a["L1_xattn_Wq"], "bk": a["L1_xattn_Wk"],
        "bvp": a["L1_xattn_Wv"].reshape(D, HP, 2, DHX).transpose(0, 2, 1, 3),
        "bo1": a["L1_xattn_Wo"].reshape(HP, P, D).transpose(1, 0, 2),
    }
    per["top"] = {"router1": a["L1_ffn_router_w"].T, "expert": a["L1_ffn_expert_w"].transpose(2, 0, 1)}
    per["rows"] = {"b2": a["L0_attn_b2"], "bv": a["L1_attn_bv"].reshape(HP, 2, DH0).transpose(1, 0, 2),
                   "bo": a["L1_attn_bo"], "router_b": a["L1_ffn_router_b"]}
    per["constants"] = constants()
    arrays = {"x": a["x"].reshape(TOKENS, D), "ctx": a["ctx_1024"].reshape(TOKENS, D)}
    down = a["L0_ffn_rd"].reshape(E1, FR, P, D).transpose(0, 2, 1, 3).reshape(E1, P, FR * D)
    arrays["mask"] = a["mask_1x1xSxS2_bk0"].reshape(SEQ, SEQ)
    arrays["rel_bias"] = a["L1_xattn_rel_bias"].T
    arrays["expert_b"] = a["L1_ffn_expert_b"]
    arrays["experts"] = np.concatenate([a["L0_ffn_rg"], a["L0_ffn_ru"], down], axis=2)
    for pack, parts in PACKS.items():
        rows = 1 if pack == "rows" else P
        arrays[pack] = np.concatenate([per[pack][name].reshape(rows, -1) for name, _ in parts], axis=1)
    return arrays


def kernel(**inputs):
    import concourse.bacc as bacc
    from concourse.bass_utils import run_bass_kernel_spmd

    nc = bacc.Bacc("TRN2", target_bir_lowering=False, num_devices=1)
    arrays = {name: np.ascontiguousarray(x) for name, x in
              layouts({name: np.asarray(x) for name, x in inputs.items()}).items()}
    dram = {name: nc.dram_tensor(name + "_dram", x.shape, mybir.dt.from_np(x.dtype), kind="ExternalInput").ap()
            for name, x in arrays.items()}
    out = nc.dram_tensor("out_dram", (TOKENS, D), F32, kind="ExternalOutput").ap()
    decoder(nc, dram, out)
    result = run_bass_kernel_spmd(nc, [{name + "_dram": x for name, x in arrays.items()}], core_ids=[0])
    return result.results[0]["out_dram"].reshape(NSEQ, SEQ, D)
```

```python
from contextlib import ExitStack

import concourse.bass as bass
from concourse import mybir
import numpy as np

F32 = mybir.dt.float32
U32 = mybir.dt.uint32
U8 = mybir.dt.uint8
ALU = mybir.AluOpType
ACT = mybir.ActivationFunctionType
AX = mybir.AxisListType

P = 128
D = 128
SEQ = 64
NSEQ = 64
TOKENS = NSEQ * SEQ
TILES = TOKENS // P
GT = 4
GROUPS = TILES // GT
GB = GT * P // SEQ
N = GT * P
H = 16
HP = H // 2
DH0 = D // H
DHX = 64
INNER = H * DHX
E0 = 4
F0 = 4
E1 = 8
FR = 4
FS = 8
CAP = max(int(1.25 * TOKENS / E1), 1)
SLOTS = E1 * CAP
CT = CAP // P
LOWEST = float(np.finfo(np.float32).min)
RMS_EPS = float(np.finfo(np.float32).eps)
LN_EPS = 1e-5


def stage_semaphore(nc, m, name):
    m.stage_semaphores.append(nc.alloc_semaphore(name=name))
    return m.stage_semaphores[-1]


def reuse_semaphores(nc, m):
    nc.clear_and_free_semaphores(m.stage_semaphores)
    m.stage_semaphores = []
    nc.all_engine_barrier()


def over(ap, axis, count):
    shape = list(ap.shape)
    return ap.unsqueeze(axis).broadcast_to(shape[:axis] + [count] + shape[axis:])


def tiles_of(ap):
    return ap.rearrange("p (t n) -> p t n", n=P)


def seqs_of(ap):
    return ap.rearrange("p (b t) -> p b t", t=SEQ)


class Shared:
    pass


class NormSemaphores:

    def __init__(self, sem, name):
        self.sums = sem(name + "_sums")
        self.stats = sem(name + "_stats")
        self.var = sem(name + "_var")
        self.rstd = sem(name + "_rstd")
        self.normed = sem(name + "_normed")


def step_of(g, d):
    return g, d


def count(step, per, extra):
    g, d = step
    return per * g + (per * d + extra)


def reach(engine, sem, value):
    if not isinstance(value, int) or value > 0:
        engine.wait_ge(sem, value)


def run_steps(engine, steps, body, depth=2):
    pairs = (steps - 1 - depth) // 2
    body(step_of(0, 0), 0, depth)
    with engine.Fori(0, pairs) as j:
        g = 2 * j
        body(step_of(g, 1), 1, depth)
        body(step_of(g, 2), 0, depth)
    for n in range(2 * pairs + 1, steps + 1):
        body(step_of(0, n), n % 2, min(depth, steps - 1 - n))


def is_first(step):
    return isinstance(step[0], int) and step[1] == 0


def later(step, n):
    return step_of(step[0], step[1] + n)


def norm_stats(dve, m, step, src, sem, count_of_norms, before, tiles=2):
    total = tiles * count_of_norms
    for t in range(tiles):
        dve.bn_stats(m.bn[:, t, :], src(t)).then_inc(sem.sums, 1)
    dve.wait_ge(sem.sums, count(step, total, tiles * (before + 1)))
    dve.memset(m.spare[:], 0.0)
    for t in range(tiles):
        dve.bn_aggr(m.mean_var[:, t, :], m.bn[:, t, :]).then_inc(sem.stats, 1)
    dve.wait_ge(sem.stats, count(step, total, tiles * (before + 1)))
    dve.tensor_scalar(m.var_eps[:, 0:tiles], m.mean_var[:, 0:tiles, 1], LN_EPS, None, ALU.add).then_inc(sem.var, 1)


def norm_root(pool, m, step, sem, count_of_norms, before, tiles=2):
    pool.wait_ge(sem.var, count(step, count_of_norms, before + 1))
    pool.tensor_tensor(m.rstd[:, 0:tiles], m.var_eps[:, 0:tiles], m.minus_half[:, 0:tiles], ALU.pow).then_inc(sem.rstd, 1)


def norm_apply(dve, m, step, src, dst, sem, count_of_norms, before, tiles=2):
    dve.wait_ge(sem.rstd, count(step, count_of_norms, before + 1))
    for t in range(tiles):
        dve.tensor_scalar(dst(t), src(t), m.mean_var[:, t, 0:1], m.rstd[:, t:t + 1],
                          ALU.subtract, ALU.mult).then_inc(sem.normed, 1)

def linear_attention(nc, m):
    w = m.w
    J = H // 4
    FJ = D // J
    HIDS = E0 * F0
    OUTS = E0 * GT
    with ExitStack() as ctx:
        def sb(name, shape):
            return ctx.enter_context(nc.sbuf_tensor("la_" + name, shape, F32))

        def sem(name):
            return stage_semaphore(nc, m, "la_" + name)

        xn = sb("xn", [P, GT, D])
        hT = sb("hT", [P, N])
        conv = sb("conv", [P, N])
        x1T = sb("x1T", [P, N])
        delta = sb("delta", [P, N])
        by_cos = sb("by_cos", [P, 2, N])
        by_sin = sb("by_sin", [P, 2, N])
        rot = sb("rot", [P, 2, N])
        low = sb("low", [P, 2, N])
        phi = sb("phi", [P, 2, N])
        k_prefix = sb("k_prefix", [P, N])
        qk = sb("qk", [P, N])
        rden = sb("rden", [P, N])
        kpar = sb("kpar", [P, GB, 2, SEQ])
        qpairs = sb("qpairs", [P, 2, HP * SEQ])
        scores = sb("scores", [P, 2, HP * SEQ])
        vheads = sb("vheads", [P, GB, HP, FJ])
        attnT = sb("attnT", [P, N])
        gate = sb("gate", [P, N])
        x2T = sb("x2T", [P, N])
        x2 = sb("x2", [P, GT, D])
        xn2 = sb("xn2", [P, GT, D])
        h2T = sb("h2T", [P, N])
        top = sb("top", [P, GT])
        gw = sb("gw", [P, GT, E0])
        gsum = sb("gsum", [P, GT])
        hid = sb("hid", [P, 2, F0, N])
        FIRST, SECOND, THIRD, FOURTH = (m.bank(n) for n in range(4))
        SCORES = (THIRD, FOURTH)
        HIDDEN, OUT = (m.bank(4), m.bank(5)), (m.bank(6), m.bank(7))

        ln = NormSemaphores(sem, "ln")
        ln2 = NormSemaphores(sem, "ln2")
        zeroed = sem("zeroed")
        hT_turned = sem("hT_turned")
        hT_ready = sem("hT_ready")
        conv_part = sem("conv_part")
        pw_done = sem("pw_done")
        x1_ready = sem("x1_ready")
        delta_ready = sem("delta_ready")
        qk_done = sem("qk_done")
        v_done = sem("v_done")
        v_ready = sem("v_ready")
        rope_part = sem("rope_part")
        rot_ready = sem("rot_ready")
        low_ready = sem("low_ready")
        exp_ready = sem("exp_ready")
        phi_ready = sem("phi_ready")
        prefix_ready = sem("prefix_ready")
        qk_ready = sem("qk_ready")
        den_done = sem("den_done")
        den_ready = sem("den_ready")
        inverse_ready = sem("inverse_ready")
        kpar_ready = sem("kpar_ready")
        qpairs_ready = sem("qpairs_ready")
        scores_done = sem("scores_done")
        scores_ready = sem("scores_ready")
        num_done = sem("num_done")
        attn_ready = sem("attn_ready")
        gate_done = sem("gate_done")
        gate_ready = sem("gate_ready")
        out_done = sem("out_done")
        gated = sem("gated")
        x2T_ready = sem("x2T_ready")
        x2_turned = sem("x2_turned")
        x2_ready = sem("x2_ready")
        x2_added = sem("x2_added")
        h2_turned = sem("h2_turned")
        h2_ready = sem("h2_ready")
        logits_done = sem("logits_done")
        gw_step = sem("gw_step")
        gw_exp = sem("gw_exp")
        hid_done = sem("hid_done")
        hid_ready = sem("hid_ready")
        expert_done = sem("expert_done")
        expert_used = sem("expert_used")

        def run_groups(engine, body):
            body(step_of(0, 0), None, step_of(0, 1))
            body(step_of(0, 1), step_of(0, 0), step_of(0, 2))
            with engine.Fori(0, GROUPS - 3) as g:
                body(step_of(g, 2), step_of(g, 1), step_of(g, 3))
            body(step_of(0, GROUPS - 1), step_of(0, GROUPS - 2), None)
            body(None, step_of(0, GROUPS - 1), None)

        with nc.Block() as block:

            @block.tensor
            def _(pe):
                pe.wait_ge(m.loaded_linear, m.loaded_linear_all)
                pe.wait_ge(m.ready_constants, m.ready_constants_all)

                def hidden(e, n):
                    if e is not None:
                        reach(pe, hid_ready, count(e, HIDS, n - 1))
                        pe.matmul(HIDDEN[n % 2], w["w1"][:, n // F0, n % F0, :], h2T[:], start=True, stop=True)\
                            .then_inc(hid_done, 1)

                def output(e, n, tiles):
                    if e is None:
                        return
                    if tiles[0] == 0:
                        pe.wait_ge(hid_ready, count(e, HIDS, F0 * n + F0))
                        reach(pe, expert_used, count(e, OUTS, GT * (n - 1)))
                    for t in tiles:
                        out = OUT[n % 2][:, P * t:P * t + P]
                        pe.matmul(out, w["ones"][0:1, :], w["b2"][0:1, n, :], start=True, stop=False)
                        for f in range(F0):
                            mm = pe.matmul(out, hid[:, n % 2, f, P * t:P * t + P], w["w2"][:, n, f, :],
                                           start=False, stop=(f == F0 - 1))
                    mm.then_inc(expert_done, 1)

                def numerator(b):
                    for up in range(2):
                        for j in range(J):
                            hp = 2 * j + up
                            mm = pe.matmul(FIRST[FJ * j:FJ * j + FJ, SEQ * b:SEQ * b + SEQ], vheads[:, b, hp, :],
                                           scores[:, b % 2, SEQ * hp:SEQ * hp + SEQ], start=(up == 0), stop=(up == 1))
                    mm.then_inc(num_done, 1)

                def body(a, e, nxt):
                    if a is not None:
                        pe.wait_ge(ln.normed, count(a, GT, GT))
                        reach(pe, h2_ready, count(a, 1, 0))
                        for t in range(GT):
                            mm = pe.transpose(FIRST[:, P * t:P * t + P], xn[:, t, :], w["ident"][:])
                        mm.then_inc(hT_turned, 1)
                    for n in range(4):
                        hidden(e, n)
                    if a is not None:
                        pe.wait_ge(conv_part, count(a, 3, 3))
                        pe.matmul(SECOND, w["pw"][:], conv[:], start=True, stop=True).then_inc(pw_done, 1)
                    hidden(e, 4)
                    if a is not None:
                        pe.wait_ge(x1_ready, count(a, 1, 1))
                        for n, out in enumerate((FIRST, SECOND, THIRD, FOURTH)):
                            mm = pe.matmul(out, w["qk"][:, n, :], x1T[:], start=True, stop=True)
                        mm.then_inc(qk_done, 1)
                    for n in range(5, 8):
                        hidden(e, n)
                    output(e, 0, (0, 1))
                    output(e, 0, (2, 3))
                    hidden(e, 8)
                    if a is not None:
                        pe.wait_ge(rope_part, count(a, 2, 2))
                        for b in range(GB):
                            for par in range(2):
                                mm = pe.matmul(FIRST[SEQ * par:SEQ * par + SEQ, HP * DH0 * b:HP * DH0 * (b + 1)],
                                               x1T[:, SEQ * b:SEQ * b + SEQ], w["v0"][:, par, :], start=True, stop=True)
                        mm.then_inc(v_done, 1)
                    hidden(e, 9)
                    if a is not None:
                        pe.wait_ge(qk_ready, count(a, 1, 1))
                        pe.matmul(SECOND, w["same_head"][:], qk[:], start=True, stop=True).then_inc(den_done, 1)
                    for b in range(GB):
                        if a is not None:
                            if b == 0:
                                pe.wait_ge(kpar_ready, count(a, 2, 2))
                            if b == 1:
                                pe.wait_ge(v_ready, count(a, 4, 4))
                            if b >= 1:
                                pe.wait_ge(scores_ready, count(a, GB, b))
                            pe.wait_ge(qpairs_ready, count(a, GB, b + 1))
                            pe.matmul(SCORES[b % 2], kpar[:, b].rearrange("p a n -> p (a n)"), qpairs[:, b % 2, :],
                                      start=True, stop=True).then_inc(scores_done, 1)
                        if b < 2:
                            hidden(e, 10 + b)
                        elif b < 4:
                            output(e, 1, (2 * b - 4, 2 * b - 3))
                        else:
                            hidden(e, 8 + b)
                        if a is not None and b >= 1:
                            numerator(b - 1)
                    if a is not None:
                        pe.wait_ge(delta_ready, count(a, 1, 1))
                        pe.wait_ge(den_ready, count(a, 1, 1))
                        pe.wait_ge(scores_ready, count(a, GB, GB))
                        pe.matmul(SECOND, w["gate"][:], delta[:], start=True, stop=True).then_inc(gate_done, 1)
                        numerator(GB - 1)
                    output(e, 2, (0, 1))
                    if a is not None:
                        pe.wait_ge(attn_ready, count(a, 1, 1))
                        pe.matmul(THIRD, w["o0"][:], attnT[:], start=True, stop=True).then_inc(out_done, 1)
                    output(e, 2, (2, 3))
                    if a is not None:
                        pe.wait_ge(x2T_ready, count(a, 1, 1))
                        for t in range(GT):
                            mm = pe.transpose(FOURTH[:, P * t:P * t + P], x2T[:, P * t:P * t + P], w["ident"][:])
                        mm.then_inc(x2_turned, 1)
                    output(e, 3, (0, 1))
                    output(e, 3, (2, 3))
                    if a is not None:
                        pe.wait_ge(ln2.normed, count(a, GT, GT))
                        for t in range(GT):
                            mm = pe.transpose(FIRST[:, P * t:P * t + P], xn2[:, t, :], w["ident"][:])
                        mm.then_inc(h2_turned, 1)
                        pe.wait_ge(h2_ready, count(a, 1, 1))
                        for t in range(GT):
                            mm = pe.matmul(SECOND[:, E0 * t:E0 * t + E0], h2T[:, P * t:P * t + P], w["moe_gate"][:],
                                           start=True, stop=True)
                        mm.then_inc(logits_done, 1)

                run_groups(pe, body)

            @block.scalar
            def _(act):
                act.wait_ge(m.loaded_linear, m.loaded_linear_all)
                act.wait_ge(zeroed, 2)

                def activate(e, which):
                    if e is None:
                        return
                    for n in which:
                        act.wait_ge(hid_done, count(e, HIDS, n + 1))
                        if n % F0 == 0:
                            reach(act, expert_done, count(e, 2 * E0, 2 * (n // F0) - 2))
                        act.activation(hid[:, n // F0 % 2, n % F0, :], HIDDEN[n % 2], ACT.Silu,
                                       bias=w["b1"][:, n:n + 1]).then_inc(hid_ready, 1)

                def body(a, e, nxt):
                    if a is not None:
                        act.wait_ge(hT_turned, count(a, 1, 1))
                        act.activation(hT[:], FIRST, ACT.Copy).then_inc(hT_ready, 1)
                    activate(e, range(8))
                    if a is not None:
                        act.wait_ge(low_ready, count(a, 1, 1))
                        act.activation(low[:], low[:], ACT.Exp).then_inc(exp_ready, 1)
                    activate(e, range(8, 9))
                    if a is not None:
                        act.wait_ge(v_done, count(a, 1, 1))
                        for par in range(2):
                            part = slice(SEQ * par, SEQ * par + SEQ)
                            src = FIRST[part].rearrange("p (b j u c) -> p b j u c", b=GB, u=2, c=DH0)
                            for up in range(2):
                                at = DH0 * (2 * up + par)
                                out = vheads[part].rearrange("p b (j u) f -> p b j u f", u=2)[:, :, :, up, at:at + DH0]
                                act.activation(out, src[:, :, :, up, :], ACT.Copy).then_inc(v_ready, 1)
                        act.wait_ge(phi_ready, count(a, 1, 1))
                        for par in range(2):
                            act.activation(kpar[:, :, par, :], seqs_of(phi[:, 1, :]), ACT.Copy,
                                           scale=w["parity"][:, par:par + 1]).then_inc(kpar_ready, 1)
                    activate(e, range(9, 16))
                    if a is not None:
                        act.wait_ge(gate_done, count(a, 1, 1))
                        act.activation(gate[:], SECOND, ACT.Sigmoid, bias=w["b_gate"][:, 0:1]).then_inc(gate_ready, 1)
                        act.wait_ge(x2_turned, count(a, 1, 1))
                        act.activation(x2[:], tiles_of(FOURTH), ACT.Copy).then_inc(x2_ready, 1)
                        act.wait_ge(h2_turned, count(a, 1, 1))
                        act.activation(h2T[:], FIRST, ACT.Identity, bias=w["ln_b"][:, 0:1], scale=w["ln_g"][:, 0:1])\
                            .then_inc(h2_ready, 1)
                        act.wait_ge(gw_step, count(a, 5, 2))
                        act.activation(gw[:], gw[:], ACT.Exp).then_inc(gw_exp, 1)

                run_groups(act, body)

            @block.gpsimd
            def _(pool):
                pool.memset(vheads[:], 0.0).then_inc(zeroed, 1)
                pool.memset(delta[:], 0.0).then_inc(zeroed, 1)
                pool.wait_ge(m.loaded_linear, m.loaded_linear_all)
                pool.wait_ge(zeroed, 2)
                norm_root(pool, m, step_of(0, 0), ln, 1, 0, GT)

                def body(a, e, nxt):
                    if a is None:
                        return
                    pool.wait_ge(x1_ready, count(a, 1, 1))
                    x1 = seqs_of(x1T[:])
                    pool.tensor_tensor(seqs_of(delta[:])[:, :, 1:], x1[:, :, 1:], x1[:, :, :SEQ - 1],
                                       ALU.subtract).then_inc(delta_ready, 1)
                    pool.wait_ge(rope_part, count(a, 2, 2))
                    pool.tensor_tensor(rot[:], by_cos[:], by_sin[:], ALU.add).then_inc(rot_ready, 1)
                    pool.wait_ge(phi_ready, count(a, 1, 1))
                    for b in range(GB):
                        if b >= 2:
                            pool.wait_ge(scores_done, count(a, GB, b - 1))
                        pool.tensor_tensor(seqs_of(qpairs[:, b % 2, :]), over(phi[:, 0, SEQ * b:SEQ * b + SEQ], 1, HP),
                                           over(w["pair_rows"][:], 2, SEQ), ALU.mult).then_inc(qpairs_ready, 1)
                    if nxt is not None:
                        norm_root(pool, m, nxt, ln, 1, 0, GT)
                    norm_root(pool, m, a, ln2, 1, 0, GT)
                    pool.wait_ge(x2_ready, count(a, 1, 1))
                    rows = m.X[:, bass.ds(count(a, GT, 0), GT), :]
                    pool.tensor_tensor(rows, rows, x2[:], ALU.add).then_inc(x2_added, 1)

                run_groups(pool, body)

            @block.vector
            def _(dve):
                dve.wait_ge(m.loaded_x, m.loaded_x_all)

                def row(step):
                    return lambda t: m.X[:, bass.ds(count(step, GT, t), 1), :]

                def add_expert(e, n):
                    if e is None:
                        return
                    dve.wait_ge(expert_done, count(e, 2 * E0, 2 * n + 2))
                    for t in range(GT):
                        reach(dve, expert_used, count(e, OUTS, GT * (n - 1) + t + 1))
                        out = m.X[:, bass.ds(count(e, GT, t), 1), :]
                        dve.scalar_tensor_tensor(out=out, in0=OUT[n % 2][:, P * t:P * t + P].unsqueeze(1),
                                                 scalar=gw[:, t, n:n + 1], in1=out,
                                                 op0=ALU.mult, op1=ALU.add).then_inc(expert_used, 1)

                def body(a, e, nxt):
                    if a is not None:
                        dve.wait_ge(hT_ready, count(a, 1, 1))
                        h, y = seqs_of(hT[:]), seqs_of(conv[:])
                        dve.tensor_scalar(conv[:], hT[:], w["dw"][:, 2:3], None, ALU.mult).then_inc(conv_part, 1)
                        for n, back in enumerate((1, 2)):
                            dve.wait_ge(conv_part, count(a, 3, n + 1))
                            dve.scalar_tensor_tensor(out=y[:, :, back:], in0=h[:, :, :SEQ - back],
                                                     scalar=w["dw"][:, 2 - back:3 - back], in1=y[:, :, back:],
                                                     op0=ALU.mult, op1=ALU.add).then_inc(conv_part, 1)
                        dve.wait_ge(pw_done, count(a, 1, 1))
                        dve.tensor_tensor(x1T[:], hT[:], SECOND, ALU.add).then_inc(x1_ready, 1)
                        dve.wait_ge(qk_done, count(a, 1, 1))
                        for out, first, table in ((by_cos, 0, w["cos"]), (by_sin, 2, w["sin"])):
                            dve.tensor_tensor(seqs_of(out[:].rearrange("p a n -> p (a n)")),
                                              seqs_of(m.ps[:, first:first + 2, :].rearrange("p a n -> p (a n)")),
                                              over(table[:], 1, 2 * GB), ALU.mult).then_inc(rope_part, 1)
                        dve.wait_ge(rot_ready, count(a, 1, 1))
                        dve.tensor_scalar(low[:], rot[:], 0.0, None, ALU.min).then_inc(low_ready, 1)
                    add_expert(e, 0)
                    if a is not None:
                        dve.wait_ge(exp_ready, count(a, 1, 1))
                        dve.scalar_tensor_tensor(out=phi[:], in0=rot[:], scalar=0.0, in1=low[:],
                                                 op0=ALU.max, op1=ALU.add).then_inc(phi_ready, 1)
                        dve.wait_ge(phi_ready, count(a, 1, 1))
                        dve.tensor_tensor_scan(k_prefix[:], w["not_first"][:], phi[:, 1, :], 0.0,
                                               ALU.mult, ALU.add).then_inc(prefix_ready, 1)
                        dve.wait_ge(prefix_ready, count(a, 1, 1))
                        dve.tensor_tensor(qk[:], phi[:, 0, :], k_prefix[:], ALU.mult).then_inc(qk_ready, 1)
                        dve.wait_ge(den_done, count(a, 1, 1))
                        dve.tensor_scalar(rden[:], SECOND, 1e-6, None, ALU.add).then_inc(den_ready, 1)
                        for b in range(GB):
                            dve.wait_ge(scores_done, count(a, GB, b + 1))
                            if b >= 2:
                                dve.wait_ge(num_done, count(a, GB, b - 1))
                            dve.tensor_tensor(seqs_of(scores[:, b % 2, :]), seqs_of(SCORES[b % 2]),
                                              over(w["causal_kq"][:], 1, HP), ALU.mult).then_inc(scores_ready, 1)
                            if b < GT:
                                part = rden[:, P * b:P * b + P]
                                dve.wait_ge(den_ready, count(a, 1, 1))
                                dve.reciprocal(part, part).then_inc(inverse_ready, 1)
                            if b == 4:
                                add_expert(e, 1)
                        if nxt is not None:
                            norm_stats(dve, m, nxt, row(nxt), ln, 1, 0, GT)
                            dve.wait_ge(hT_turned, count(a, 1, 1))
                            norm_apply(dve, m, nxt, row(nxt), lambda t: xn[:, t, :], ln, 1, 0, GT)
                        dve.wait_ge(inverse_ready, count(a, GT, GT))
                        dve.wait_ge(num_done, count(a, GB, GB))
                        dve.tensor_tensor(attnT[:], FIRST, rden[:], ALU.mult).then_inc(attn_ready, 1)
                        dve.wait_ge(gate_ready, count(a, 1, 1))
                        dve.wait_ge(out_done, count(a, 1, 1))
                        dve.tensor_tensor(gate[:], THIRD, gate[:], ALU.mult).then_inc(gated, 1)
                        dve.wait_ge(gated, count(a, 1, 1))
                        dve.tensor_tensor(x2T[:], x1T[:], gate[:], ALU.add).then_inc(x2T_ready, 1)
                    else:
                        add_expert(e, 1)
                    add_expert(e, 2)
                    if a is not None:
                        dve.wait_ge(x2_ready, count(a, 1, 1))
                        norm_stats(dve, m, a, lambda t: x2[:, t, :], ln2, 1, 0, GT)
                        norm_apply(dve, m, a, lambda t: x2[:, t, :], lambda t: xn2[:, t, :], ln2, 1, 0, GT)
                    add_expert(e, 3)
                    if a is not None:
                        dve.wait_ge(logits_done, count(a, 1, 1))
                        lg = SECOND[:, 0:GT * E0].rearrange("p (t e) -> p t e", e=E0)
                        dve.tensor_reduce(top[:], lg, AX.X, ALU.max).then_inc(gw_step, 1)
                        dve.wait_ge(gw_step, count(a, 5, 1))
                        if e is not None:
                            dve.wait_ge(expert_used, count(e, OUTS, OUTS))
                        dve.tensor_tensor(gw[:], lg, over(top[:], 2, E0), ALU.subtract).then_inc(gw_step, 1)
                        dve.wait_ge(gw_exp, count(a, 1, 1))
                        dve.tensor_reduce(gsum[:], gw[:], AX.X, ALU.add).then_inc(gw_step, 1)
                        dve.wait_ge(gw_step, count(a, 5, 3))
                        dve.reciprocal(gsum[:], gsum[:]).then_inc(gw_step, 1)
                        dve.wait_ge(gw_step, count(a, 5, 4))
                        dve.tensor_tensor(gw[:], gw[:], over(gsum[:], 2, E0), ALU.mult).then_inc(gw_step, 1)
                        dve.wait_ge(gw_step, count(a, 5, 5))
                        dve.wait_ge(x2_added, count(a, 1, 1))

                norm_stats(dve, m, step_of(0, 0), row(step_of(0, 0)), ln, 1, 0, GT)
                norm_apply(dve, m, step_of(0, 0), row(step_of(0, 0)), lambda t: xn[:, t, :], ln, 1, 0, GT)
                dve.wait_ge(m.loaded_linear, m.loaded_linear_all)
                dve.wait_ge(m.ready_constants, m.ready_constants_all)
                run_groups(dve, body)
                dve.wait_ge(expert_used, GROUPS * OUTS)

def latent_attention(nc, m):
    w = m.w
    STEPS = TILES // 2
    SB = 2 * P // SEQ
    NS = 2 * P
    KEYS = 2 * SEQ
    UNITS = 8
    UH = HP // 2
    PROJ = 24
    COPIES = PROJ // 2
    PROJ_SLOTS = (range(0, 4), range(4, 8), range(8, 12), range(12, 15), range(15, 18), range(18, 21), range(21, 24),
                  range(0))
    NORMS = 3
    with ExitStack() as ctx:
        def sb(name, shape):
            return ctx.enter_context(nc.sbuf_tensor("xa_" + name, shape, F32))

        def sem(name):
            return stage_semaphore(nc, m, "xa_" + name)

        cn = sb("cn", [P, 2, D])
        xn = sb("xn", [P, 2, D])
        lat = sb("lat", [P, 2, D])
        kvT = sb("kvT", [P, SB, KEYS])
        qT = sb("qT", [P, 2, HP, NS])
        kT = sb("kT", [P, 2, HP, SB * KEYS])
        v = sb("v", [P, 2, SB, INNER])
        probs = sb("probs", [P, 4, UH, KEYS])
        probsT = sb("probsT", [P, 2, UH, P])
        top = sb("top", [P, 4, UH])
        total = sb("total", [P, 4, UH])
        attnT = sb("attnT", [P, 2, HP, P])
        bank = m.bank
        TURN_BANK, ATTN_BANK, OUT_BANK, PROJ_BANK = 2, 3, 4, 5

        ln = NormSemaphores(sem, "ln")
        kv_turned = sem("kv_turned")
        kv_ready = sem("kv_ready")
        proj_done = sem("proj_done")
        proj_even = sem("proj_even")
        proj_odd = sem("proj_odd")
        scores_done = sem("scores_done")
        top_ready = sem("top_ready")
        less_top = sem("less_top")
        exp_ready = sem("exp_ready")
        sum_ready = sem("sum_ready")
        inverse_ready = sem("inverse_ready")
        probs_ready = sem("probs_ready")
        probs_turned = sem("probs_turned")
        probsT_ready = sem("probsT_ready")
        attn_done = sem("attn_done")
        attn_ready = sem("attn_ready")
        out_done = sem("out_done")
        x_added = sem("x_added")

        def unit(u):
            n = u % UNITS
            return n // 4, n // 2 % 2, n % 2

        def copied(engine, step, n):
            reach(engine, (proj_even, proj_odd)[n % 2], count(step, COPIES, n // 2 + 1))

        def projected(k, n):
            if n < 8:
                return qT[:, k, n, :]
            if n < 16:
                return kT[:, k, n - 8, :]
            return v[:, k, (n - 16) // 2, N * (n % 2):N * (n % 2 + 1)]

        def proj_bank(n):
            return bank(PROJ_BANK + n % 3)[:, 0:NS] if n < 8 else bank(PROJ_BANK + n % 3)

        with nc.Block() as block:

            @block.tensor
            def _(pe):
                pe.wait_ge(m.loaded_latent, m.loaded_latent_all)

                def turn_inputs(step):
                    pe.wait_ge(ln.normed, count(step, 2 * NORMS, 2 * NORMS))
                    copied(pe, step, -3)
                    for n, src in enumerate((cn, lat)):
                        for t in range(2):
                            mm = pe.transpose(bank(PROJ_BANK)[:, NS * n + P * t:NS * n + P * t + P], src[:, t, :],
                                              w["ident"][:])
                    mm.then_inc(kv_turned, 1)

                def projections(step, which):
                    for n in which:
                        if n == 0:
                            pe.wait_ge(kv_ready, count(step, 2, 2))
                        copied(pe, step, n - 3)
                        if n < 8:
                            lhsT, rhs = w["xq"][:, P * n:P * n + P], kvT[:, :, SEQ:]
                        elif n < 16:
                            lhsT, rhs = w["xk"][:, P * (n - 8):P * (n - 7)], kvT[:]
                        else:
                            lhsT, rhs = kvT[:, (n - 16) // 2, :], w["xv"][:, N * (n % 2):N * (n % 2 + 1)]
                        pe.matmul(proj_bank(n), lhsT, rhs, start=True, stop=True).then_inc(proj_done, 1)

                def score(k, u):
                    t, half, par = unit(u)
                    rows = slice(DHX * par, DHX * par + DHX)
                    for n in range(UH):
                        for b in range(2):
                            seq = 2 * t + b
                            mm = pe.matmul(bank(par)[SEQ * b:SEQ * b + SEQ, KEYS * n:KEYS * (n + 1)],
                                           qT[rows, k, UH * half + n, SEQ * seq:SEQ * seq + SEQ],
                                           kT[rows, k, UH * half + n, KEYS * seq:KEYS * (seq + 1)], start=True, stop=True)
                    mm.then_inc(scores_done, 1)

                def turn(step, u):
                    reach(pe, probs_ready, count(step, UNITS, u + 1))
                    reach(pe, probsT_ready, count(step, UNITS, u))
                    for n in range(UH):
                        mm = pe.transpose(bank(TURN_BANK)[:, P * n:P * n + P], probs[:, u % 4, n, :], w["ident"][:])
                    mm.then_inc(probs_turned, 1)

                def attend(step, k, u):
                    t, half, par = unit(u)
                    pe.wait_ge(probsT_ready, count(step, UNITS, u + 1))
                    if par == 0:
                        reach(pe, attn_ready, count(step, UNITS // 2, u // 2))
                    for n in range(UH):
                        head = 2 * (UH * half + n) + par
                        for b in range(2):
                            mm = pe.matmul(bank(ATTN_BANK)[DHX * par:DHX * par + DHX, P * n + SEQ * b:P * n + SEQ * (b + 1)],
                                           v[:, k, 2 * t + b, DHX * head:DHX * (head + 1)],
                                           probsT[:, u % 2, n, SEQ * b:SEQ * b + SEQ], start=True, stop=True)
                    mm.then_inc(attn_done, 1)

                def project(step, t):
                    pe.wait_ge(attn_ready, count(step, UNITS // 2, 2 * t + 2))
                    if t == 0:
                        reach(pe, x_added, count(step, 1, 0))
                    for hp in range(HP):
                        mm = pe.matmul(bank(OUT_BANK)[:, P * t:P * t + P], attnT[:, t, hp, :], w["xo"][:, hp, :],
                                       start=(hp == 0), stop=(hp == HP - 1))
                    mm.then_inc(out_done, 1)

                def body(step, k, ahead):
                    for s in range(UNITS if ahead >= 0 else 4):
                        here, before = ahead >= 0, not is_first(step)
                        if s == 7 and ahead >= 2:
                            turn_inputs(later(step, 2))
                        if ahead >= 1:
                            projections(later(step, 1), PROJ_SLOTS[s])
                        if s == 0 and here:
                            copied(pe, step, 14)
                            copied(pe, step, 15)
                        if here and s >= 2 or before and s < 2:
                            turn(step, s - 2)
                        if here:
                            score(k, s)
                        if s == 3 and here:
                            copied(pe, step, 22)
                            copied(pe, step, 23)
                        if here and s >= 3 or before and s < 3:
                            attend(step, k if s >= 3 else 1 - k, s - 3)
                        if s == 3 and before:
                            project(later(step, -1), 1)
                        if s == 7:
                            project(step, 0)

                turn_inputs(step_of(0, 0))
                projections(step_of(0, 0), range(PROJ))
                turn_inputs(step_of(0, 1))
                run_steps(pe, STEPS, body)

            @block.scalar
            def _(act):
                act.wait_ge(m.loaded_latent, m.loaded_latent_all)

                def inputs(step):
                    act.wait_ge(kv_turned, count(step, 1, 1))
                    for n in range(2):
                        act.activation(kvT[:, :, SEQ * n:SEQ * n + SEQ],
                                       seqs_of(bank(PROJ_BANK)[:, NS * n:NS * n + NS]), ACT.Identity,
                                       bias=w["x_affine"][:, 2 * n + 1:2 * n + 2], scale=w["x_affine"][:, 2 * n:2 * n + 1])\
                            .then_inc(kv_ready, 1)

                def copies(step, k, which):
                    for n in which:
                        if n % 2 == 0:
                            act.wait_ge(proj_done, count(step, PROJ, n + 1))
                            act.activation(projected(k, n), proj_bank(n), ACT.Copy).then_inc(proj_even, 1)

                def body(step, k, ahead):
                    for s in range(UNITS if ahead >= 0 else 4):
                        here, before = ahead >= 0, not is_first(step)
                        if s == 7 and ahead >= 2:
                            inputs(later(step, 2))
                        if ahead >= 1:
                            copies(later(step, 1), 1 - k, PROJ_SLOTS[s])
                        if here and s >= 2 or before and s < 2:
                            u = s - 2
                            act.wait_ge(probs_turned, count(step, UNITS, u + 1))
                            reach(act, attn_done, count(step, UNITS, u - 1))
                            act.activation(probsT[:, u % 2].rearrange("p a n -> p (a n)"), bank(TURN_BANK), ACT.Copy)\
                                .then_inc(probsT_ready, 1)
                        u = s - 3
                        if u % 2 and (here and s >= 3 or before and s < 3):
                            t, half, _ = unit(u)
                            act.wait_ge(attn_done, count(step, UNITS, u + 1))
                            if half == 0:
                                reach(act, out_done, count(later(step, 0 if u >= 0 else -1), 2, t - 1))
                            act.activation(attnT[:, t, UH * half:UH * half + UH, :], tiles_of(bank(ATTN_BANK)), ACT.Copy)\
                                .then_inc(attn_ready, 1)
                        if here:
                            act.wait_ge(less_top, count(step, UNITS, s + 1))
                            act.activation(probs[:, s % 4], probs[:, s % 4], ACT.Exp, scale=DHX ** -0.5)\
                                .then_inc(exp_ready, 1)

                inputs(step_of(0, 0))
                copies(step_of(0, 0), 0, range(PROJ))
                inputs(step_of(0, 1))
                run_steps(act, STEPS, body)

            @block.gpsimd
            def _(pool):
                def body(step, k, ahead):
                    for s in range(UNITS if ahead >= 0 else 1):
                        if s >= 1 or not is_first(step):
                            u = s - 1
                            pool.wait_ge(inverse_ready, count(step, UNITS, u + 1))
                            pool.tensor_tensor(probs[:, u % 4], probs[:, u % 4], over(total[:, u % 4], 2, KEYS),
                                               ALU.mult).then_inc(probs_ready, 1)
                        if ahead >= 2 and s in (0, 1, 3):
                            norm_root(pool, m, later(step, 2), ln, NORMS, (0, 1, None, 2)[s])

                for first in range(2):
                    for n in range(NORMS):
                        norm_root(pool, m, step_of(0, first), ln, NORMS, n)
                run_steps(pool, STEPS, body)

            @block.vector
            def _(dve):
                dve.wait_ge(m.loaded_ctx, 16)

                def normed(step, part):
                    def row(x):
                        return lambda t: x[:, bass.ds(count(step, 2, t), 1), :]

                    if part == 1:
                        reach(dve, kv_turned, count(step, 1, 0))
                        norm_apply(dve, m, step, row(m.C), lambda t: cn[:, t, :], ln, NORMS, 0)
                    if part == 2:
                        norm_apply(dve, m, step, row(m.X), lambda t: xn[:, t, :], ln, NORMS, 1)
                    if part == 4:
                        norm_apply(dve, m, step, lambda t: xn[:, t, :], lambda t: lat[:, t, :], ln, NORMS, 2)
                    if part == 0:
                        norm_stats(dve, m, step, row(m.C), ln, NORMS, 0)
                    if part == 1:
                        norm_stats(dve, m, step, row(m.X), ln, NORMS, 1)
                    if part == 3:
                        dve.wait_ge(ln.normed, count(step, 2 * NORMS, 4))
                        norm_stats(dve, m, step, lambda t: xn[:, t, :], ln, NORMS, 2)

                def copies(step, k, which):
                    for n in which:
                        if n % 2:
                            dve.wait_ge(proj_done, count(step, PROJ, n + 1))
                            dve.tensor_copy(projected(k, n), proj_bank(n)).then_inc(proj_odd, 1)

                def body(step, k, ahead):
                    for s in range(UNITS if ahead >= 0 else 5):
                        here, before = ahead >= 0, not is_first(step)
                        if ahead >= 1:
                            copies(later(step, 1), 1 - k, PROJ_SLOTS[s])
                        if here and s >= 1 or before and s < 1:
                            u = s - 1
                            dve.wait_ge(exp_ready, count(step, UNITS, u + 1))
                            dve.tensor_reduce(total[:, u % 4], probs[:, u % 4], AX.X, ALU.add).then_inc(sum_ready, 1)
                            dve.wait_ge(sum_ready, count(step, UNITS, u + 1))
                            dve.reciprocal(total[:, u % 4], total[:, u % 4]).then_inc(inverse_ready, 1)
                        if here:
                            scores = bank(s % 2).rearrange("p (h k) -> p h k", k=KEYS)
                            dve.wait_ge(scores_done, count(step, UNITS, s + 1))
                            dve.tensor_reduce(top[:, s % 4], scores, AX.X, ALU.max).then_inc(top_ready, 1)
                            reach(dve, probs_turned, count(step, UNITS, s - 3))
                            dve.wait_ge(top_ready, count(step, UNITS, s + 1))
                            dve.tensor_tensor(probs[:, s % 4], scores, over(top[:, s % 4], 2, KEYS), ALU.subtract)\
                                .then_inc(less_top, 1)
                        if s == 4 and before:
                            dve.wait_ge(out_done, count(step, 2, 0))
                            rows = m.X[:, bass.ds(count(step, 2, -2), 2), :]
                            dve.tensor_tensor(rows, bank(OUT_BANK)[:, 0:NS].rearrange("p (t n) -> p t n", n=P), rows,
                                              ALU.add).then_inc(x_added, 1)
                        if ahead >= 2 and s < 5:
                            normed(later(step, 2), s)

                for first in range(2):
                    for part in range(5):
                        normed(step_of(0, first), part)
                copies(step_of(0, 0), 0, range(PROJ))
                run_steps(dve, STEPS, body)
                dve.wait_ge(x_added, STEPS)

def routed_experts(nc, m):
    with ExitStack() as ctx:
        m.expert_weights = ctx.enter_context(nc.sbuf_tensor("expert_weights", [P, 2, 3 * FR * P], F32))
        m.expert_loaded = [stage_semaphore(nc, m, "expert_loaded_" + name) for name in ("even", "odd")]
        route_and_share(nc, m)
        run_experts(nc, m)


def load_weights(sp, m, e, k):
    sp.dma_start(m.expert_weights[:, k, :], m.dram["experts"][bass.ds(e, 1)].rearrange("e p n -> p (e n)"))\
        .then_inc(m.expert_loaded[k], 16)


def route_and_share(nc, m):
    w = m.w
    PAIRS = 2 * GT
    ROUTE = 31
    with ExitStack() as ctx:
        def sb(name, shape, dtype=F32):
            return ctx.enter_context(nc.sbuf_tensor("rt_" + name, shape, dtype))

        def sem(name):
            return stage_semaphore(nc, m, "rt_" + name)

        xn = sb("xn", [P, 2, GT, D])
        square = sb("square", [P, GT, D])
        square_sum = sb("square_sum", [P, GT])
        mean_square = sb("mean_square", [P, GT])
        inverse_rms = sb("inverse_rms", [P, GT])
        xT = sb("xT", [P, N])
        prob = sb("prob", [P, GT, E1])
        top = sb("top", [P, GT])
        ranked = sb("ranked", [P, GT, E1])
        index = sb("index", [P, GT, E1], U32)
        pick = sb("pick", [P, 2, GT])
        chosen = sb("chosen", [P, PAIRS, E1])
        mask = sb("mask", [P, GT, E1])
        before = sb("before", [P, E1])
        rank = sb("rank", [P, GT, E1])
        slot_of = sb("slot_of", [P, GT, E1])
        pair_rank = sb("pair_rank", [P, PAIRS, E1])
        pair_slot = sb("pair_slot", [P, PAIRS, E1])
        rank8 = sb("rank8", [P, PAIRS])
        slot8 = sb("slot8", [P, PAIRS])
        slot_index = sb("slot_index", [P, PAIRS], U32)
        silu = sb("silu", [P, 3, N])
        mid = sb("mid", [P, FS, N])
        bank = m.bank
        DOWN_BANK, ROUTE_BANK, GATE_BANK, UP_BANK = 0, 1, 2, 3
        RANKS = slice(GT * E1, (2 * GT + 1) * E1)

        ln = NormSemaphores(sem, "ln")
        cleared = sem("cleared")
        xT_turned = sem("xT_turned")
        xT_ready = sem("xT_ready")
        squared = sem("squared")
        mean_ready = sem("mean_ready")
        rms_ready = sem("rms_ready")
        logits_done = sem("logits_done")
        routed = sem("routed")
        exp_ready = sem("exp_ready")
        rank_done = sem("rank_done")
        scattered = sem("scattered")
        gate_up_done = sem("gate_up_done")
        silu_ready = sem("silu_ready")
        mid_ready = sem("mid_ready")
        shared_done = sem("shared_done")
        shared_added = sem("shared_added")

        with nc.Block() as block:

            @block.sync
            def _(sp):
                sp.dma_start(m.biased_weights[:], m.dram["biased"]).then_inc(m.loaded_biased, 16)
                sp.dma_start(m.top_weights[:], m.dram["top"]).then_inc(m.loaded_top, 16)
                for e in range(2):
                    load_weights(sp, m, e, e)

            @block.tensor
            def _(pe):
                pe.wait_ge(m.loaded_shared, 16)

                def turn_rows(a, k):
                    pe.wait_ge(ln.normed, count(a, GT, GT))
                    reach(pe, mid_ready, count(a, FS, -2))
                    for t in range(GT):
                        mm = pe.transpose(bank(GATE_BANK + 4)[:, P * t:P * t + P], xn[:, k, t, :], w["ident"][:])
                    mm.then_inc(xT_turned, 1)

                def logits(a):
                    pe.wait_ge(xT_ready, count(a, 1, 1))
                    reach(pe, routed, count(a, ROUTE, 23 - ROUTE))
                    for t in range(GT):
                        mm = pe.matmul(bank(ROUTE_BANK)[:, E1 * t:E1 * t + E1], xT[:, P * t:P * t + P], w["router"][:],
                                       start=True, stop=True)
                    mm.then_inc(logits_done, 1)

                def ranks(g):
                    pe.wait_ge(routed, count(g, ROUTE, 20))
                    for t in range(GT + 1):
                        out = bank(ROUTE_BANK)[:, RANKS][:, E1 * t:E1 * t + E1]
                        for s in range(min(t + 1, GT)):
                            mm = pe.matmul(out, (w["earlier"] if s == t else w["ones"])[:], mask[:, s, :],
                                           start=(s == 0), stop=(s == min(t, GT - 1)))
                    mm.then_inc(rank_done, 1)

                def down(g, tiles):
                    for t in tiles:
                        for f in range(FS):
                            if t == 0:
                                if f == 0:
                                    reach(pe, shared_added, count(g, 1, 0))
                                pe.wait_ge(mid_ready, count(g, FS, f + 1))
                            mm = pe.matmul(bank(DOWN_BANK)[:, P * t:P * t + P], mid[:, f, P * t:P * t + P], w["sd"][:, f, :],
                                           start=(f == 0), stop=(f == FS - 1))
                    if t == GT - 1:
                        mm.then_inc(shared_done, 1)

                def body(g, k, ahead):
                    if ahead < 0:
                        return
                    for f in range(FS):
                        reach(pe, mid_ready, count(g, FS, f - 2))
                        pe.matmul(bank(GATE_BANK + 2 * (f % 3)), w["sg"][:, f, :], xT[:], start=True, stop=True)
                        pe.matmul(bank(UP_BANK + 2 * (f % 3)), w["su"][:, f, :], xT[:], start=True, stop=True)\
                            .then_inc(gate_up_done, 1)
                        if f == 4:
                            ranks(g)
                    if ahead >= 1:
                        turn_rows(later(g, 1), 1 - k)
                    down(g, (0, 1))
                    if ahead >= 1:
                        logits(later(g, 1))
                    down(g, (2, 3))

                turn_rows(step_of(0, 0), 0)
                logits(step_of(0, 0))
                run_steps(pe, GROUPS, body)

            @block.scalar
            def _(act):
                def squares(a, k):
                    act.wait_ge(ln.normed, count(a, GT, GT))
                    for t in range(GT):
                        act.activation(square[:, t, :], xn[:, k, t, :], ACT.Square, accum_out=square_sum[:, t:t + 1])\
                            .then_inc(squared, 1)

                def rows(a):
                    act.wait_ge(xT_turned, count(a, 1, 1))
                    act.activation(xT[:], bank(GATE_BANK + 4), ACT.Copy).then_inc(xT_ready, 1)

                def exp(a):
                    act.wait_ge(routed, count(a, ROUTE, 3))
                    act.activation(prob[:], prob[:], ACT.Exp).then_inc(exp_ready, 1)

                def body(g, k, ahead):
                    if ahead < 0:
                        return
                    for f in range(FS):
                        act.wait_ge(gate_up_done, count(g, FS, f + 1))
                        reach(act, mid_ready, count(g, FS, f - 2))
                        act.activation(silu[:, f % 3, :], bank(GATE_BANK + 2 * (f % 3)), ACT.Silu).then_inc(silu_ready, 1)
                        if f == 5 and ahead >= 1:
                            squares(later(g, 1), 1 - k)
                    if ahead >= 1:
                        rows(later(g, 1))
                        exp(later(g, 1))

                squares(step_of(0, 0), 0)
                rows(step_of(0, 0))
                exp(step_of(0, 0))
                run_steps(act, GROUPS, body)

            @block.gpsimd
            def _(pool):
                def root_mean_square(a):
                    pool.wait_ge(mean_ready, count(a, 1, 1))
                    pool.tensor_tensor(inverse_rms[:], mean_square[:], m.minus_half[:], ALU.pow).then_inc(rms_ready, 1)

                def body(g, k, ahead):
                    if ahead < 0:
                        return
                    if ahead >= 1:
                        norm_root(pool, m, later(g, 1), ln, 1, 0, GT)
                    pool.wait_ge(routed, count(g, ROUTE, 30))
                    pool.tensor_tensor(m.pool_spare[:, 0, :], m.minus_half[:], m.minus_half[:], ALU.add)
                    for n in range(PAIRS):
                        pool.indirect_dma_start(
                            out=m.slot_rows, out_offset=bass.IndirectOffsetOnAxis(ap=slot_index[:, n:n + 1], axis=0),
                            in_=xn[:, k, n % GT, :], in_offset=None, bounds_check=SLOTS - 1, oob_is_err=False)\
                            .then_inc(scattered, 16)
                    if ahead >= 1:
                        root_mean_square(later(g, 1))

                pool.memset(before[:], 0.0).then_inc(cleared, 1)
                pool.wait_ge(m.slots_cleared, 32)
                norm_root(pool, m, step_of(0, 0), ln, 1, 0, GT)
                root_mean_square(step_of(0, 0))
                run_steps(pool, GROUPS, body)

            @block.vector
            def _(dve):
                def row(step):
                    return lambda t: m.X[:, bass.ds(count(step, GT, t), 1), :]

                def norm(a, k):
                    reach(dve, scattered, count(a, 16 * PAIRS, -16 * PAIRS))
                    norm_apply(dve, m, a, row(a), lambda t: xn[:, k, t, :], ln, 1, 0, GT)

                def pick_experts(a):
                    dve.wait_ge(squared, count(a, GT, GT))
                    dve.tensor_scalar(mean_square[:], square_sum[:], 1.0 / D, RMS_EPS, ALU.mult, ALU.add)\
                        .then_inc(mean_ready, 1)
                    dve.wait_ge(logits_done, count(a, 1, 1))
                    dve.wait_ge(rms_ready, count(a, 1, 1))
                    lg = bank(ROUTE_BANK)[:, 0:GT * E1].rearrange("p (t e) -> p t e", e=E1)
                    dve.tensor_tensor(prob[:], lg, over(inverse_rms[:], 2, E1), ALU.mult).then_inc(routed, 1)
                    dve.wait_ge(routed, count(a, ROUTE, 1))
                    dve.tensor_reduce(top[:], prob[:], AX.X, ALU.max).then_inc(routed, 1)
                    dve.wait_ge(routed, count(a, ROUTE, 2))
                    dve.tensor_tensor(prob[:], prob[:], over(top[:], 2, E1), ALU.subtract).then_inc(routed, 1)
                    dve.wait_ge(exp_ready, count(a, 1, 1))
                    dve.tensor_reduce(top[:], prob[:], AX.X, ALU.add).then_inc(routed, 1)
                    dve.wait_ge(routed, count(a, ROUTE, 4))
                    dve.reciprocal(top[:], top[:]).then_inc(routed, 1)
                    dve.wait_ge(routed, count(a, ROUTE, 5))
                    dve.tensor_tensor(prob[:], prob[:], over(top[:], 2, E1), ALU.mult).then_inc(routed, 1)
                    dve.wait_ge(routed, count(a, ROUTE, 6))
                    dve.memset(m.spare[:], 0.0)
                    for t in range(GT):
                        dve.max(ranked[:, t, :], prob[:, t, :]).then_inc(routed, 1)
                    dve.wait_ge(routed, count(a, ROUTE, 10))
                    dve.memset(m.spare[:], 0.0)
                    for t in range(GT):
                        dve.max_index(index[:, t, :], ranked[:, t, :], prob[:, t, :]).then_inc(routed, 1)
                    dve.tensor_tensor(top[:], ranked[:, :, 0], ranked[:, :, 1], ALU.add).then_inc(routed, 1)
                    dve.wait_ge(routed, count(a, ROUTE, 15))
                    dve.reciprocal(top[:], top[:]).then_inc(routed, 1)
                    dve.wait_ge(routed, count(a, ROUTE, 16))
                    dve.tensor_tensor(m.pair_weights[:, :, bass.ds(count(a, GT, 0), GT)],
                                      ranked[:, :, 0:2].rearrange("p t j -> p j t"), over(top[:], 1, 2), ALU.mult)\
                        .then_inc(routed, 1)
                    dve.tensor_copy(pick[:], index[:, :, 0:2].rearrange("p t j -> p j t")).then_inc(routed, 1)
                    dve.wait_ge(routed, count(a, ROUTE, 18))
                    dve.tensor_tensor(chosen[:], over(w["expert_ids"][:], 1, PAIRS),
                                      over(pick[:].rearrange("p j t -> p (j t)"), 2, E1), ALU.is_equal).then_inc(routed, 1)
                    dve.wait_ge(routed, count(a, ROUTE, 19))
                    dve.tensor_tensor(mask[:], chosen[:, 0:GT, :], chosen[:, GT:PAIRS, :], ALU.add).then_inc(routed, 1)

                def place_rows(a):
                    dve.wait_ge(rank_done, count(a, 1, 1))
                    counted = bank(ROUTE_BANK)[:, RANKS].rearrange("p (t e) -> p t e", e=E1)
                    dve.tensor_tensor(rank[:], counted[:, 0:GT, :], over(before[:], 1, GT), ALU.add).then_inc(routed, 1)
                    dve.wait_ge(routed, count(a, ROUTE, 21))
                    dve.tensor_tensor(slot_of[:], rank[:], over(w["expert_base"][:], 1, GT), ALU.add).then_inc(routed, 1)
                    dve.tensor_tensor(before[:], counted[:, GT, :], before[:], ALU.add).then_inc(routed, 1)
                    dve.wait_ge(routed, count(a, ROUTE, 22))
                    for values, out in ((slot_of, pair_slot), (rank, pair_rank)):
                        for j in range(2):
                            ins = dve.tensor_tensor(out[:, GT * j:GT * j + GT, :], chosen[:, GT * j:GT * j + GT, :],
                                                    values[:], ALU.mult)
                        ins.then_inc(routed, 1)
                    dve.wait_ge(routed, count(a, ROUTE, 25))
                    dve.tensor_reduce(slot8[:], pair_slot[:], AX.X, ALU.add).then_inc(routed, 1)
                    dve.tensor_reduce(rank8[:], pair_rank[:], AX.X, ALU.add).then_inc(routed, 1)
                    dve.wait_ge(routed, count(a, ROUTE, 27))
                    dve.tensor_scalar(rank8[:], rank8[:], float(CAP), float(4 * SLOTS), ALU.is_ge, ALU.mult)\
                        .then_inc(routed, 1)
                    dve.wait_ge(routed, count(a, ROUTE, 28))
                    dve.tensor_tensor(slot8[:], slot8[:], rank8[:], ALU.add).then_inc(routed, 1)
                    dve.wait_ge(routed, count(a, ROUTE, 29))
                    reach(dve, scattered, count(a, 16 * PAIRS, 0))
                    dve.tensor_copy(slot_index[:], slot8[:]).then_inc(routed, 1)
                    dve.tensor_scalar(m.pair_slots[:, :, bass.ds(count(a, GT, 0), GT)],
                                      slot8[:].rearrange("p (j t) -> p j t", j=2), float(SLOTS), None, ALU.min)\
                        .then_inc(routed, 1)

                def shared(g, f):
                    dve.wait_ge(silu_ready, count(g, FS, f + 1))
                    dve.tensor_tensor(mid[:, f, :], bank(UP_BANK + 2 * (f % 3)), silu[:, f % 3, :], ALU.mult)\
                        .then_inc(mid_ready, 1)

                def body(g, k, ahead):
                    if ahead < 0:
                        return
                    for f in range(FS):
                        shared(g, f)
                        if f == 2 and ahead >= 1:
                            norm_stats(dve, m, later(g, 1), row(later(g, 1)), ln, 1, 0, GT)
                        if f == 3 and ahead >= 1:
                            norm(later(g, 1), 1 - k)
                        if f == 5:
                            place_rows(g)
                    if ahead >= 1:
                        pick_experts(later(g, 1))
                    dve.wait_ge(shared_done, count(g, 1, 1))
                    rows = m.X[:, bass.ds(count(g, GT, 0), GT), :]
                    dve.tensor_tensor(rows, tiles_of(bank(DOWN_BANK)), rows, ALU.add).then_inc(shared_added, 1)

                dve.wait_ge(cleared, 1)
                norm_stats(dve, m, step_of(0, 0), row(step_of(0, 0)), ln, 1, 0, GT)
                norm(step_of(0, 0), 0)
                pick_experts(step_of(0, 0))
                run_steps(dve, GROUPS, body)
                dve.wait_ge(shared_added, GROUPS)
                dve.wait_ge(routed, ROUTE * GROUPS)
                dve.wait_ge(scattered, 16 * PAIRS * GROUPS)


def run_experts(nc, m):
    HALF = CAP // 2
    UNITS = 2 * FR
    w = m.w
    with ExitStack() as ctx:
        def sb(name, shape):
            return ctx.enter_context(nc.sbuf_tensor("ex_" + name, shape, F32))

        def sem(name):
            return stage_semaphore(nc, m, "ex_" + name)

        gate_w, up_w, down_w = (m.expert_weights[:, :, FR * P * n:FR * P * (n + 1)].rearrange("p k (f c) -> p k f c", c=P)
                                for n in range(3))
        rows = sb("rows", [P, 2, CT, D])
        xT = sb("xT", [P, CAP])
        silu = sb("silu", [P, 3, HALF])
        mid = sb("mid", [P, FR, CAP])
        result = sb("result", [P, 2, CT, D])
        bank = m.bank
        DOWN_BANK, GATE_BANK, UP_BANK, ROWS_BANK = 0, 2, 3, 6

        loaded = m.expert_loaded
        turned = sem("turned")
        xT_ready = sem("xT_ready")
        gate_up_done = sem("gate_up_done")
        silu_ready = sem("silu_ready")
        mid_ready = sem("mid_ready")
        down_done = sem("down_done")
        result_ready = sem("result_ready")
        stored = [sem("stored_even"), sem("stored_odd")]

        def slots_of(first):
            return m.ps[:, first:first + 2, :].rearrange("p a n -> p (a n)")[:, 0:CAP]

        with nc.Block() as block:

            @block.sync
            def _(sp):
                def load_rows(e, k):
                    sp.dma_start(rows[:, k], slot_tiles(m.slot_rows, e)).then_inc(loaded[k], 16)

                def store(e, k, results):
                    sp.wait_ge(result_ready, results)
                    sp.dma_start(slot_tiles(m.result_rows[0:SLOTS], e), result[:, k]).then_inc(stored[k], 16)

                for e in range(2):
                    load_rows(e, e)
                with sp.Fori(0, E1 // 2 - 1) as i:
                    for k in range(2):
                        store(2 * i + k, k, 2 * i + k + 1)
                        sp.wait_ge(stored[k], 16 * (i + 1))
                        load_rows(2 * i + k + 2, k)
                        load_weights(sp, m, 2 * i + k + 2, k)
                for k in range(2):
                    store(E1 - 2 + k, k, E1 - 1 + k)
                for k in range(2):
                    sp.wait_ge(stored[k], 16 * (E1 // 2))

            @block.tensor
            def _(pe):
                def turn_rows(e, k):
                    pe.wait_ge(loaded[k], count(e, 16, 32 - 16 * k))
                    reach(pe, mid_ready, count(e, UNITS, -2))
                    for c in range(CT):
                        mm = pe.transpose(bank(ROWS_BANK + c // GT)[:, P * (c % GT):P * (c % GT) + P], rows[:, k, c, :],
                                          w["ident"][:])
                    mm.then_inc(turned, 1)

                def body(e, k, ahead):
                    if ahead < 0:
                        return
                    pe.wait_ge(xT_ready, count(e, 1, 1))
                    for n in range(UNITS):
                        f, half = n // 2, n % 2
                        if n != 2:
                            reach(pe, mid_ready, count(e, UNITS, n - 2 if n > 2 else n - 1))
                        for buf, first in ((gate_w, GATE_BANK), (up_w, UP_BANK)):
                            mm = pe.matmul(bank(first + 2 * (n % 3))[:, 0:HALF], buf[:, k, f, :],
                                           xT[:, HALF * half:HALF * half + HALF], start=True, stop=True)
                        mm.then_inc(gate_up_done, 1)
                    if ahead >= 1:
                        turn_rows(later(e, 1), 1 - k)
                    reach(pe, result_ready, count(e, 1, 0))
                    for c in range(CT):
                        if c in (0, 2):
                            pe.wait_ge(mid_ready, count(e, UNITS, UNITS - 1 + c // 2))
                        for f in range(FR):
                            mm = pe.matmul(bank(DOWN_BANK + c // GT)[:, P * (c % GT):P * (c % GT) + P],
                                           mid[:, f, P * c:P * c + P], down_w[:, k, f, :],
                                           start=(f == 0), stop=(f == FR - 1))
                    mm.then_inc(down_done, 1)

                turn_rows(step_of(0, 0), 0)
                run_steps(pe, E1, body)

            @block.scalar
            def _(act):
                def rows_turned(e):
                    act.wait_ge(turned, count(e, 1, 1))
                    act.activation(xT[:], slots_of(ROWS_BANK), ACT.Copy).then_inc(xT_ready, 1)

                def body(e, k, ahead):
                    if ahead < 0:
                        return
                    for n in range(UNITS):
                        act.wait_ge(gate_up_done, count(e, UNITS, n + 1))
                        reach(act, mid_ready, count(e, UNITS, n - 2 if n > 2 else 0))
                        act.activation(silu[:, n % 3, :], bank(GATE_BANK + 2 * (n % 3))[:, 0:HALF], ACT.Silu)\
                            .then_inc(silu_ready, 1)
                    if ahead >= 1:
                        rows_turned(later(e, 1))
                    act.wait_ge(down_done, count(e, 1, 1))
                    act.activation(result[:, k].rearrange("p c d -> p (c d)"), slots_of(DOWN_BANK), ACT.Copy)\
                        .then_inc(result_ready, 1)

                rows_turned(step_of(0, 0))
                run_steps(act, E1, body)

            @block.vector
            def _(dve):
                def body(e, k, ahead):
                    if ahead < 0:
                        return
                    for n in range(UNITS):
                        f, half = n // 2, n % 2
                        dve.wait_ge(silu_ready, count(e, UNITS, n + 1))
                        dve.tensor_tensor(mid[:, f, HALF * half:HALF * half + HALF], bank(UP_BANK + 2 * (n % 3))[:, 0:HALF],
                                          silu[:, n % 3, :], ALU.mult).then_inc(mid_ready, 1)

                run_steps(dve, E1, body)


def slot_tiles(rows, e):
    return rows.rearrange("(e c p) d -> e p c d", c=CT, p=P)[bass.ds(e, 1)].rearrange("e p c d -> p (e c) d")

def causal_attention(nc, m):
    w = m.w
    STEPS = TILES // 2
    NS = 2 * P
    UNITS = NS // SEQ
    PAIRS = 2 * 2
    DEPTH = 4
    BUCKETS = 32
    J = H // 4
    FJ = D // J
    with ExitStack() as ctx:
        def sb(name, shape):
            return ctx.enter_context(nc.sbuf_tensor("ca_" + name, shape, F32))

        def sem(name):
            return stage_semaphore(nc, m, "ca_" + name)

        got = sb("got", [P, 2, PAIRS, D])
        weight = sb("weight", [P, 2, PAIRS])
        slot = ctx.enter_context(nc.sbuf_tensor("ca_slot", [P, 2, PAIRS], U32))
        xn = sb("xn", [P, 2, D])
        hT = sb("hT", [P, 2, NS])
        qbias = sb("qbias", [P, 2])
        qpar = sb("qpar", [P, 2, UNITS, 2, SEQ])
        kT = sb("kT", [P, NS])
        kpairs = sb("kpairs", [P, 2, UNITS, HP * SEQ])
        vheads = sb("vheads", [P, 2, UNITS, 2, J, FJ])
        probs = sb("probs", [P, UNITS, HP, SEQ])
        probsT = sb("probsT", [P, 2, J, P])
        top = sb("top", [P, UNITS, HP])
        total = sb("total", [P, UNITS, HP])
        attnT = sb("attnT", [P, NS])
        bank = m.bank
        TURN_BANK, ATTN_BANK, IN_BANK, OUT_BANK, QK_BANK, V_BANK = 2, 3, 4, 5, 6, 7

        ln = NormSemaphores(sem, "ln")
        bias_done = sem("bias_done")
        bias_copied = sem("bias_copied")
        slot_ready = sem("slot_ready")
        weight_ready = sem("weight_ready")
        gathered = [sem("gathered_even"), sem("gathered_odd")]
        combined = sem("combined")
        zeroed = sem("zeroed")
        qbias_ready = sem("qbias_ready")
        hT_turned = sem("hT_turned")
        hT_ready = sem("hT_ready")
        qk_done = sem("qk_done")
        q_ready = sem("q_ready")
        k_ready = sem("k_ready")
        kpairs_ready = sem("kpairs_ready")
        v_done = sem("v_done")
        v_ready = sem("v_ready")
        scores_done = sem("scores_done")
        masked = sem("masked")
        top_ready = sem("top_ready")
        less_top = sem("less_top")
        exp_ready = sem("exp_ready")
        sum_ready = sem("sum_ready")
        inverse_ready = sem("inverse_ready")
        probs_ready = sem("probs_ready")
        probs_turned = sem("probs_turned")
        probsT_ready = sem("probsT_ready")
        attn_done = sem("attn_done")
        attn_ready = sem("attn_ready")
        out_done = sem("out_done")
        x_added = sem("x_added")

        def present(step, ahead, u):
            return ahead >= 0 if u >= 0 else not is_first(step)

        with nc.Block() as block:

            @block.tensor
            def _(pe):
                pe.wait_ge(m.loaded_causal, 16)

                def turn_rows(step, k):
                    pe.wait_ge(ln.normed, count(step, 2, 2))
                    reach(pe, hT_ready, count(step, 1, 0))
                    for t in range(2):
                        mm = pe.transpose(bank(IN_BANK)[:, P * t:P * t + P], xn[:, t, :], w["ident"][:])
                    mm.then_inc(hT_turned, 1)

                def project_qk(step, k):
                    pe.wait_ge(hT_ready, count(step, 1, 1))
                    reach(pe, q_ready, count(step, 2, 0))
                    reach(pe, k_ready, count(step, 1, 0))
                    for n in range(2):
                        mm = pe.matmul(bank(QK_BANK)[:, NS * n:NS * n + NS], w["cqk"][:, n, :], hT[:, k, :],
                                       start=True, stop=True)
                    mm.then_inc(qk_done, 1)

                def project_v(step, k):
                    reach(pe, v_ready, count(step, 4, 0))
                    for b in range(UNITS):
                        for up in range(2):
                            mm = pe.matmul(bank(V_BANK)[SEQ * up:SEQ * up + SEQ, SEQ * b:SEQ * b + SEQ],
                                           hT[:, k, SEQ * b:SEQ * b + SEQ], w["cv"][:, up, :], start=True, stop=True)
                    mm.then_inc(v_done, 1)

                def score(step, k, u):
                    if u == 0:
                        pe.wait_ge(q_ready, count(step, 2, 2))
                    pe.wait_ge(kpairs_ready, count(step, UNITS, u + 1))
                    reach(pe, masked, count(step, UNITS, u - 1))
                    pe.matmul(bank(u % 2), qpar[:, k, u].rearrange("p a n -> p (a n)"), kpairs[:, k, u, :],
                              start=True, stop=True).then_inc(scores_done, 1)

                def turn(step, u):
                    reach(pe, probs_ready, count(step, UNITS, u + 1))
                    reach(pe, probsT_ready, count(step, UNITS, u))
                    for j in range(J):
                        mm = pe.transpose(bank(TURN_BANK)[:, P * j:P * j + P],
                                          probs[:, u % UNITS, 2 * j:2 * j + 2, :].rearrange("p a k -> p (a k)"),
                                          w["ident"][:])
                    mm.then_inc(probs_turned, 1)

                def attend(k, u):
                    seq = u % UNITS
                    for par in range(2):
                        for j in range(J):
                            mm = pe.matmul(bank(ATTN_BANK)[FJ * j:FJ * j + FJ, SEQ * seq:SEQ * seq + SEQ],
                                           vheads[:, k, seq, par, j, :], probsT[:, u % 2, j, SEQ * par:SEQ * par + SEQ],
                                           start=(par == 0), stop=(par == 1))
                    mm.then_inc(attn_done, 1)

                def project(step):
                    pe.wait_ge(attn_ready, count(step, 1, 1))
                    reach(pe, x_added, count(step, 1, 0))
                    for t in range(2):
                        out = bank(OUT_BANK)[:, P * t:P * t + P]
                        pe.matmul(out, w["ones"][0:1, :], w["bo"][0:1, :], start=True, stop=False)
                        mm = pe.matmul(out, attnT[:, P * t:P * t + P], w["co"][:], start=False, stop=True)
                    mm.then_inc(out_done, 1)

                def body(step, k, ahead):
                    for s in range(UNITS):
                        if ahead >= 0:
                            score(step, k, s)
                        if s == 0 and ahead >= 1:
                            project_qk(later(step, 1), 1 - k)
                        if s == 0 and not is_first(step):
                            reach(pe, v_ready, count(step, 4, 0))
                            reach(pe, attn_ready, count(step, 1, -1))
                        if present(step, ahead, s - 3):
                            turn(step, s - 3)
                        elif present(step, ahead, s - 4):
                            reach(pe, probsT_ready, count(step, UNITS, s - 3))
                        if present(step, ahead, s - 4):
                            attend(1 - k, s - 4)
                        if s == 1 and ahead >= 0:
                            project_v(step, k)
                        if s == 3 and ahead >= 2:
                            turn_rows(later(step, 2), k)
                        if s == 3 and not is_first(step):
                            project(later(step, -1))

                pe.wait_ge(m.loaded_biased, 32)
                for key in range(SEQ):
                    mm = pe.matmul(bank(0)[:, HP * key:HP * key + HP],
                                   w["distance"][0:2 * BUCKETS, 2 * (SEQ - 1 - key):2 * (2 * SEQ - 1 - key)],
                                   w["rel_bias"][:], start=True, stop=True)
                mm.then_inc(bias_done, 1)
                pe.wait_ge(bias_copied, 1)
                pe.matmul(bank(1), w["par_first"][:], m.bias_values[:], start=True, stop=True).then_inc(bias_done, 1)
                turn_rows(step_of(0, 0), 0)
                project_qk(step_of(0, 0), 0)
                turn_rows(step_of(0, 1), 1)
                pe.wait_ge(bias_copied, 2)
                run_steps(pe, STEPS, body, DEPTH)

            @block.scalar
            def _(act):
                act.wait_ge(m.loaded_causal, 16)
                act.wait_ge(qbias_ready, 1)

                def rows(step, k):
                    act.wait_ge(hT_turned, count(step, 1, 1))
                    act.activation(hT[:, k, :], bank(IN_BANK)[:, 0:NS], ACT.Copy).then_inc(hT_ready, 1)

                def copies(step, k):
                    act.wait_ge(qk_done, count(step, 1, 1))
                    reach(act, kpairs_ready, count(step, UNITS, 0))
                    act.activation(kT[:], bank(QK_BANK)[:, NS:], ACT.Identity, bias=w["c_bias"][:, 1:2]).then_inc(k_ready, 1)
                    for par in range(2):
                        act.activation(qpar[:, k, :, par, :], seqs_of(bank(QK_BANK)[:, 0:NS]), ACT.Identity,
                                       bias=qbias[:, par:par + 1], scale=w["parity"][:, par:par + 1]).then_inc(q_ready, 1)

                def body(step, k, ahead):
                    for s in range(UNITS):
                        if s == 0 and ahead >= 1:
                            copies(later(step, 1), 1 - k)
                        if present(step, ahead, s - 3):
                            u = s - 3
                            act.wait_ge(probs_turned, count(step, UNITS, u + 1))
                            reach(act, attn_done, count(step, UNITS, u - 1))
                            act.activation(probsT[:, u % 2].rearrange("p a n -> p (a n)"), bank(TURN_BANK), ACT.Copy)\
                                .then_inc(probsT_ready, 1)
                        if s == 3 and not is_first(step):
                            act.wait_ge(attn_done, count(step, UNITS, 0))
                            act.activation(attnT[:], bank(ATTN_BANK)[:, 0:NS], ACT.Copy).then_inc(attn_ready, 1)
                        if s == 3 and ahead >= 2:
                            rows(later(step, 2), k)
                        if ahead >= 0:
                            act.wait_ge(less_top, count(step, UNITS, s + 1))
                            act.activation(probs[:, s], probs[:, s], ACT.Exp).then_inc(exp_ready, 1)

                for n in range(2):
                    act.wait_ge(bias_done, n + 1)
                    act.activation(m.bias_values[:], bank(n), ACT.Copy).then_inc(bias_copied, 1)
                rows(step_of(0, 0), 0)
                copies(step_of(0, 0), 0)
                rows(step_of(0, 1), 1)
                run_steps(act, STEPS, body, DEPTH)

            @block.gpsimd
            def _(pool):
                def gather(k, n):
                    pool.indirect_dma_start(
                        out=got[:, k, n, :], out_offset=None, in_=m.result_rows,
                        in_offset=bass.IndirectOffsetOnAxis(ap=slot[:, k, n:n + 1], axis=0)).then_inc(gathered[k], 16)

                def spread(step, k, b):
                    pool.wait_ge(k_ready, count(step, 1, 1))
                    pool.tensor_tensor(seqs_of(kpairs[:, k, b, :]), over(kT[:, SEQ * b:SEQ * b + SEQ], 1, HP),
                                       over(w["pair_rows"][:], 2, SEQ), ALU.mult).then_inc(kpairs_ready, 1)

                def body(step, k, ahead):
                    for s in range(UNITS):
                        if present(step, ahead, s - 1):
                            u = (s - 1) % UNITS
                            pool.wait_ge(inverse_ready, count(step, UNITS, s))
                            pool.tensor_tensor(probs[:, u], probs[:, u], over(total[:, u], 2, SEQ), ALU.mult)\
                                .then_inc(probs_ready, 1)
                        if s == 0 and ahead >= 2:
                            if ahead >= 3:
                                pool.wait_ge(slot_ready, count(step, 1, 4))
                            norm_root(pool, m, later(step, 2), ln, 1, 0)
                        if ahead >= 1 and s >= 1:
                            for b in ((), (0,), (1, 2), (3,))[s]:
                                spread(later(step, 1), 1 - k, b)
                        if ahead >= 3:
                            for n in ((0, 1), (2, 3), (), ())[s]:
                                gather(1 - k, n)
                        if ahead < 0:
                            break

                for first in range(3):
                    pool.wait_ge(slot_ready, first + 1)
                    for n in range(PAIRS):
                        gather(first % 2, n)
                    if first == 1:
                        norm_root(pool, m, step_of(0, 0), ln, 1, 0)
                pool.memset(vheads[:], 0.0).then_inc(zeroed, 1)
                norm_root(pool, m, step_of(0, 1), ln, 1, 0)
                for b in range(UNITS):
                    spread(step_of(0, 0), 0, b)
                run_steps(pool, STEPS, body, DEPTH)

            @block.vector
            def _(dve):
                def row(step):
                    return lambda t: m.X[:, bass.ds(count(step, 2, t), 1), :]

                def picks(step, k):
                    reach(dve, combined, count(step, PAIRS, -PAIRS))
                    where = bass.ds(count(step, 2, 0), 2)
                    dve.tensor_copy(weight[:, k].rearrange("p (j t) -> p j t", j=2), m.pair_weights[:, :, where])\
                        .then_inc(weight_ready, 1)
                    dve.tensor_copy(slot[:, k].rearrange("p (j t) -> p j t", j=2), m.pair_slots[:, :, where])\
                        .then_inc(slot_ready, 1)

                def combine(step, k):
                    dve.wait_ge(weight_ready, count(step, 1, 1))
                    dve.wait_ge(gathered[k], count(step, 8 * PAIRS, 8 * PAIRS * (2 - k)))
                    for n in range(PAIRS):
                        if n >= 2:
                            dve.wait_ge(combined, count(step, PAIRS, n - 1))
                        out = m.X[:, bass.ds(count(step, 2, n % 2), 1), :]
                        dve.scalar_tensor_tensor(out=out, in0=got[:, k, n:n + 1, :], scalar=weight[:, k, n:n + 1], in1=out,
                                                 op0=ALU.mult, op1=ALU.add).then_inc(combined, 1)

                def normed(step):
                    reach(dve, hT_turned, count(step, 1, 0))
                    norm_apply(dve, m, step, row(step), lambda t: xn[:, t, :], ln, 1, 0)

                def spread_v(step, k):
                    dve.wait_ge(v_done, count(step, 1, 1))
                    for up in range(2):
                        part = slice(SEQ * up, SEQ * up + SEQ)
                        for par in range(2):
                            src = bank(V_BANK)[part, 0:NS].rearrange("p (b j a c) -> p b j a c", j=J, a=2, c=DH0)[:, :, :, par, :]
                            one = w["c_bv"][part].rearrange("p (j a c) -> p j a c", a=2, c=DH0)[:, :, par, :]
                            at = DH0 * (2 * up + par)
                            dve.tensor_tensor(vheads[part, k, :, par, :, at:at + DH0], src, over(one, 1, UNITS), ALU.add)\
                                .then_inc(v_ready, 1)

                def body(step, k, ahead):
                    for s in range(UNITS):
                        if ahead >= 0:
                            dve.wait_ge(scores_done, count(step, UNITS, s + 1))
                            reach(dve, probs_turned, count(step, UNITS, s - 3))
                            dve.scalar_tensor_tensor(out=probs[:, s], in0=bank(s % 2).rearrange("p (h k) -> p h k", k=SEQ),
                                                     scalar=float(DH0) ** -0.5, in1=over(w["causal_bias"][:], 1, HP),
                                                     op0=ALU.mult, op1=ALU.add).then_inc(masked, 1)
                            dve.wait_ge(masked, count(step, UNITS, s + 1))
                            dve.tensor_reduce(top[:, s], probs[:, s], AX.X, ALU.max).then_inc(top_ready, 1)
                        if present(step, ahead, s - 1) and (ahead >= 0 or s == 0):
                            u = (s - 1) % UNITS
                            dve.wait_ge(exp_ready, count(step, UNITS, s))
                            dve.tensor_reduce(total[:, u], probs[:, u], AX.X, ALU.add).then_inc(sum_ready, 1)
                            dve.wait_ge(sum_ready, count(step, UNITS, s))
                            dve.reciprocal(total[:, u], total[:, u]).then_inc(inverse_ready, 1)
                        if ahead >= 0:
                            dve.wait_ge(top_ready, count(step, UNITS, s + 1))
                            dve.tensor_tensor(probs[:, s], probs[:, s], over(top[:, s], 2, SEQ), ALU.subtract)\
                                .then_inc(less_top, 1)
                        if s == 0 and ahead >= 2:
                            dve.wait_ge(combined, count(step, PAIRS, 3 * PAIRS))
                            dve.memset(m.spare[:], 0.0)
                            norm_stats(dve, m, later(step, 2), row(later(step, 2)), ln, 1, 0)
                        if s == 1 and ahead >= 2:
                            normed(later(step, 2))
                        if s == 2 and ahead >= 0:
                            spread_v(step, k)
                        if s == 3 and ahead >= 3:
                            combine(later(step, 3), 1 - k)
                        if s == 3 and ahead >= 4:
                            picks(later(step, 4), k)
                        if s == 3 and not is_first(step):
                            dve.wait_ge(out_done, count(step, 1, 0))
                            out = m.X[:, bass.ds(count(step, 2, -2), 2), :]
                            dve.tensor_tensor(out, bank(OUT_BANK)[:, 0:NS].rearrange("p (t n) -> p t n", n=P), out, ALU.add)\
                                .then_inc(x_added, 1)

                dve.wait_ge(m.loaded_causal, 16)
                dve.tensor_scalar(qbias[:], w["parity"][:], w["c_bias"][:, 0:1], None, ALU.mult).then_inc(qbias_ready, 1)
                picks(step_of(0, 0), 0)
                picks(step_of(0, 1), 1)
                for first in range(3):
                    combine(step_of(0, first), first % 2)
                    if first < 2:
                        picks(step_of(0, first + 2), first % 2)
                        dve.wait_ge(combined, PAIRS * (first + 1))
                        norm_stats(dve, m, step_of(0, first), row(step_of(0, first)), ln, 1, 0)
                        normed(step_of(0, first))
                dve.wait_ge(zeroed, 1)
                run_steps(dve, STEPS, body, DEPTH)
                dve.wait_ge(x_added, STEPS)

def biased_attention(nc, m):
    w = m.w
    STEPS = TILES // 2
    NS = 2 * P
    UNITS = 4
    UH = HP // 2
    PROJ = 12
    COPIES = PROJ // 2
    PER_SLOT = PROJ // UNITS
    with ExitStack() as ctx:
        def sb(name, shape, dtype=F32):
            return ctx.enter_context(nc.sbuf_tensor("ba_" + name, shape, dtype))

        def sem(name):
            return stage_semaphore(nc, m, "ba_" + name)

        mask_bits = sb("mask_bits", [P, SEQ], U8)
        mask = sb("mask", [P, SEQ])
        hidden = sb("hidden", [P, SEQ])
        scaled_mask = sb("scaled_mask", [P, SEQ])
        bias = sb("bias", [P, HP, SEQ])
        xn = sb("xn", [P, 2, D])
        rows = sb("rows", [P, 2, D])
        inT = sb("inT", [P, 2, NS])
        qT = sb("qT", [P, 2, HP, NS])
        kT = sb("kT", [P, 2, HP, NS])
        v = sb("v", [P, 2, 2, INNER])
        probs = sb("probs", [P, 4, UH, 2, SEQ])
        probsT = sb("probsT", [P, 2, UH, P])
        top = sb("top", [P, 4, 2 * UH])
        total = sb("total", [P, 4, 2 * UH])
        attnT = sb("attnT", [P, 2, HP, P])
        bank = m.bank
        TURN_BANK, ATTN_BANK, OUT_BANK, PROJ_BANK = 2, 3, 5, 6

        ln = NormSemaphores(sem, "ln")
        loaded_mask = sem("loaded_mask")
        bias_step = sem("bias_step")
        bias_ready = sem("bias_ready")
        rows_ready = sem("rows_ready")
        in_turned = sem("in_turned")
        in_ready = sem("in_ready")
        proj_done = sem("proj_done")
        proj_even = sem("proj_even")
        proj_odd = sem("proj_odd")
        scores_done = sem("scores_done")
        masked = sem("masked")
        biased = sem("biased")
        top_ready = sem("top_ready")
        less_top = sem("less_top")
        exp_ready = sem("exp_ready")
        sum_ready = sem("sum_ready")
        inverse_ready = sem("inverse_ready")
        probs_ready = sem("probs_ready")
        probs_turned = sem("probs_turned")
        probsT_ready = sem("probsT_ready")
        attn_done = sem("attn_done")
        attn_ready = sem("attn_ready")
        out_done = sem("out_done")
        x_added = sem("x_added")

        def unit(u):
            return u % UNITS // 2, u % 2

        def copied(engine, step, n):
            reach(engine, (proj_even, proj_odd)[n % 2], count(step, COPIES, n // 2 + 1))

        def projected(k, n):
            if n < 8:
                return (qT, kT)[n // 4][:, k, 2 * (n % 4):2 * (n % 4) + 2, :].rearrange("p h n -> p (h n)")
            return v[:, k, (n - 8) // 2, N * (n % 2):N * (n % 2 + 1)]

        def proj_bank(n):
            return bank(PROJ_BANK + n % 2)

        def by_head(u):
            return probs[:, u % 4].rearrange("p h b k -> p (h b) k")

        with nc.Block() as block:

            @block.sync
            def _(sp):
                for b in range(2):
                    sp.dma_start(mask_bits[SEQ * b:SEQ * b + SEQ, :], m.dram["mask"]).then_inc(loaded_mask, 16)

            @block.tensor
            def _(pe):
                pe.wait_ge(m.loaded_biased, 32)

                def turn_inputs(step):
                    pe.wait_ge(ln.normed, count(step, 2, 2))
                    pe.wait_ge(rows_ready, count(step, 1, 1))
                    copied(pe, step, -2)
                    for n, src in enumerate((xn, rows)):
                        for t in range(2):
                            mm = pe.transpose(bank(PROJ_BANK)[:, NS * n + P * t:NS * n + P * t + P], src[:, t, :],
                                              w["ident"][:])
                    mm.then_inc(in_turned, 1)

                def projection(step, n):
                    if n == 0:
                        pe.wait_ge(in_ready, count(step, 1, 1))
                    copied(pe, step, n - 2)
                    if n < 8:
                        for h in range(2):
                            hp = 2 * (n % 4) + h
                            mm = pe.matmul(proj_bank(n)[:, NS * h:NS * h + NS], (w["bq"], w["bk"])[n // 4][:, P * hp:P * hp + P],
                                           inT[:, n // 4, :], start=True, stop=True)
                    else:
                        t = (n - 8) // 2
                        mm = pe.matmul(proj_bank(n), inT[:, 1, P * t:P * t + P], w["bv1"][:, N * (n % 2):N * (n % 2 + 1)],
                                       start=True, stop=True)
                    mm.then_inc(proj_done, 1)

                def score(k, u):
                    t, half = unit(u)
                    for n in range(UH):
                        for b in range(2):
                            for par in range(2):
                                part = slice(DHX * par, DHX * par + DHX)
                                at = slice(P * t + SEQ * b, P * t + SEQ * b + SEQ)
                                mm = pe.matmul(bank(u % 2)[SEQ * par:SEQ * par + SEQ, P * n + SEQ * b:P * n + SEQ * b + SEQ],
                                               qT[part, k, UH * half + n, at], kT[part, k, UH * half + n, at],
                                               start=True, stop=True)
                    mm.then_inc(scores_done, 1)

                def turn(step, u):
                    reach(pe, probs_ready, count(step, UNITS, u + 1))
                    reach(pe, probsT_ready, count(step, UNITS, u))
                    for n in range(UH):
                        mm = pe.transpose(bank(TURN_BANK)[:, P * n:P * n + P],
                                          probs[:, u % 4, n].rearrange("p b k -> p (b k)"), w["ident"][:])
                    mm.then_inc(probs_turned, 1)

                def attend(k, u):
                    t, half = unit(u)
                    for n in range(UH):
                        for par in range(2):
                            head = 2 * (UH * half + n) + par
                            for b in range(2):
                                part = slice(SEQ * b, SEQ * b + SEQ)
                                mm = pe.matmul(bank(ATTN_BANK + b)[DHX * par:DHX * par + DHX, SEQ * n:SEQ * n + SEQ],
                                               v[part, k, t, DHX * head:DHX * head + DHX],
                                               probsT[part, u % 2, n, SEQ * par:SEQ * par + SEQ], start=True, stop=True)
                    mm.then_inc(attn_done, 1)

                def attendable(step, u):
                    pe.wait_ge(probsT_ready, count(step, UNITS, u + 1))
                    reach(pe, attn_ready, count(step, UNITS, u))

                def project(step, t):
                    pe.wait_ge(attn_ready, count(step, UNITS, 2 * t + 2))
                    if t == 0:
                        reach(pe, x_added, count(step, 1, 0))
                    for hp in range(HP):
                        mm = pe.matmul(bank(OUT_BANK)[:, P * t:P * t + P], attnT[:, t, hp, :], w["bo1"][:, hp, :],
                                       start=(hp == 0), stop=(hp == HP - 1))
                    mm.then_inc(out_done, 1)

                def body(step, k, ahead):
                    here, before = ahead >= 0, not is_first(step)
                    for s in range(UNITS):
                        if ahead >= 1:
                            projection(later(step, 1), PER_SLOT * s)
                        if s == 0 and ahead == 0:
                            copied(pe, step, PROJ - 2)
                            copied(pe, step, PROJ - 1)
                        if before and s % 2:
                            project(later(step, -1), s // 2)
                        if here and s >= 2 or before and s < 2:
                            turn(step, s - 2)
                        if ahead >= 1:
                            projection(later(step, 1), PER_SLOT * s + 1)
                        if here:
                            score(k, s)
                        attends = here and s >= 3 or before and s < 3
                        if attends:
                            attendable(step, s - 3)
                        if ahead >= 1:
                            projection(later(step, 1), PER_SLOT * s + 2)
                        if s == UNITS - 1 and ahead >= 2:
                            turn_inputs(later(step, 2))
                        if attends:
                            attend(k if s >= 3 else 1 - k, s - 3)

                turn_inputs(step_of(0, 0))
                for n in range(PROJ):
                    projection(step_of(0, 0), n)
                turn_inputs(step_of(0, 1))
                run_steps(pe, STEPS, body)

            @block.scalar
            def _(act):
                def inputs(step):
                    act.wait_ge(in_turned, count(step, 1, 1))
                    act.activation(inT[:].rearrange("p a n -> p (a n)"), bank(PROJ_BANK), ACT.Copy).then_inc(in_ready, 1)

                def copy(step, k, n):
                    if n % 2 == 0:
                        act.wait_ge(proj_done, count(step, PROJ, n + 1))
                        act.activation(projected(k, n), proj_bank(n), ACT.Copy).then_inc(proj_even, 1)

                def body(step, k, ahead):
                    here, before = ahead >= 0, not is_first(step)
                    for s in range(UNITS):
                        if ahead >= 1:
                            copy(later(step, 1), 1 - k, PER_SLOT * s)
                        if here and s >= 2 or before and s < 2:
                            u = s - 2
                            act.wait_ge(probs_turned, count(step, UNITS, u + 1))
                            reach(act, attn_done, count(step, UNITS, u - 1))
                            act.activation(probsT[:, u % 2].rearrange("p a n -> p (a n)"), bank(TURN_BANK), ACT.Copy)\
                                .then_inc(probsT_ready, 1)
                        if ahead >= 1:
                            copy(later(step, 1), 1 - k, PER_SLOT * s + 1)
                            copy(later(step, 1), 1 - k, PER_SLOT * s + 2)
                        if s == UNITS - 1 and ahead >= 2:
                            inputs(later(step, 2))
                        if here and s >= 3 or before and s < 3:
                            u = s - 3
                            t, half = unit(u)
                            act.wait_ge(attn_done, count(step, UNITS, u + 1))
                            if half == 0:
                                reach(act, out_done, count(later(step, 0 if u >= 0 else -1), 2, t - 1))
                            act.activation(attnT[:, t, UH * half:UH * half + UH, :].rearrange("p h (b q) -> p b h q", q=SEQ),
                                           m.ps[:, ATTN_BANK:ATTN_BANK + 2, 0:UH * SEQ].rearrange("p b (h q) -> p b h q", q=SEQ),
                                           ACT.Copy).then_inc(attn_ready, 1)
                        if here:
                            act.wait_ge(less_top, count(step, UNITS, s + 1))
                            act.activation(probs[:, s % 4], probs[:, s % 4], ACT.Exp).then_inc(exp_ready, 1)

                inputs(step_of(0, 0))
                for n in range(PROJ):
                    copy(step_of(0, 0), 0, n)
                inputs(step_of(0, 1))
                run_steps(act, STEPS, body)

            @block.gpsimd
            def _(pool):
                pool.wait_ge(m.loaded_ctx, 16)

                def inputs(step):
                    norm_root(pool, m, step, ln, 1, 0)
                    reach(pool, in_turned, count(step, 1, 0))
                    pool.tensor_copy(rows[:], m.C[:, bass.ds(count(step, 2, 0), 2), :]).then_inc(rows_ready, 1)

                def body(step, k, ahead):
                    for s in range(UNITS if ahead >= 0 else 1):
                        if s >= 1 or not is_first(step):
                            u = s - 1
                            pool.wait_ge(inverse_ready, count(step, UNITS, u + 1))
                            pool.tensor_tensor(by_head(u), by_head(u), over(total[:, u % 4], 2, SEQ), ALU.mult)\
                                .then_inc(probs_ready, 1)
                        if ahead >= 0:
                            part = bias[:, UH * (s % 2):UH * (s % 2) + UH, :]
                            pool.wait_ge(masked, count(step, UNITS, s + 1))
                            pool.tensor_tensor(probs[:, s % 4], probs[:, s % 4], over(part, 2, 2), ALU.add).then_inc(biased, 1)
                        if ahead >= 2 and s == 0:
                            inputs(later(step, 2))

                inputs(step_of(0, 0))
                inputs(step_of(0, 1))
                pool.wait_ge(bias_ready, 1)
                run_steps(pool, STEPS, body)

            @block.vector
            def _(dve):
                def row(step):
                    return lambda t: m.X[:, bass.ds(count(step, 2, t), 1), :]

                def normed(step):
                    reach(dve, in_turned, count(step, 1, 0))
                    norm_apply(dve, m, step, row(step), lambda t: xn[:, t, :], ln, 1, 0)

                def copy(step, k, n):
                    if n % 2:
                        dve.wait_ge(proj_done, count(step, PROJ, n + 1))
                        dve.tensor_copy(projected(k, n), proj_bank(n)).then_inc(proj_odd, 1)

                def body(step, k, ahead):
                    here, before = ahead >= 0, not is_first(step)
                    for s in range(UNITS):
                        if ahead >= 1:
                            copy(later(step, 1), 1 - k, PER_SLOT * s)
                        if here and s >= 1 or before and s < 1:
                            u = s - 1
                            dve.wait_ge(exp_ready, count(step, UNITS, u + 1))
                            dve.tensor_reduce(total[:, u % 4], by_head(u), AX.X, ALU.add).then_inc(sum_ready, 1)
                            dve.wait_ge(sum_ready, count(step, UNITS, u + 1))
                            dve.reciprocal(total[:, u % 4], total[:, u % 4]).then_inc(inverse_ready, 1)
                        if ahead >= 1:
                            copy(later(step, 1), 1 - k, PER_SLOT * s + 1)
                        if here:
                            dve.wait_ge(scores_done, count(step, UNITS, s + 1))
                            reach(dve, probs_turned, count(step, UNITS, s - 3))
                            dve.tensor_tensor(by_head(s), bank(s % 2).rearrange("p (h k) -> p h k", k=SEQ),
                                              over(scaled_mask[:], 1, 2 * UH), ALU.mult).then_inc(masked, 1)
                        if ahead >= 1:
                            copy(later(step, 1), 1 - k, PER_SLOT * s + 2)
                        if s == 0 and ahead >= 2:
                            norm_stats(dve, m, later(step, 2), row(later(step, 2)), ln, 1, 0)
                        if s == 1 and ahead >= 2:
                            normed(later(step, 2))
                        if here:
                            dve.wait_ge(biased, count(step, UNITS, s + 1))
                            dve.tensor_reduce(top[:, s % 4], by_head(s), AX.X, ALU.max).then_inc(top_ready, 1)
                            dve.wait_ge(top_ready, count(step, UNITS, s + 1))
                            dve.tensor_tensor(by_head(s), by_head(s), over(top[:, s % 4], 2, SEQ), ALU.subtract)\
                                .then_inc(less_top, 1)
                        if s == 3 and before:
                            dve.wait_ge(out_done, count(step, 2, 0))
                            out = m.X[:, bass.ds(count(step, 2, -2), 2), :]
                            dve.tensor_tensor(out, bank(OUT_BANK)[:, 0:NS].rearrange("p (t n) -> p t n", n=P), out, ALU.add)\
                                .then_inc(x_added, 1)

                norm_stats(dve, m, step_of(0, 0), row(step_of(0, 0)), ln, 1, 0)
                normed(step_of(0, 0))
                dve.wait_ge(loaded_mask, 32)
                dve.tensor_copy(mask[:], mask_bits[:]).then_inc(bias_step, 1)
                dve.wait_ge(bias_step, 1)
                dve.tensor_scalar(hidden[:], mask[:], 1.0, -LOWEST, ALU.subtract, ALU.mult).then_inc(bias_step, 1)
                dve.tensor_scalar(scaled_mask[:], mask[:], DHX ** -0.5, None, ALU.mult).then_inc(bias_step, 1)
                dve.tensor_tensor(bias[:], m.bias_values[:].rearrange("p (k h) -> p h k", h=HP), over(mask[:], 1, HP), ALU.mult)\
                    .then_inc(bias_step, 1)
                dve.wait_ge(bias_step, 4)
                dve.tensor_tensor(bias[:], bias[:], over(hidden[:], 1, HP), ALU.add).then_inc(bias_ready, 1)
                for n in range(PROJ):
                    copy(step_of(0, 0), 0, n)
                norm_stats(dve, m, step_of(0, 1), row(step_of(0, 1)), ln, 1, 0)
                normed(step_of(0, 1))
                run_steps(dve, STEPS, body)
                dve.wait_ge(x_added, STEPS)

def top_expert(nc, m):
    w = m.w
    ROUTE = 17
    DVE_TILES, ACT_TILES = (0, 1), (2, 3)
    with ExitStack() as ctx:
        def sb(name, shape, dtype=F32):
            return ctx.enter_context(nc.sbuf_tensor("te_" + name, shape, dtype))

        def sem(name):
            return stage_semaphore(nc, m, "te_" + name)

        xn = sb("xn", [P, GT, D])
        xT = sb("xT", [P, 2, N])
        prob = sb("prob", [P, GT, E1])
        top = sb("top", [P, GT])
        ranked = sb("ranked", [P, GT, E1])
        index = sb("index", [P, GT, E1], U32)
        pick = sb("pick", [P, GT])
        chosen = sb("chosen", [P, 2, GT, E1])
        chosenT = sb("chosenT", [E1, N])
        parts = sb("parts", [P, 2, E1, D])
        bank = m.bank

        ln = NormSemaphores(sem, "ln")
        xT_turned = sem("xT_turned")
        xT_ready = sem("xT_ready")
        logits_done = sem("logits_done")
        exp_ready = sem("exp_ready")
        routed = sem("routed")
        chosen_turned = sem("chosen_turned")
        chosenT_ready = sem("chosenT_ready")
        bias_done = sem("bias_done")
        bias_added = sem("bias_added")
        experts_done = sem("experts_done")
        added = sem("added")
        weighted = sem("weighted")
        halved = sem("halved")
        pool_added = sem("pool_added")
        out_stored = sem("out_stored")

        ADDS = E1 * len(DVE_TILES)
        ORDER = (0, 2, 1, 3)

        def expert_bank(t, e):
            return bank(2 + 2 * (ORDER.index(t) % 2) + e // GT)[:, P * (e % GT):P * (e % GT + 1)]

        with nc.Block() as block:

            @block.sync
            def _(sp):
                with sp.Fori(0, GROUPS) as g:
                    sp.wait_ge(added, ADDS * g + ADDS)
                    sp.wait_ge(pool_added, len(ACT_TILES) * g + len(ACT_TILES))
                    sp.dma_start(m.out.rearrange("(t p) d -> p t d", p=P)[:, bass.ds(GT * g, GT), :],
                                 m.X[:, bass.ds(GT * g, GT), :]).then_inc(out_stored, 16)
                sp.wait_ge(out_stored, 16 * GROUPS)

            @block.tensor
            def _(pe):
                pe.wait_ge(m.loaded_top, 32)

                def turn_rows(a):
                    pe.wait_ge(ln.normed, count(a, GT, GT))
                    reach(pe, xT_ready, count(a, 1, 0))
                    for t in range(GT):
                        mm = pe.transpose(bank(0)[:, P * t:P * t + P], xn[:, t, :], w["ident"][:])
                    mm.then_inc(xT_turned, 1)

                def logits(a, k):
                    pe.wait_ge(xT_ready, count(a, 1, 1))
                    for t in range(GT):
                        out = bank(1)[:, E1 * t:E1 * t + E1]
                        pe.matmul(out, w["ones"][0:1, :], w["router_b"][0:1, :], start=True, stop=False)
                        mm = pe.matmul(out, xT[:, k, P * t:P * t + P], w["router1"][:], start=False, stop=True)
                    mm.then_inc(logits_done, 1)

                def bias(a, k):
                    pe.wait_ge(routed, count(a, ROUTE, ROUTE))
                    for t in range(GT):
                        mm = pe.transpose(bank(6)[0:E1, P * t:P * t + P], chosen[:, k, t, :], w["ident"][:])
                    mm.then_inc(chosen_turned, 1)
                    pe.wait_ge(chosenT_ready, count(a, 1, 1))
                    for t in range(GT):
                        mm = pe.matmul(bank(7)[:, P * t:P * t + P], chosenT[:, P * t:P * t + P], w["expert_b"][:],
                                       start=True, stop=True)
                    mm.then_inc(bias_done, 1)

                def expert(e, k, n):
                    t = ORDER[n]
                    if n % 2 == 0:
                        reach(pe, added, count(e, ADDS, E1 * (n // 2)))
                    else:
                        reach(pe, weighted, count(e, 2 * E1, E1 * (n // 2)))
                    for half in range(2):
                        mm = pe.matmul(bank(2 + 2 * (n % 2) + half), xT[:, k, P * t:P * t + P],
                                       w["expert"][:, N * half:N * half + N], start=True, stop=True)
                    mm.then_inc(experts_done, 1)

                def body(e, k, ahead):
                    if ahead < 0:
                        return
                    if ahead >= 1:
                        turn_rows(later(e, 1))
                    expert(e, k, 0)
                    if ahead >= 1:
                        logits(later(e, 1), 1 - k)
                    for n in range(1, GT):
                        expert(e, k, n)
                    if ahead >= 1:
                        bias(later(e, 1), 1 - k)

                turn_rows(step_of(0, 0))
                logits(step_of(0, 0), 0)
                bias(step_of(0, 0), 0)
                run_steps(pe, GROUPS, body)

            @block.scalar
            def _(act):
                def rows(a, k):
                    act.wait_ge(xT_turned, count(a, 1, 1))
                    act.activation(xT[:, k, :], bank(0), ACT.Copy).then_inc(xT_ready, 1)

                def exp(a):
                    act.wait_ge(routed, count(a, ROUTE, 2))
                    act.activation(prob[:], prob[:], ACT.Exp).then_inc(exp_ready, 1)

                def chosen_rows(a):
                    act.wait_ge(chosen_turned, count(a, 1, 1))
                    act.activation(chosenT[:], bank(6)[0:E1, :], ACT.Copy).then_inc(chosenT_ready, 1)

                def body(e, k, ahead):
                    if ahead < 0:
                        return
                    if ahead >= 1:
                        rows(later(e, 1), 1 - k)
                        exp(later(e, 1))
                    for n, t in enumerate(ACT_TILES):
                        act.wait_ge(experts_done, count(e, GT, ORDER.index(t) + 1))
                        reach(act, pool_added, count(e, 2, n - 1))
                        for i in range(E1):
                            act.activation(parts[:, n, i, :], expert_bank(t, i), ACT.Copy, scale=chosen[:, k, t, i:i + 1])\
                                .then_inc(weighted, 1)
                    if ahead >= 1:
                        chosen_rows(later(e, 1))

                rows(step_of(0, 0), 0)
                exp(step_of(0, 0))
                chosen_rows(step_of(0, 0))
                run_steps(act, GROUPS, body)

            @block.gpsimd
            def _(pool):
                def body(e, k, ahead):
                    if ahead < 0:
                        return
                    for n, t in enumerate(ACT_TILES):
                        pool.wait_ge(weighted, count(e, 2 * E1, E1 * (n + 1)))
                        for i, size in enumerate((4, 2, 1)):
                            if i:
                                pool.wait_ge(halved, count(e, 6, 3 * n + i))
                            pool.tensor_tensor(parts[:, n, 0:size, :], parts[:, n, 0:size, :], parts[:, n, size:2 * size, :],
                                               ALU.add).then_inc(halved, 1)
                        pool.wait_ge(halved, count(e, 6, 3 * n + 3))
                        if n == 0:
                            pool.wait_ge(bias_added, count(e, 1, 1))
                        row = m.X[:, bass.ds(count(e, GT, t), 1), :]
                        pool.tensor_tensor(row, row, parts[:, n, 0:1, :], ALU.add).then_inc(pool_added, 1)
                        if n == 0 and ahead >= 2:
                            norm_root(pool, m, later(e, 2), ln, 1, 0, GT)

                norm_root(pool, m, step_of(0, 0), ln, 1, 0, GT)
                norm_root(pool, m, step_of(0, 1), ln, 1, 0, GT)
                run_steps(pool, GROUPS, body)

            @block.vector
            def _(dve):
                def row(step):
                    return lambda t: m.X[:, bass.ds(count(step, GT, t), 1), :]

                def norm(a):
                    reach(dve, xT_turned, count(a, 1, 0))
                    norm_apply(dve, m, a, row(a), lambda t: xn[:, t, :], ln, 1, 0, GT)

                def route(a, k):
                    def step(n):
                        dve.wait_ge(routed, count(a, ROUTE, n))

                    dve.wait_ge(logits_done, count(a, 1, 1))
                    lg = bank(1)[:, 0:GT * E1].rearrange("p (t e) -> p t e", e=E1)
                    dve.tensor_reduce(top[:], lg, AX.X, ALU.max).then_inc(routed, 1)
                    step(1)
                    dve.tensor_tensor(prob[:], lg, over(top[:], 2, E1), ALU.subtract).then_inc(routed, 1)
                    dve.wait_ge(exp_ready, count(a, 1, 1))
                    dve.tensor_reduce(top[:], prob[:], AX.X, ALU.add).then_inc(routed, 1)
                    step(3)
                    dve.reciprocal(top[:], top[:]).then_inc(routed, 1)
                    step(4)
                    dve.tensor_tensor(prob[:], prob[:], over(top[:], 2, E1), ALU.mult).then_inc(routed, 1)
                    step(5)
                    dve.memset(m.spare[:], 0.0)
                    for t in range(GT):
                        dve.max(ranked[:, t, :], prob[:, t, :]).then_inc(routed, 1)
                    step(9)
                    dve.memset(m.spare[:], 0.0)
                    for t in range(GT):
                        dve.max_index(index[:, t, :], ranked[:, t, :], prob[:, t, :]).then_inc(routed, 1)
                    dve.tensor_copy(top[:], ranked[:, :, 0]).then_inc(routed, 1)
                    step(13)
                    dve.tensor_copy(pick[:], index[:, :, 0]).then_inc(routed, 1)
                    step(15)
                    reach(dve, weighted, count(a, 2 * E1, -2 * E1))
                    reach(dve, added, count(a, ADDS, -ADDS))
                    dve.tensor_tensor(chosen[:, k], over(w["expert_ids"][:], 1, GT), over(pick[:], 2, E1), ALU.is_equal)\
                        .then_inc(routed, 1)
                    step(16)
                    dve.tensor_tensor(chosen[:, k], chosen[:, k], over(top[:], 2, E1), ALU.mult).then_inc(routed, 1)

                def bias(a):
                    dve.wait_ge(bias_done, count(a, 1, 1))
                    rows = m.X[:, bass.ds(count(a, GT, 0), GT), :]
                    dve.tensor_tensor(rows, tiles_of(bank(7)), rows, ALU.add).then_inc(bias_added, 1)

                def add_experts(e, k, n):
                    t = DVE_TILES[n]
                    dve.wait_ge(experts_done, count(e, GT, ORDER.index(t) + 1))
                    out = m.X[:, bass.ds(count(e, GT, t), 1), :]
                    for i in range(E1):
                        if i >= 1:
                            dve.wait_ge(added, count(e, ADDS, E1 * n + i))
                        dve.scalar_tensor_tensor(out=out, in0=expert_bank(t, i).unsqueeze(1), scalar=chosen[:, k, t, i:i + 1],
                                                 in1=out, op0=ALU.mult, op1=ALU.add).then_inc(added, 1)

                def body(e, k, ahead):
                    if ahead < 0:
                        return
                    dve.wait_ge(bias_added, count(e, 1, 1))
                    dve.wait_ge(routed, count(e, ROUTE, ROUTE))
                    add_experts(e, k, 0)
                    if ahead >= 1:
                        route(later(e, 1), 1 - k)
                    if ahead >= 2:
                        norm_stats(dve, m, later(e, 2), row(later(e, 2)), ln, 1, 0, GT)
                    add_experts(e, k, 1)
                    if ahead >= 2:
                        norm(later(e, 2))
                    if ahead >= 1:
                        bias(later(e, 1))

                for first in range(2):
                    norm_stats(dve, m, step_of(0, first), row(step_of(0, first)), ln, 1, 0, GT)
                    norm(step_of(0, first))
                route(step_of(0, 0), 0)
                bias(step_of(0, 0))
                run_steps(dve, GROUPS, body)
                dve.wait_ge(added, ADDS * GROUPS)

PACKS = {
    "constants": [("ident", (P,)), ("ones", (P,)), ("same_head", (P,)), ("pair_rows", (HP,)), ("parity", (2,)), ("causal_kq", (SEQ,)),
                  ("causal_bias", (SEQ,)), ("cos", (SEQ,)), ("sin", (SEQ,)), ("not_first", (N,)),
                  ("earlier", (P,)), ("expert_ids", (E1,)), ("expert_base", (E1,)), ("distance", (2 * P,)), ("par_first", (P,))],
    "linear": [("dw", (3,)), ("b_gate", (1,)), ("ln_g", (1,)), ("ln_b", (1,)), ("pw", (D,)), ("qk", (4, D)),
               ("v0", (2, HP * DH0)), ("gate", (D,)), ("o0", (D,)), ("moe_gate", (E0,)), ("b1", (E0 * F0,)),
               ("w1", (E0, F0, P)), ("w2", (E0, F0, D))],
    "latent": [("x_affine", (4,)), ("xq", (INNER,)), ("xk", (INNER,)), ("xv", (INNER,)), ("xo", (HP, D))],
    "shared": [("router", (E1,)), ("sg", (FS, P)), ("su", (FS, P)), ("sd", (FS, D))],
    "causal": [("c_bias", (2,)), ("cqk", (2, D)), ("cv", (2, HP * DH0)), ("c_bv", (HP * DH0,)), ("co", (D,))],
    "biased": [("bq", (INNER,)), ("bk", (INNER,)), ("bv1", (INNER,)), ("bo1", (HP, D))],
    "top": [("router1", (E1,)), ("expert", (E1 * D,))],
    "rows": [("b2", (E0, D)), ("bo", (D,)), ("router_b", (E1,))],
}


def decoder(nc, dram, out):
    with ExitStack() as ctx:
        m, w = Shared(), {}
        m.w = w
        m.stage_semaphores = []

        def sb(name, shape, dtype=F32):
            return ctx.enter_context(nc.sbuf_tensor(name, shape, dtype))

        def sem(name):
            return ctx.enter_context(nc.semaphore(name))

        m.X = sb("X", [P, TILES, D])
        m.C = sb("C", [P, TILES, D])
        m.ps = ctx.enter_context(nc.psum_tensor("ps", [P, 8, 512], F32))
        m.bank = lambda n: m.ps[:, n, :]
        m.bn = sb("bn", [P, GT, 6])
        m.mean_var = sb("mean_var", [P, GT, 2])
        m.var_eps = sb("var_eps", [P, GT])
        m.rstd = sb("rstd", [P, GT])
        m.minus_half = sb("minus_half", [P, GT])
        w["rel_bias"] = sb("rel_bias", [64, HP])
        m.bias_values = sb("bias_values", [P, SEQ * HP])
        w["expert_b"] = sb("expert_b", [E1, D])
        m.spare = sb("spare", [P, 1])
        m.pool_spare = sb("pool_spare", [P, 2, GT])
        m.pair_weights = sb("pair_weights", [P, 2, TILES])
        m.pair_slots = sb("pair_slots", [P, 2, TILES], U32)
        m.dram, m.out = dram, out
        m.slot_rows = nc.dram_tensor("slot_rows", (SLOTS, D), F32, kind="Internal").ap()
        m.result_rows = nc.dram_tensor("result_rows", (SLOTS + 1, D), F32, kind="Internal").ap()
        zeros = sb("zeros", [P, D])
        packed = {}
        for pack, parts in PACKS.items():
            rows = 1 if pack == "rows" else P
            width = sum(int(np.prod(shape)) for _, shape in parts)
            if pack in ("biased", "top"):
                packed[pack] = packed[{"biased": "latent", "top": "linear"}[pack]][:, 0:width]
            else:
                packed[pack] = sb("pack_" + pack, [rows, width])
            at = 0
            for name, shape in parts:
                size = int(np.prod(shape))
                view = packed[pack][:, at:at + size]
                if len(shape) == 2:
                    view = view.rearrange("p (a b) -> p a b", a=shape[0])
                elif len(shape) == 3:
                    view = view.rearrange("p (a b c) -> p a b c", a=shape[0], b=shape[1])
                w[name] = view
                at += size

        m.biased_weights, m.top_weights = packed["biased"], packed["top"]
        m.loaded_x = sem("loaded_x")
        m.loaded_constants = sem("loaded_constants")
        m.loaded_linear = sem("loaded_linear")
        m.loaded_latent = sem("loaded_latent")
        m.loaded_ctx = sem("loaded_ctx")
        m.loaded_latent_all = 16
        m.loaded_shared = sem("loaded_shared")
        m.slots_cleared = sem("slots_cleared")
        zeros_ready = sem("zeros_ready")
        m.loaded_causal = sem("loaded_causal")
        m.loaded_biased = sem("loaded_biased")
        m.loaded_top = sem("loaded_top")
        power_ready = sem("power_ready")
        m.loaded_x_all, m.ready_constants_all, m.loaded_linear_all = 16, 16, 32
        m.ready_constants = m.loaded_constants

        with nc.Block() as block:
            @block.sync
            def _(sp):
                sp.dma_start(packed["constants"][:], dram["constants"]).then_inc(m.loaded_constants, 16)
                sp.dma_start(m.X[:], dram["x"].rearrange("(t p) d -> p t d", p=P)).then_inc(m.loaded_x, 16)
                sp.dma_start(packed["rows"][:], dram["rows"]).then_inc(m.loaded_linear, 16)
                sp.dma_start(packed["linear"][:], dram["linear"]).then_inc(m.loaded_linear, 16)
                sp.dma_start(m.C[:], dram["ctx"].rearrange("(t p) d -> p t d", p=P)).then_inc(m.loaded_ctx, 16)
                sp.dma_start(packed["latent"][:], dram["latent"]).then_inc(m.loaded_latent, 16)
                sp.dma_start(packed["shared"][:], dram["shared"]).then_inc(m.loaded_shared, 16)
                sp.dma_start(packed["causal"][:], dram["causal"]).then_inc(m.loaded_causal, 16)
                sp.dma_start(w["rel_bias"][:], dram["rel_bias"]).then_inc(m.loaded_biased, 16)
                sp.dma_start(w["expert_b"][:], dram["expert_b"]).then_inc(m.loaded_top, 16)
                sp.wait_ge(zeros_ready, 1)
                sp.dma_start(m.slot_rows.rearrange("(c p) d -> p c d", p=P), over(zeros[:], 1, SLOTS // P))\
                    .then_inc(m.slots_cleared, 16)
                sp.dma_start(m.result_rows[SLOTS:], zeros[0:1, :]).then_inc(m.slots_cleared, 16)

            @block.gpsimd
            def _(pool):
                pool.memset(zeros[:], 0.0).then_inc(zeros_ready, 1)
                pool.memset(m.minus_half[:], -0.5).then_inc(power_ready, 1)

        linear_attention(nc, m)
        latent_attention(nc, m)
        routed_experts(nc, m)
        reuse_semaphores(nc, m)
        causal_attention(nc, m)
        biased_attention(nc, m)
        top_expert(nc, m)


def constants():
    p = np.arange(P)
    c = {}
    c["ident"] = np.eye(P)
    c["ones"] = np.ones((P, P))
    c["same_head"] = p[:, None] // DH0 == p[None] // DH0
    c["pair_rows"] = p[:, None] // (2 * DH0) == np.arange(HP)[None]
    c["parity"] = p[:, None] // DH0 % 2 == np.arange(2)[None]
    c["causal_kq"] = np.arange(SEQ)[None] >= p[:, None] % SEQ
    c["causal_bias"] = np.where(np.arange(SEQ)[None] <= p[:, None] % SEQ, 0.0, LOWEST)
    inv_freq = np.float32(1.0) / np.float32(10000.0) ** (np.arange(0, DH0, 2, dtype=np.float32) / np.float32(DH0))
    theta = np.arange(SEQ, dtype=np.float32)[:, None] * inv_freq[None]
    pair = p % DH0 // 2
    c["cos"] = np.cos(theta).T[pair]
    c["sin"] = np.sin(theta).T[pair] * np.where(p % 2, 1.0, -1.0)[:, None]
    c["not_first"] = np.broadcast_to(np.arange(N) % SEQ != 0, (P, N))
    c["earlier"] = p[:, None] < p[None]
    c["expert_ids"] = np.broadcast_to(np.arange(E1), (P, E1))
    c["expert_base"] = np.broadcast_to(np.arange(E1) * CAP, (P, E1))
    c["distance"] = bucket_rows()
    c["par_first"] = p[:, None] == 2 * (p[None] % SEQ) + p[None] // SEQ
    return {name: np.asarray(a, np.float32) for name, a in c.items()}


def bucket_rows():
    buckets, furthest = 32, 128
    exact = buckets // 2
    distance = np.maximum(np.arange(P) - (SEQ - 1), 0)
    safe = np.maximum(distance, 1).astype(np.float32)
    log = np.log(safe / np.float32(exact)) / np.log(np.float32(furthest / exact))
    large = np.minimum(exact + (log * np.float32(buckets - exact)).astype(np.int32), buckets - 1)
    bucket = np.where(distance < exact, distance, large)
    row = np.arange(P)[:, None, None]
    return ((row % buckets == bucket[None, :, None]) & (row // buckets == np.arange(2)[None, None])).reshape(P, -1)


def layouts(a):
    per = {}
    swap = np.arange(D) ^ 1
    qkv = a["L0_attn_w_qkv"]
    wq, wk, wv = qkv[:D], qkv[D:2 * D], qkv[2 * D:]
    per["linear"] = {
        "dw": a["L0_attn_w_dw"], "b_gate": a["L0_attn_b_gate"][:, None], "ln_g": a["L0_attn_ln_g"][:, None],
        "ln_b": a["L0_attn_ln_b"][:, None], "pw": a["L0_attn_w_pw"].T,
        "qk": np.stack([wq.T, wk.T, wq[swap].T, wk[swap].T], 1),
        "v0": wv.reshape(HP, 2, DH0, D).transpose(3, 1, 0, 2),
        "gate": a["L0_attn_w_gate"].T, "o0": a["L0_attn_w_o"].T, "moe_gate": a["L0_attn_w_moe_gate"].T,
        "b1": a["L0_attn_b1"].reshape(E0 * F0, P).T,
        "w1": a["L0_attn_w1"].reshape(E0, F0, P, D).transpose(3, 0, 1, 2),
        "w2": a["L0_attn_w2"].reshape(E0, D, F0, P).transpose(3, 0, 2, 1),
    }
    wkv = a["L0_xattn_Wkv"]
    per["latent"] = {
        "x_affine": np.stack([a["L0_xattn_" + n] for n in ("g1", "b1", "g2", "b2")], 1),
        "xq": a["L0_xattn_Wq"], "xk": wkv[:, :INNER], "xv": wkv[:, INNER:],
        "xo": a["L0_xattn_Wout"].reshape(HP, P, D).transpose(1, 0, 2),
    }
    per["shared"] = {
        "router": a["L0_ffn_router_w"].T, "sg": a["L0_ffn_sg"], "su": a["L0_ffn_su"],
        "sd": a["L0_ffn_sd"].reshape(FS, P, D).transpose(1, 0, 2),
    }
    per["causal"] = {
        "c_bias": np.stack([a["L1_attn_bq"], a["L1_attn_bk"]], 1),
        "cqk": np.stack([a["L1_attn_Wq"], a["L1_attn_Wk"]], 1),
        "cv": a["L1_attn_Wv"].reshape(D, H // 4, 2, 2 * DH0).transpose(0, 2, 1, 3),
        "c_bv": np.repeat(a["L1_attn_bv"].reshape(H // 4, 2, 2 * DH0).transpose(1, 0, 2).reshape(2, -1), SEQ, axis=0),
        "co": a["L1_attn_Wo"],
    }
    per["biased"] = {
        "bq": a["L1_xattn_Wq"], "bk": a["L1_xattn_Wk"],
        "bv1": a["L1_xattn_Wv"],
        "bo1": a["L1_xattn_Wo"].reshape(HP, P, D).transpose(1, 0, 2),
    }
    per["top"] = {"router1": a["L1_ffn_router_w"].T, "expert": a["L1_ffn_expert_w"].transpose(2, 0, 1)}
    per["rows"] = {"b2": a["L0_attn_b2"], "bo": a["L1_attn_bo"], "router_b": a["L1_ffn_router_b"]}
    per["constants"] = constants()
    arrays = {"x": a["x"].reshape(TOKENS, D), "ctx": a["ctx_1024"].reshape(TOKENS, D)}
    down = a["L0_ffn_rd"].reshape(E1, FR, P, D).transpose(0, 2, 1, 3).reshape(E1, P, FR * D)
    arrays["mask"] = a["mask_1x1xSxS2_bk0"].reshape(SEQ, SEQ)
    arrays["rel_bias"] = a["L1_xattn_rel_bias"].T.reshape(-1, HP, 2).transpose(2, 0, 1).reshape(-1, HP)
    arrays["expert_b"] = a["L1_ffn_expert_b"]
    arrays["experts"] = np.concatenate([a["L0_ffn_rg"], a["L0_ffn_ru"], down], axis=2)
    for pack, parts in PACKS.items():
        rows = 1 if pack == "rows" else P
        arrays[pack] = np.concatenate([per[pack][name].reshape(rows, -1) for name, _ in parts], axis=1)
    return arrays


def kernel(**inputs):
    import concourse.bacc as bacc
    from concourse.bass_utils import run_bass_kernel_spmd

    nc = bacc.Bacc("TRN2", target_bir_lowering=False, num_devices=1)
    arrays = {name: np.ascontiguousarray(x) for name, x in
              layouts({name: np.asarray(x) for name, x in inputs.items()}).items()}
    dram = {name: nc.dram_tensor(name + "_dram", x.shape, mybir.dt.from_np(x.dtype), kind="ExternalInput").ap()
            for name, x in arrays.items()}
    out = nc.dram_tensor("out_dram", (TOKENS, D), F32, kind="ExternalOutput").ap()
    decoder(nc, dram, out)
    result = run_bass_kernel_spmd(nc, [{name + "_dram": x for name, x in arrays.items()}], core_ids=[0])
    return result.results[0]["out_dram"].reshape(NSEQ, SEQ, D)
```
